# Optimizing a Trainium2 kernel written in Bass

```python
import numpy as np
import jax
import jax.numpy as jnp

def _softmax(x, axis=-1):
    return jax.nn.softmax(x, axis=axis)

def _gelu(x):
    return jax.nn.gelu(x, approximate=True)

def _silu(x):
    return jax.nn.silu(x)

def _sigmoid(x):
    return jax.nn.sigmoid(x)

def _layernorm(x, axis=-1, eps=1e-05):
    m = jnp.mean(x, axis=axis, keepdims=True)
    v = jnp.var(x, axis=axis, keepdims=True)
    return (x - m) / jnp.sqrt(v + eps)

def _scatter_add(tgt, idx, src, axis=0):
    return tgt.at[idx].add(src)

def _segment_sum(src, seg, n):
    return jax.ops.segment_sum(src, seg, n)
kernel_name = 'mk_recurrent_d1_jaxref_r4_1ce301'

def setup_inputs(seed: int=0):
    np.random.seed(seed)
    _w = jnp.asarray

    def _L0_attn_setup():
        import jax, jax.numpy as jnp
        import numpy as np
        HEADS = 16
        BIAS_STRENGTH = 0.1
        LN_EPS = 1e-05

        def _layernorm(x, gamma, beta):
            mu = jnp.mean(x, axis=-1, keepdims=True)
            var = jnp.mean((x - mu) ** 2, axis=-1, keepdims=True)
            return (x - mu) * jax.lax.rsqrt(var + LN_EPS) * gamma + beta

        def _spatial_bias(spatial_centers, N, dtype):
            diff = spatial_centers[:, None, :] - spatial_centers[None, :, :]
            dist = jnp.sqrt(jnp.sum(diff * diff, axis=-1))
            max_dist = jnp.max(dist)
            core = jnp.where(max_dist > 1e-06, -dist / max_dist, 0.0) * BIAS_STRENGTH
            P = spatial_centers.shape[0]
            bias = jnp.zeros((N, N), dtype=dtype)
            return bias.at[1:P + 1, 1:P + 1].set(core.astype(dtype))
        key = jax.random.key(seed)
        ks = jax.random.split(key, 4)
        B, N, D, P = (2, 512, 256, 256)
        return {'x': jax.random.normal(ks[0], (B, N, D), dtype=jnp.float32), 'W_qkv': jax.random.normal(ks[1], (3 * D, D), dtype=jnp.float32) * D ** (-0.5), 'W_proj': jax.random.normal(ks[2], (D, D), dtype=jnp.float32) * D ** (-0.5), 'b_proj': jnp.zeros((D,), dtype=jnp.float32), 'ln_gamma': jnp.ones((D,), dtype=jnp.float32), 'ln_beta': jnp.zeros((D,), dtype=jnp.float32), 'spatial_centers': jax.random.uniform(ks[3], (P, 2), dtype=jnp.float32)}
    _L0_attn_in = _L0_attn_setup()

    def _L0_ffn_setup():
        import jax, jax.numpy as jnp
        import numpy as np
        DIM = 256
        DEPTH = 2
        HEADS = 8
        DIM_HEAD = 64
        WINDOW = 128
        INNER = HEADS * DIM_HEAD
        HID = int(DIM * 4 * 2 / 3)
        B, N = (2, 2048)
        QK_SCALE = 8.0

        def shift_token(t):
            t1, t2 = jnp.split(t, 2, axis=-1)
            t2 = jnp.pad(t2, ((0, 0), (1, 0), (0, 0)))[:, :-1]
            return jnp.concatenate([t1, t2], axis=-1)

        def l2norm(t):
            return t / jnp.clip(jnp.linalg.norm(t, axis=-1, keepdims=True), 1e-12)

        def rotate_half(x):
            x1, x2 = jnp.split(x, 2, axis=-1)
            return jnp.concatenate([-x2, x1], axis=-1)

        def rotary_xpos(q, k):
            n = q.shape[-2]
            half_idx = jnp.arange(0, DIM_HEAD, 2, dtype=jnp.float32)
            inv_freq = 1.0 / 10000.0 ** (half_idx / DIM_HEAD)
            t = jnp.arange(n, dtype=jnp.float32)
            freqs = t[:, None] * inv_freq[None, :]
            freqs = jnp.concatenate([freqs, freqs], axis=-1)
            base = (half_idx + 0.4 * DIM_HEAD) / (1.4 * DIM_HEAD)
            power = (t - n // 2) / float(WINDOW // 2)
            scale = base[None, :] ** power[:, None]
            scale = jnp.concatenate([scale, scale], axis=-1)
            cos, sin = (jnp.cos(freqs), jnp.sin(freqs))
            q = q * cos * scale + rotate_half(q) * sin * scale
            k = k * cos / scale + rotate_half(k) * sin / scale
            return (q, k)

        def local_attention(q, k, v):
            b, h, n, d = q.shape
            w = n // WINDOW
            bq = q.reshape(b, h, w, WINDOW, d) * QK_SCALE
            bk = k.reshape(b, h, w, WINDOW, d)
            bv = v.reshape(b, h, w, WINDOW, d)

            def look_around(t):
                p = jnp.pad(t, ((0, 0), (0, 0), (1, 0), (0, 0), (0, 0)))
                return jnp.concatenate([p[:, :, :w], p[:, :, 1:]], axis=3)
            bk, bv = (look_around(bk), look_around(bv))
            bt = jnp.arange(n).reshape(w, WINDOW)
            btp = jnp.pad(bt, ((1, 0), (0, 0)), constant_values=-1)
            btk = jnp.concatenate([btp[:w], btp[1:]], axis=1)
            sim = jnp.einsum('bhwid,bhwjd->bhwij', bq, bk)
            i = bt[:, :, None]
            j = btk[:, None, :]
            mask = (i < j) | (i > j + WINDOW) | (j == -1)
            sim = jnp.where(mask, -jnp.finfo(sim.dtype).max, sim)
            attn = jax.nn.softmax(sim, axis=-1)
            out = jnp.einsum('bhwij,bhwjd->bhwid', attn, bv)
            return out.reshape(b, h, n, d)

        def _layer(x, wqkv, qs, ksc, wo, lg, lb, w1, b1, w2, b2):
            b, n, _ = x.shape
            h = shift_token(x)
            qkv = h @ wqkv
            q, k, v = jnp.split(qkv, 3, axis=-1)
            to_heads = lambda t: t.reshape(b, n, HEADS, DIM_HEAD).transpose(0, 2, 1, 3)
            q, k, v = (to_heads(q), to_heads(k), to_heads(v))
            q = l2norm(q) * qs
            k = l2norm(k) * ksc
            q, k = rotary_xpos(q, k)
            o = local_attention(q, k, v)
            o = o.transpose(0, 2, 1, 3).reshape(b, n, INNER)
            x = x + o @ wo
            h = shift_token(x)
            mu = h.mean(-1, keepdims=True)
            var = h.var(-1, keepdims=True)
            h = (h - mu) / jnp.sqrt(var + 1e-05) * lg + lb
            h = h @ w1 + b1
            a, g = jnp.split(h, 2, axis=-1)
            h = a * jax.nn.gelu(g, approximate=False)
            x = x + h @ w2 + b2
            return x
        key = jax.random.key(seed)
        ks = jax.random.split(key, 6)
        return {'x': jax.random.normal(ks[0], (B, N, DIM), jnp.float32), 'wqkv': jax.random.normal(ks[1], (DEPTH, DIM, 3 * INNER), jnp.float32) * 0.02, 'q_scale': jnp.ones((DEPTH, DIM_HEAD), jnp.float32), 'k_scale': jnp.ones((DEPTH, DIM_HEAD), jnp.float32), 'wo': jax.random.normal(ks[2], (DEPTH, INNER, DIM), jnp.float32) * 0.02, 'ln_g': jnp.ones((DEPTH, DIM), jnp.float32), 'ln_b': jnp.zeros((DEPTH, DIM), jnp.float32), 'w1': jax.random.normal(ks[3], (DEPTH, DIM, 2 * HID), jnp.float32) * 0.02, 'b1': jnp.zeros((DEPTH, 2 * HID), jnp.float32), 'w2': jax.random.normal(ks[4], (DEPTH, HID, DIM), jnp.float32) * 0.02, 'b2': jnp.zeros((DEPTH, DIM), jnp.float32)}
    _L0_ffn_in = _L0_ffn_setup()
    _d = {'L0_attn_x': _L0_attn_in['x'], 'L0_attn_W_qkv': _L0_attn_in['W_qkv'], 'L0_attn_W_proj': _L0_attn_in['W_proj'], 'L0_attn_b_proj': _L0_attn_in['b_proj'], 'L0_attn_ln_gamma': _L0_attn_in['ln_gamma'], 'L0_attn_ln_beta': _L0_attn_in['ln_beta'], 'L0_attn_spatial_centers': _L0_attn_in['spatial_centers'], 'L0_ffn_wqkv': _L0_ffn_in['wqkv'], 'L0_ffn_q_scale': _L0_ffn_in['q_scale'], 'L0_ffn_k_scale': _L0_ffn_in['k_scale'], 'L0_ffn_wo': _L0_ffn_in['wo'], 'L0_ffn_ln_g': _L0_ffn_in['ln_g'], 'L0_ffn_ln_b': _L0_ffn_in['ln_b'], 'L0_ffn_w1': _L0_ffn_in['w1'], 'L0_ffn_b1': _L0_ffn_in['b1'], 'L0_ffn_w2': _L0_ffn_in['w2'], 'L0_ffn_b2': _L0_ffn_in['b2']}
    _x0 = _d['L0_attn_x']
    _d['L0_attn_x'] = jax.random.normal(jax.random.fold_in(jax.random.key(seed), 1), (2, 2048, 256), dtype=_x0.dtype)
    del _x0
    return _d

def reference(L0_attn_x, L0_attn_W_qkv, L0_attn_W_proj, L0_attn_b_proj, L0_attn_ln_gamma, L0_attn_ln_beta, L0_attn_spatial_centers, L0_ffn_wqkv, L0_ffn_q_scale, L0_ffn_k_scale, L0_ffn_wo, L0_ffn_ln_g, L0_ffn_ln_b, L0_ffn_w1, L0_ffn_b1, L0_ffn_w2, L0_ffn_b2):

    def _L0_attn_ref(x, W_qkv, W_proj, b_proj, ln_gamma, ln_beta, spatial_centers):
        import jax, jax.numpy as jnp
        import numpy as np
        HEADS = 16
        BIAS_STRENGTH = 0.1
        LN_EPS = 1e-05

        def _layernorm(x, gamma, beta):
            mu = jnp.mean(x, axis=-1, keepdims=True)
            var = jnp.mean((x - mu) ** 2, axis=-1, keepdims=True)
            return (x - mu) * jax.lax.rsqrt(var + LN_EPS) * gamma + beta

        def _spatial_bias(spatial_centers, N, dtype):
            diff = spatial_centers[:, None, :] - spatial_centers[None, :, :]
            dist = jnp.sqrt(jnp.sum(diff * diff, axis=-1))
            max_dist = jnp.max(dist)
            core = jnp.where(max_dist > 1e-06, -dist / max_dist, 0.0) * BIAS_STRENGTH
            P = spatial_centers.shape[0]
            bias = jnp.zeros((N, N), dtype=dtype)
            return bias.at[1:P + 1, 1:P + 1].set(core.astype(dtype))
        B, N, D = x.shape
        H = HEADS
        hd = D // H
        scale = hd ** (-0.5)
        qkv = jnp.einsum('bnd,ed->bne', x, W_qkv)
        qkv = qkv.reshape(B, N, 3, H, hd).transpose(2, 0, 3, 1, 4)
        q, k, v = (qkv[0], qkv[1], qkv[2])
        attn = jnp.einsum('bhnd,bhmd->bhnm', q, k) * scale
        P = spatial_centers.shape[0]
        if N >= P + 1:
            attn = attn + _spatial_bias(spatial_centers, N, x.dtype)[None, None]
        attn = jax.nn.softmax(attn, axis=-1)
        out = jnp.einsum('bhnm,bhmd->bhnd', attn, v)
        out = out.transpose(0, 2, 1, 3).reshape(B, N, D)
        out = jnp.einsum('bnd,ed->bne', out, W_proj) + b_proj
        return out + _layernorm(x, ln_gamma, ln_beta)

    def _L0_ffn_ref(x, wqkv, q_scale, k_scale, wo, ln_g, ln_b, w1, b1, w2, b2):
        import jax, jax.numpy as jnp
        import numpy as np
        DIM = 256
        DEPTH = 2
        HEADS = 8
        DIM_HEAD = 64
        WINDOW = 128
        INNER = HEADS * DIM_HEAD
        HID = int(DIM * 4 * 2 / 3)
        B, N = (2, 2048)
        QK_SCALE = 8.0

        def shift_token(t):
            t1, t2 = jnp.split(t, 2, axis=-1)
            t2 = jnp.pad(t2, ((0, 0), (1, 0), (0, 0)))[:, :-1]
            return jnp.concatenate([t1, t2], axis=-1)

        def l2norm(t):
            return t / jnp.clip(jnp.linalg.norm(t, axis=-1, keepdims=True), 1e-12)

        def rotate_half(x):
            x1, x2 = jnp.split(x, 2, axis=-1)
            return jnp.concatenate([-x2, x1], axis=-1)

        def rotary_xpos(q, k):
            n = q.shape[-2]
            half_idx = jnp.arange(0, DIM_HEAD, 2, dtype=jnp.float32)
            inv_freq = 1.0 / 10000.0 ** (half_idx / DIM_HEAD)
            t = jnp.arange(n, dtype=jnp.float32)
            freqs = t[:, None] * inv_freq[None, :]
            freqs = jnp.concatenate([freqs, freqs], axis=-1)
            base = (half_idx + 0.4 * DIM_HEAD) / (1.4 * DIM_HEAD)
            power = (t - n // 2) / float(WINDOW // 2)
            scale = base[None, :] ** power[:, None]
            scale = jnp.concatenate([scale, scale], axis=-1)
            cos, sin = (jnp.cos(freqs), jnp.sin(freqs))
            q = q * cos * scale + rotate_half(q) * sin * scale
            k = k * cos / scale + rotate_half(k) * sin / scale
            return (q, k)

        def local_attention(q, k, v):
            b, h, n, d = q.shape
            w = n // WINDOW
            bq = q.reshape(b, h, w, WINDOW, d) * QK_SCALE
            bk = k.reshape(b, h, w, WINDOW, d)
            bv = v.reshape(b, h, w, WINDOW, d)

            def look_around(t):
                p = jnp.pad(t, ((0, 0), (0, 0), (1, 0), (0, 0), (0, 0)))
                return jnp.concatenate([p[:, :, :w], p[:, :, 1:]], axis=3)
            bk, bv = (look_around(bk), look_around(bv))
            bt = jnp.arange(n).reshape(w, WINDOW)
            btp = jnp.pad(bt, ((1, 0), (0, 0)), constant_values=-1)
            btk = jnp.concatenate([btp[:w], btp[1:]], axis=1)
            sim = jnp.einsum('bhwid,bhwjd->bhwij', bq, bk)
            i = bt[:, :, None]
            j = btk[:, None, :]
            mask = (i < j) | (i > j + WINDOW) | (j == -1)
            sim = jnp.where(mask, -jnp.finfo(sim.dtype).max, sim)
            attn = jax.nn.softmax(sim, axis=-1)
            out = jnp.einsum('bhwij,bhwjd->bhwid', attn, bv)
            return out.reshape(b, h, n, d)

        def _layer(x, wqkv, qs, ksc, wo, lg, lb, w1, b1, w2, b2):
            b, n, _ = x.shape
            h = shift_token(x)
            qkv = h @ wqkv
            q, k, v = jnp.split(qkv, 3, axis=-1)
            to_heads = lambda t: t.reshape(b, n, HEADS, DIM_HEAD).transpose(0, 2, 1, 3)
            q, k, v = (to_heads(q), to_heads(k), to_heads(v))
            q = l2norm(q) * qs
            k = l2norm(k) * ksc
            q, k = rotary_xpos(q, k)
            o = local_attention(q, k, v)
            o = o.transpose(0, 2, 1, 3).reshape(b, n, INNER)
            x = x + o @ wo
            h = shift_token(x)
            mu = h.mean(-1, keepdims=True)
            var = h.var(-1, keepdims=True)
            h = (h - mu) / jnp.sqrt(var + 1e-05) * lg + lb
            h = h @ w1 + b1
            a, g = jnp.split(h, 2, axis=-1)
            h = a * jax.nn.gelu(g, approximate=False)
            x = x + h @ w2 + b2
            return x
        for l in range(DEPTH):
            x = _layer(x, wqkv[l], q_scale[l], k_scale[l], wo[l], ln_g[l], ln_b[l], w1[l], b1[l], w2[l], b2[l])
        return x
    x = L0_attn_x
    xn = _layernorm(x, axis=-1)
    s = _L0_attn_ref(xn, L0_attn_W_qkv, L0_attn_W_proj, L0_attn_b_proj, L0_attn_ln_gamma, L0_attn_ln_beta, L0_attn_spatial_centers)
    g = _silu(_L0_ffn_ref(xn, L0_ffn_wqkv, L0_ffn_q_scale, L0_ffn_k_scale, L0_ffn_wo, L0_ffn_ln_g, L0_ffn_ln_b, L0_ffn_w1, L0_ffn_b1, L0_ffn_w2, L0_ffn_b2))
    x = x + s * g
    return x

_drawn_inputs = setup_inputs


def setup_inputs(seed=0):
    import zlib

    import numpy as np

    out = dict(_drawn_inputs(seed))
    spreads = {'L0_attn_b_proj': (0.0, 0.1),
     'L0_attn_ln_gamma': (1.0, 0.2),
     'L0_attn_ln_beta': (0.0, 0.1),
     'L0_ffn_q_scale': (1.0, 0.6),
     'L0_ffn_k_scale': (1.0, 0.6),
     'L0_ffn_ln_g': (1.0, 0.6),
     'L0_ffn_ln_b': (0.0, 0.8),
     'L0_ffn_b1': (0.0, 0.8),
     'L0_ffn_b2': (0.0, 0.1)}
    factors = {'L0_attn_spatial_centers': 8.0,
     'L0_ffn_wqkv': 4.309,
     'L0_ffn_wo': 4.217,
     'L0_ffn_w1': 2.759,
     'L0_ffn_w2': 2.755}
    for name, (base, spread) in spreads.items():
        noise = np.random.default_rng([zlib.crc32(name.encode()), seed]).standard_normal(out[name].shape)
        drawn = base * np.exp(spread * noise) if base else spread * noise
        out[name] = jnp.asarray(drawn.astype(out[name].dtype))
    for name, factor in factors.items():
        out[name] = (out[name] * factor).astype(out[name].dtype)
    return out
```

```python
from contextlib import ExitStack

import numpy as np

import concourse.bass as bass
from concourse import mybir

P = 128
F32 = mybir.dt.float32
BF16 = mybir.dt.bfloat16
ALU = mybir.AluOpType
ACT = mybir.ActivationFunctionType
AX = mybir.AxisListType
RMAX = bass.bass_isa.ReduceOp.max
BANK = 512

B, N, D = 2, 2048, 256
T = B * N
HEADS, HD = 16, 16
SCALE = float(HD) ** -0.5
PTS = 256
LN_EPS = 1e-5

CHUNK = 512
NCHUNK = T // CHUNK
JT = CHUNK // P
NMB = 2 * D // P

QC = N // CHUNK
KB = N // P
STEPS = B * QC * KB
GROUPS = B * QC
PARTS = 3
TERM_ROWS = 6 * HD
MAX_ROWS = 3 * HD
SHIFT_ROWS = 2
AUG = TERM_ROWS + SHIFT_ROWS
LEAD = KB + 5
MSTEP = 13
PRING = 16
SRING = 3
ST_USES = STEPS + GROUPS
PAIRS = STEPS // 2
VW = 32

LAYERS = 2
WINDOW = 128
NWIN = N // WINDOW
LH, LD = 8, 64
INNER = LH * LD
PAIR = P // LD
NPAIR = LH // PAIR
HID = int(D * 4 * 2 / 3)
HB = 6
HP = -(-HID // HB)
QK_SCALE = 8.0
NORM_MIN = 1e-12
MASKED = -1e30
ITEMS = LAYERS * B
DVE_STEPS = 40
DIST_MIN = 1e-6
BIAS_STRENGTH = 0.1


PV_PLAN = {9: (0, 0), 12: (0, 4), 15: (0, 8), 2: (-1, 12)}
SUMS_STEP, ADD_STEP, KEEP_STEP = 3, 6, 7


def build(nc, x, wqkT, wvT, wpT, b_proj, gamma, beta, centers, centersT, wqkv, qk_gain, qk_gain_swapped, rotary,
          wo, ln_gain, ln_bias, w1, b1, w2, b2, out):
    xT_dram = nc.dram_tensor("xT_scratch", (2, P, T), F32, kind="Internal").ap()
    q_dram = nc.dram_tensor("q_parts", (HEADS, PARTS * HD, T), BF16, kind="Internal").ap()
    k_dram = nc.dram_tensor("k_parts", (HEADS, PARTS * HD, T), BF16, kind="Internal").ap()
    res_dram = nc.dram_tensor("res_scratch", (T, D), F32, kind="Internal").ap()

    with ExitStack() as top:
        def sem(name):
            return top.enter_context(nc.semaphore(name))

        banks = top.enter_context(nc.psum_tensor("banks", [P, 8, BANK], F32))

        def keep(name, shape, dt):
            return top.enter_context(nc.sbuf_tensor(name, shape, dt))

        ident = keep("ident", [P, P], F32)
        attn_tok = keep("attn_tok", [P, T // P, D], F32)

        early = ExitStack()

        def sb(name, shape, dt):
            return early.enter_context(nc.sbuf_tensor(name, shape, dt))

        identb = sb("identb", [P, P], BF16)
        wqk_sb = sb("wqk_sb", [P, 2, 2 * D], F32)
        wv_sb = sb("wv_sb", [P, 2, D], F32)
        gamma_sb = sb("gamma_sb", [P, D], F32)
        beta_sb = sb("beta_sb", [P, D], F32)
        bproj_sb = sb("bproj_sb", [P, D], F32)
        crow = sb("crow", [P, 2, PTS], F32)
        ccol = sb("ccol", [P, 3, 2], F32)
        dist = sb("dist", [P, 3, PTS], F32)
        dtmp = sb("dtmp", [P, 3, PTS], F32)
        bias_exp = sb("bias_exp", [P, 3, PTS], F32)
        dmax = sb("dmax", [P, 8], F32)
        v_all = sb("v_all", [P, T // P, D], F32)
        phase1 = ExitStack()
        x_in = phase1.enter_context(nc.sbuf_tensor("x_in", [P, 2, JT, D], F32))
        xn = phase1.enter_context(nc.sbuf_tensor("xn", [P, JT, D], F32))
        xn2 = phase1.enter_context(nc.sbuf_tensor("xn2", [P, JT, D], F32))
        xnT = phase1.enter_context(nc.sbuf_tensor("xnT", [P, 2, CHUNK], F32))
        stats = phase1.enter_context(nc.sbuf_tensor("stats", [P, JT, 6], F32))
        total = phase1.enter_context(nc.sbuf_tensor("total", [P, JT, 2], F32))
        between = phase1.enter_context(nc.sbuf_tensor("between", [P, JT], F32))
        mv = phase1.enter_context(nc.sbuf_tensor("mv", [P, 2, JT, 2], F32))
        rstd = phase1.enter_context(nc.sbuf_tensor("rstd", [P, 2, JT], F32))
        rest = phase1.enter_context(nc.sbuf_tensor("rest", [P, NMB, CHUNK], F32))
        parts = phase1.enter_context(nc.sbuf_tensor("parts", [P, NMB, PARTS, CHUNK], BF16))
        phase1.close()
        q_aug = sb("q_aug", [P, B, N], BF16)
        k_aug = sb("k_aug", [P, B, N], BF16)
        v_cur = sb("v_cur", [P, B, KB, VW], F32)
        probs = sb("probs", [P, PRING, CHUNK], F32)
        acc_sb = sb("acc_sb", [P, CHUNK], F32)
        pair_max = sb("pair_max", [P, QC, 2], F32)
        row_max = sb("row_max", [P, QC], F32)
        shift = sb("shift", [P, QC, SHIFT_ROWS], BF16)
        sums = sb("sums", [P, JT, HD + 1], F32)
        inv_sum = sb("inv_sum", [P, QC], F32)
        early.close()

        late = ExitStack()

        def fb(name, shape, dt=F32):
            return late.enter_context(nc.sbuf_tensor(name, shape, dt))

        wqkv_sb = fb("wqkv_sb", [P, LAYERS, 2, 3 * INNER])
        wo_sb = fb("wo_sb", [P, LAYERS, NPAIR, D])
        w1_sb = fb("w1_sb", [P, LAYERS, 2, 2 * HB * HP])
        w2_sb = fb("w2_sb", [HP, LAYERS, HB, D])
        wp_sb = fb("wp_sb", [P, 2, D])
        b1_sb = fb("b1_sb", [HP, LAYERS, 2 * HB])
        b2_sb = fb("b2_sb", [P, LAYERS, 2])
        lng_sb = fb("lng_sb", [P, LAYERS, 2])
        lnb_sb = fb("lnb_sb", [P, LAYERS, 2])
        gains = fb("gains", [P, LAYERS, 4, LD])
        tables = fb("tables", [P, 4, LD])
        tab = fb("tab", [P, B, LAYERS, 4, LD])
        mask = fb("mask", [P, 2 * WINDOW])
        mask_prev = fb("mask_prev", [P, WINDOW])
        half_power = fb("half_power", [P, 2 * LH])
        one = fb("one", [P, 1])
        xT = fb("xT", [P, LAYERS, B, 2, 1 + WINDOW])
        x1T = fb("x1T", [P, LAYERS, B, 2, 1 + WINDOW])
        kT = fb("kT", [P, LAYERS, B, NPAIR, 2 * WINDOW])
        vw = fb("vw", [P, LAYERS, B, 2, INNER])
        qT = fb("qT", [P, B, NPAIR, WINDOW])
        norms = fb("norms", [P, B, 2 * LH])
        masked = fb("masked", [P, B, LH, 2 * WINDOW])
        peak = fb("peak", [P, B, LH])
        npeak = fb("npeak", [P, B, LH])
        psum_rows = fb("psum_rows", [P, B, LH])
        pT = fb("pT", [P, B, LH, 2, WINDOW])
        flat_masked = masked[:].rearrange("p b h t -> p b (h t)")
        squares = flat_masked[:, :, 0:2 * INNER].rearrange("p b (s e) -> p b s e", s=2)
        crossed = flat_masked[:, :, 2 * INNER:4 * INNER].rearrange("p b (s e) -> p b s e", s=2)
        flat_pT = pT[:].rearrange("p b h c t -> p b (h c t)")
        turned = flat_pT[:, :, 0:2 * INNER].rearrange("p b (s e) -> p b s e", s=2)
        gated = flat_pT[0:HP, :, 0:HB * WINDOW].rearrange("p b (j t) -> p b j t", t=WINDOW)
        uT = flat_pT[0:HP, :, HB * WINDOW:2 * HB * WINDOW].rearrange("p b (j t) -> p b j t", t=WINDOW)
        oT = fb("oT", [P, B, NPAIR, WINDOW])
        fstats = fb("fstats", [P, B, 6])
        ftotal = fb("ftotal", [P, B, 2])
        fbetween = fb("fbetween", [P, B, 1])
        fmv = fb("fmv", [P, B, 2])
        hn = fb("hn", [P, B, D])
        hnT = fb("hnT", [P, B, 2, WINDOW])
        yT = fb("yT", [P, B, 2, WINDOW])
        o_win, o_winT = hn, hnT
        x_win = fb("x_win", [P, B, D])
        res_win = fb("res_win", [P, B, D])
        silu = fb("silu", [P, B, D])
        s_win = fb("s_win", [P, B, D])
        late.close()

        consts_in = sem("consts_in")
        dist_in = sem("dist_in")
        pool_const = sem("pool_const")
        dve_const = sem("dve_const")
        dist_step = sem("dist_step")
        dist_sqrt = sem("dist_sqrt")
        dist_red = sem("dist_red")
        dist_scale = sem("dist_scale")
        dist_exp = sem("dist_exp")
        bias_ready = sem("bias_ready")
        x_loaded = [sem(f"x_loaded{u}") for u in range(2)]
        ln_dve = sem("ln_dve")
        ln_var = sem("ln_var")
        ln_sqrt = sem("ln_sqrt")
        xn_ready = sem("xn_ready")
        xn2_ready = sem("xn2_ready")
        res_step = sem("res_step")
        res_ready = sem("res_ready")
        res_stored = sem("res_stored")
        xT_done = sem("xT_done")
        xnT_ready = sem("xnT_ready")
        xT_stored = sem("xT_stored")
        qk_done = sem("qk_done")
        v_done = sem("v_done")
        v_saved = sem("v_saved")
        part1 = sem("part1")
        rest_ready = sem("rest_ready")
        part2 = sem("part2")
        part3 = sem("part3")
        parts_stored = sem("parts_stored")
        aug_loaded = [sem(f"aug_loaded{b}") for b in range(B)]
        v_copied = sem("v_copied")
        st_ready = sem("st_ready")
        smax_ready = sem("smax_ready")
        smax_read = sem("smax_read")
        max_step = sem("max_step")
        shift_ready = sem("shift_ready")
        shift_saved = sem("shift_saved")
        prob_ready = sem("prob_ready")
        bias_done = sem("bias_done")
        pv_done = sem("pv_done")
        acc_saved = sem("acc_saved")
        sel_done = sem("sel_done")
        inv_done = sem("inv_done")
        sums_done = sem("sums_done")
        attn_saved = sem("attn_saved")
        phase1_end = sem("phase1_end")

        phase2_end = sem("phase2_end")
        ff_weights = sem("ff_weights")
        ff_const = sem("ff_const")
        tab_ready = sem("tab_ready")
        tables_in = sem("tables_in")
        x_window = [sem(f"x_window{b}") for b in range(B)]
        final_in = [sem(f"final_in{b}") for b in range(B)]
        qkv_done = sem("qkv_done")
        squares_done = sem("squares_done")
        v_kept = sem("v_kept")
        square_sums = sem("square_sums")
        inv_norms = sem("inv_norms")
        turned_done = sem("turned_done")
        qkT_done = sem("qkT_done")
        qT_kept = sem("qT_kept")
        kT_kept = sem("kT_kept")
        scores_done = sem("scores_done")
        masked_done = sem("masked_done")
        peaks_done = sem("peaks_done")
        exp_done = sem("exp_done")
        inv_rows = sem("inv_rows")
        probs_scaled = sem("probs_scaled")
        pT_done = sem("pT_done")
        pT_kept0 = sem("pT_kept0")
        pT_kept1 = sem("pT_kept1")
        oT_done = sem("oT_done")
        oT_kept = sem("oT_kept")
        wo_done = sem("wo_done")
        x1_ready = sem("x1_ready")
        h_done = sem("h_done")
        var_done = sem("var_done")
        norm_sums = sem("norm_sums")
        rstd_done = sem("rstd_done")
        hn_ready = sem("hn_ready")
        hnT_done = sem("hnT_done")
        hnT_kept = sem("hnT_kept")
        w1_done = sem("w1_done")
        gelu_done = sem("gelu_done")
        u_ready = sem("u_ready")
        w2_done = sem("w2_done")
        x2_ready = sem("x2_ready")
        k_carried = sem("k_carried")
        v_carried = sem("v_carried")
        x_carried = sem("x_carried")
        x1_carried = sem("x1_carried")
        mask_set = sem("mask_set")
        o_copied = sem("o_copied")
        owT_done = sem("owT_done")
        owT_kept = sem("owT_kept")
        y_done = sem("y_done")
        exp_neg = sem("exp_neg")
        result_ready = sem("result_ready")
        result_stored = [sem(f"result_stored{b}") for b in range(B)]
        dve_step = sem("dve_step")

        def turn(i, l, b):
            return i * ITEMS + (l * B + b + 1)

        def lanes(b):
            return 4 * b

        def place(hh):
            return (hh % 2) * (LH // 2) + hh // 2

        block = top.enter_context(nc.Block())

        NCONST = 5
        FF_WEIGHTS = 16 * 13

        @block.sync
        def _(sp):
            sp.dma_start(wqk_sb[:], wqkT.rearrange("(k p) e -> p k e", p=P)).then_inc(consts_in, 16)
            sp.dma_start(wv_sb[:], wvT.rearrange("(k p) e -> p k e", p=P)).then_inc(consts_in, 16)
            sp.dma_start(gamma_sb[:], gamma.partition_broadcast(P)).then_inc(consts_in, 16)
            sp.dma_start(beta_sb[:], beta.partition_broadcast(P)).then_inc(consts_in, 16)
            sp.dma_start(bproj_sb[:], b_proj.partition_broadcast(P)).then_inc(consts_in, 16)
            sp.dma_start(crow[:], centersT.partition_broadcast(P)).then_inc(dist_in, 16)
            sp.dma_start(ccol[1:P, 0, :], centers[0:P - 1, :]).then_inc(dist_in, 16)
            sp.dma_start(ccol[0:1, 0, :], centers[0:1, :]).then_inc(dist_in, 16)
            sp.dma_start(ccol[:, 1, :], centers[P - 1:2 * P - 1, :]).then_inc(dist_in, 16)
            sp.dma_start(ccol[:, 2, :], centers[PTS - 1, :].partition_broadcast(P)).then_inc(dist_in, 16)
            xv = x.rearrange("b (c j p) d -> (b c) p j d", p=P, j=JT)

            def load(c, half):
                sp.dma_start(x_in[:, half], xv[c]).then_inc(x_loaded[half], 16)

            load(0, 0)
            load(1, 1)
            nc.sync.sem_inc(xT_stored, 16)
            nc.sync.sem_inc(parts_stored, 16 * PARTS * NMB)
            nc.sync.sem_inc(res_stored, 16)
            with nc.sync.Fori(0, NCHUNK // 2) as it:
                for u in range(2):
                    c = it * 2 + u
                    after_next = nc.sync.snap((c + 2) % NCHUNK)
                    token = nc.sync.snap(c * CHUNK)
                    sp.wait_ge(xn_ready, c + 1)
                    sp.dma_start(x_in[:, u], xv[bass.ds(after_next, 1)][0]).then_inc(x_loaded[u], 16)
                    sp.wait_ge(part3, c * NMB + 1)
                    sp.wait_ge(xnT_ready, c + 2)
                    sp.dma_start(xT_dram[:, :, bass.ds(token, CHUNK)].rearrange("k p t -> p k t"),
                                 xnT[:]).then_inc(xT_stored, 16)
                    for mb in range(NMB):
                        if mb > 0:
                            sp.wait_ge(part3, c * NMB + (mb + 1))
                        heads = (mb % 2) * (P // HD)
                        dst = (q_dram if mb < 2 else k_dram)[heads:heads + P // HD, :, bass.ds(token, CHUNK)]
                        for part in range(PARTS):
                            sp.dma_start(dst[:, part * HD:(part + 1) * HD, :], parts[:, mb, part]
                                         ).then_inc(parts_stored, 16)
                    sp.wait_ge(res_ready, c + 1)
                    sp.dma_start(res_dram[bass.ds(token, CHUNK), :].rearrange("(j p) d -> p j d", p=P),
                                 xn2[:]).then_inc(res_stored, 16)
            sp.wait_ge(parts_stored, 16 * PARTS * NMB * (NCHUNK + 1))
            sp.wait_ge(xT_stored, 16 * (NCHUNK + 1))
            sp.wait_ge(res_stored, 16 * (NCHUNK + 1))
            for u in range(2):
                sp.wait_ge(x_loaded[u], 16 * (NCHUNK // 2 + 1))
            nc.sync.sem_inc(phase1_end, 1)
            sp.wait_ge(phase1_end, 5)

            def load_aug(h, b):
                for dram, aug, first, single in ((q_dram, q_aug, 0, 0), (k_dram, k_aug, 1, 2)):
                    src = dram[bass.ds(h, 1), :, b * N:(b + 1) * N][0]
                    for row, part, n in ((0, first, 2), (2, single, 1), (3, 0, 3)):
                        sp.dma_start(aug[row * HD:(row + n) * HD, b, :],
                                     src[part * HD:(part + n) * HD]).then_inc(aug_loaded[b], 16)

            for b in range(B):
                nc.sync.sem_inc(result_stored[b], 16)
            load_aug(0, 0)
            with nc.sync.Fori(0, HEADS) as h:
                next_head = nc.sync.snap((h + 1) % HEADS)
                sp.wait_ge(st_ready, h * ST_USES + 1)
                load_aug(h, 1)
                sp.wait_ge(st_ready, h * ST_USES + (STEPS // 2 + GROUPS // 2 + 1))
                load_aug(next_head, 0)
            sp.wait_ge(aug_loaded[0], 16 * 6 * (HEADS + 1))
            sp.wait_ge(aug_loaded[1], 16 * 6 * HEADS)
            sp.wait_ge(phase2_end, 4)
            sp.dma_start(wqkv_sb[:], wqkv.rearrange("l (k p) e -> p l k e", p=P)).then_inc(ff_weights, 16)
            sp.dma_start(wo_sb[:], wo.rearrange("l (k p) e -> p l k e", p=P)).then_inc(ff_weights, 16)
            sp.dma_start(w1_sb[:], w1.rearrange("l (k p) e -> p l k e", p=P)).then_inc(ff_weights, 16)
            sp.dma_start(w2_sb[:], w2.rearrange("l (j p) e -> p l j e", p=HP)).then_inc(ff_weights, 16)
            sp.dma_start(wp_sb[:], wpT.rearrange("(k p) e -> p k e", p=P)).then_inc(ff_weights, 16)
            sp.dma_start(b1_sb[:], b1).then_inc(ff_weights, 16)
            sp.dma_start(b2_sb[:], b2).then_inc(ff_weights, 16)
            sp.dma_start(lng_sb[:], ln_gain).then_inc(ff_weights, 16)
            sp.dma_start(lnb_sb[:], ln_bias).then_inc(ff_weights, 16)
            for k, src in ((0, qk_gain), (1, qk_gain_swapped)):
                for l in range(LAYERS):
                    sp.dma_start(gains[:, l, k::2, :], src[l].partition_broadcast(P)).then_inc(ff_weights, 16)

            def load_window(w, b):
                sp.dma_start(xT[:, 0, b, :, 1:], xT_dram[:, :, bass.ds(w * WINDOW + b * N, WINDOW)]
                             .rearrange("k p t -> p k t")).then_inc(x_window[b], 16)

            for b in range(B):
                load_window(0, b)
            sp.dma_start(tables[:], rotary[0]).then_inc(tables_in, 16)
            with nc.sync.Fori(0, NWIN) as i:
                for b in range(B):
                    sp.wait_ge(result_stored[b], i * 16 + 16)
                    rows = bass.ds(i * WINDOW, WINDOW)
                    sp.dma_start(x_win[:, b], x[b, rows, :]).then_inc(final_in[b], 16)
                    sp.dma_start(res_win[:, b], res_dram[bass.ds(i * WINDOW + b * N, WINDOW), :]).then_inc(final_in[b], 16)
                after = nc.sync.snap((i + 1) % NWIN)
                sp.wait_ge(tab_ready, (i + 1) * ITEMS)
                sp.dma_start(tables[:], rotary[bass.ds(after, 1)][0]).then_inc(tables_in, 16)
                for b in range(B):
                    sp.wait_ge(x_carried, turn(i, 0, b) + ITEMS)
                    load_window(after, b)
                for b in range(B):
                    sp.wait_ge(result_ready, i * B + (b + 1 + B))
                    sp.dma_start(out[b, bass.ds(i * WINDOW, WINDOW), :], s_win[:, b]).then_inc(result_stored[b], 16)
            for b in range(B):
                sp.wait_ge(result_stored[b], 16 * (NWIN + 1))
                sp.wait_ge(final_in[b], 32 * NWIN)
                sp.wait_ge(x_window[b], 16 * (NWIN + 1))
            sp.wait_ge(tables_in, 16 * (NWIN + 1))

        @block.gpsimd
        def _(pool):
            nc.gpsimd.memset(ident[:], 0.0).then_inc(pool_const, 1)
            pool.wait_ge(pool_const, 1)
            nc.gpsimd.affine_select(out=ident[:], in_=ident[:], compare_op=ALU.not_equal, fill=1.0, base=0,
                                    pattern=[[-1, P]], channel_multiplier=1).then_inc(pool_const, 1)
            pool.wait_ge(dist_red, 1)
            nc.gpsimd.partition_all_reduce(dmax[:, 1:2], dmax[:, 0:1], P, RMAX).then_inc(dist_red, 1)
            pool.wait_ge(consts_in, 16 * NCONST)
            nc.gpsimd.tensor_tensor(beta_sb[:], beta_sb[:], bproj_sb[:], ALU.add).then_inc(res_step, 1)
            with nc.gpsimd.Fori(0, NCHUNK) as c:
                for mb in range(NMB):
                    pool.wait_ge(part2, c * NMB + (mb + 1))
                    nc.gpsimd.tensor_tensor(parts[:, mb, 2 if mb < 2 else 0], rest[:, mb], parts[:, mb, 1],
                                            ALU.subtract).then_inc(part3, 1)
                pool.wait_ge(xn2_ready, c + 1)
                pool.wait_ge(res_step, c + 1)
                nc.gpsimd.tensor_tensor(xn2[:], xn2[:], gamma_sb[:].unsqueeze(1).to_broadcast([P, JT, D]),
                                        ALU.mult).then_inc(res_step, 1)
                pool.wait_ge(res_step, c + 2)
                nc.gpsimd.tensor_tensor(xn2[:], xn2[:], beta_sb[:].unsqueeze(1).to_broadcast([P, JT, D]),
                                        ALU.add).then_inc(res_ready, 1)
            nc.gpsimd.sem_inc(phase1_end, 1)
            pool.wait_ge(phase1_end, 5)
            nc.gpsimd.memset(v_cur[:], 0.0).then_inc(v_copied, 1)
            pool.wait_ge(v_copied, 1)
            nc.gpsimd.memset(v_cur[:, :, :, HD:HD + 1], 1.0).then_inc(v_copied, 1)
            pool.wait_ge(v_copied, 2)
            pool.wait_ge(v_saved, NCHUNK + 1)
            pool.wait_ge(bias_ready, 1)
            with nc.gpsimd.Fori(0, HEADS) as h:
                pool.wait_ge(pv_done, h * STEPS + 1)
                for b in range(B):
                    nc.gpsimd.tensor_copy(v_cur[:, b, :, 0:HD],
                                          v_all[:, b * KB:(b + 1) * KB, bass.ds(h * HD, HD)]).then_inc(v_copied, 1)
                for b in range(B):
                    for kb in range(3):
                        step = b * QC * KB + kb
                        pool.wait_ge(prob_ready, h * STEPS + (step + 2))
                        rows = P if kb < 2 else 1
                        tile = probs[0:rows, step % PRING, 1:PTS + 1]
                        nc.gpsimd.tensor_tensor(tile, tile, bias_exp[0:rows, kb, :], ALU.mult).then_inc(bias_done, 1)

            pool.wait_ge(bias_done, HEADS * 6)
            nc.gpsimd.sem_inc(phase2_end, 1)
            pool.wait_ge(phase2_end, 4)
            nc.gpsimd.memset(kT[:], 0.0).then_inc(ff_const, 1)
            nc.gpsimd.memset(vw[:], 0.0).then_inc(ff_const, 1)
            nc.gpsimd.memset(xT[:, 1], 0.0).then_inc(ff_const, 1)
            nc.gpsimd.memset(xT[:, 0, :, :, 0:1], 0.0).then_inc(ff_const, 1)
            nc.gpsimd.memset(x1T[:], 0.0).then_inc(ff_const, 1)
            nc.gpsimd.memset(half_power[:], -0.5).then_inc(ff_const, 1)
            nc.gpsimd.memset(one[:], 1.0).then_inc(ff_const, 1)
            nc.gpsimd.memset(mask_prev[:], 0.0).then_inc(ff_const, 1)
            nc.gpsimd.memset(mask[:, 0:WINDOW], MASKED).then_inc(ff_const, 1)
            nc.gpsimd.memset(mask[:, WINDOW:], 0.0).then_inc(ff_const, 1)
            pool.wait_ge(ff_const, 10)
            nc.gpsimd.affine_select(out=mask_prev[:], in_=mask_prev[:], compare_op=ALU.is_ge, fill=MASKED, base=0,
                                    pattern=[[1, WINDOW]], channel_multiplier=-1).then_inc(ff_const, 1)
            nc.gpsimd.affine_select(out=mask[:, WINDOW:], in_=mask[:, WINDOW:], compare_op=ALU.is_ge, fill=MASKED,
                                    base=0, pattern=[[-1, WINDOW]], channel_multiplier=1).then_inc(ff_const, 1)
            pool.wait_ge(ff_const, 12)
            for carried in (k_carried, v_carried, x_carried, x1_carried):
                nc.gpsimd.sem_inc(carried, ITEMS)
            nc.gpsimd.sem_inc(mask_set, 1)
            pool.wait_ge(ff_weights, FF_WEIGHTS)

            def move(dst, src):
                shape = src.shape
                ones = one[:]
                while len(ones.shape) < len(shape):
                    ones = ones.unsqueeze(1)
                return nc.gpsimd.tensor_tensor(dst, src, ones.to_broadcast(shape), ALU.mult)

            with nc.gpsimd.Fori(0, NWIN) as i:
                pool.wait_ge(tables_in, i * 16 + 16)
                for b in range(B):
                    for l in range(LAYERS):
                        if l == 0:
                            pool.wait_ge(turned_done, turn(i, LAYERS - 1, b))
                        nc.gpsimd.tensor_tensor(tab[:, b, l], tables[:], gains[:, l],
                                                ALU.mult).then_inc(tab_ready, 1)
                for l in range(LAYERS):
                    for b in range(B):
                        pool.wait_ge(square_sums, turn(i, l, b))
                        nc.gpsimd.tensor_tensor(norms[:, b], norms[:, b], half_power[:], ALU.pow).then_inc(inv_norms, 1)
                    for b in range(B):
                        pool.wait_ge(inv_rows, turn(i, l, b))
                        nc.gpsimd.tensor_tensor(masked[:, b], masked[:, b],
                                                psum_rows[:, b].unsqueeze(2).to_broadcast([P, LH, 2 * WINDOW]),
                                                ALU.mult).then_inc(probs_scaled, 1)
                        move(kT[:, l, b, :, 0:WINDOW], kT[:, l, b, :, WINDOW:]).then_inc(k_carried, 1)
                    for b in range(B):
                        pool.wait_ge(oT_done, turn(i, l, b))
                        move(vw[:, l, b, 0], vw[:, l, b, 1]).then_inc(v_carried, 1)
                        pool.wait_ge(x1_ready, turn(i, l, b))
                        move(xT[:, l, b, :, 0:1], xT[:, l, b, :, WINDOW:]).then_inc(x_carried, 1)
                        pool.wait_ge(var_done, turn(i, l, b))
                        nc.gpsimd.tensor_tensor(fmv[:, b, 1:2], fmv[:, b, 1:2], half_power[:, 0:1],
                                                ALU.pow).then_inc(rstd_done, 1)
                    for b in range(B):
                        pool.wait_ge(x2_ready, turn(i, l, b))
                        move(x1T[:, l, b, :, 0:1], x1T[:, l, b, :, WINDOW:]).then_inc(x1_carried, 1)
                pool.wait_ge(masked_done, i * ITEMS + ITEMS)
                move(mask[:, 0:WINDOW], mask_prev[:]).then_inc(mask_set, 1)

        @block.scalar
        def _(act):
            act.wait_ge(dist_step, 5)
            nc.scalar.activation(dist[:], dist[:], ACT.Sqrt).then_inc(dist_sqrt, 1)
            nc.scalar.sem_inc(xnT_ready, 1)
            nc.scalar.sem_inc(v_saved, 1)
            with nc.scalar.Fori(0, NCHUNK) as c:
                for n in range(2):
                    act.wait_ge(ln_var, c * 2 + (n + 1))
                    nc.scalar.activation(rstd[:, n], mv[:, n, :, 1], ACT.Sqrt).then_inc(ln_sqrt, 1)
                    if n == 0:
                        act.wait_ge(xT_done, c + 2)
                        act.wait_ge(xT_stored, (c + 1) * 16)
                        nc.scalar.copy(xnT[:], banks[:, 0:2, :]).then_inc(xnT_ready, 1)
                act.wait_ge(parts_stored, (c + 1) * (16 * PARTS * NMB))
                for mb in range(NMB):
                    act.wait_ge(qk_done, c * NMB + (mb + 1))
                    nc.scalar.copy(parts[:, mb, 0 if mb < 2 else 2], banks[:, 2 + mb, :]).then_inc(part1, 1)
                    act.wait_ge(rest_ready, (c + 1) * NMB + (mb + 1))
                    nc.scalar.copy(parts[:, mb, 1], rest[:, mb]).then_inc(part2, 1)
                act.wait_ge(v_done, c + 1)
                nc.scalar.copy(v_all[:, bass.ds(c * JT, JT), :],
                               banks[:, 6:8, :].rearrange("p a (j d) -> p (a j) d", d=D)).then_inc(v_saved, 1)
            nc.scalar.sem_inc(phase1_end, 1)
            act.wait_ge(phase1_end, 5)
            act.wait_ge(dist_scale, 1)
            nc.scalar.activation(bias_exp[:], dist[:], ACT.Exp, scale=dmax[:, 4:5]).then_inc(dist_exp, 1)

            def save_shift(group, use):
                b, qc = (group // QC) % B, group % QC
                nc.scalar.copy(q_aug[TERM_ROWS:AUG, b, qc * CHUNK:(qc + 1) * CHUNK],
                               banks[TERM_ROWS:AUG, use % SRING, 0:CHUNK // 2].bitcast(BF16)).then_inc(shift_saved, 1)

            def save_sums(h, group):
                act.wait_ge(pv_done, h * STEPS + ((group + 1) * KB + 1))
                act.wait_ge(sel_done, h * GROUPS + (group + 1))
                nc.scalar.copy(acc_sb[:], banks[:, 3, :]).then_inc(acc_saved, 1)

            nc.scalar.sem_inc(prob_ready, 1)
            act.wait_ge(st_ready, 1)
            save_shift(0, 0)
            with nc.scalar.Fori(0, HEADS) as h:
                use = 0
                for step in range(STEPS):
                    group, kb = step // KB, step % KB
                    act.wait_ge(st_ready, h * ST_USES + (use + 2))
                    act.wait_ge(pv_done, h * STEPS + max(1, step - PRING + 2))
                    nc.scalar.activation(probs[:, step % PRING, :], banks[:, use % SRING, :], ACT.Exp,
                                         scale=SCALE).then_inc(prob_ready, 1)
                    use += 1
                    if kb == MSTEP:
                        act.wait_ge(st_ready, h * ST_USES + (use + 2))
                        save_shift(group + 1, use)
                        use += 1
                    if kb == SUMS_STEP and group > 0:
                        save_sums(h, group - 1)
                save_sums(h, GROUPS - 1)

            act.wait_ge(acc_saved, HEADS * GROUPS)
            act.wait_ge(prob_ready, HEADS * STEPS + 1)
            act.wait_ge(shift_saved, HEADS * GROUPS + 1)
            nc.scalar.sem_inc(phase2_end, 1)
            act.wait_ge(phase2_end, 4)
            act.wait_ge(ff_const, 12)
            act.wait_ge(ff_weights, FF_WEIGHTS)
            with nc.scalar.Fori(0, NWIN) as i:
                for l in range(LAYERS):
                    for b in range(B):
                        act.wait_ge(qkv_done, turn(i, l, b))
                        nc.scalar.activation(squares[:, b], banks[:, lanes(b):lanes(b) + 2, :],
                                             ACT.Square).then_inc(squares_done, 1)
                        act.wait_ge(v_carried, turn(i, l, b))
                        nc.scalar.copy(vw[:, l, b, 1], banks[:, lanes(b) + 2, :]).then_inc(v_kept, 1)
                    for b in range(B):
                        act.wait_ge(qkT_done, turn(i, l, b))
                        nc.scalar.copy(qT[:, b], banks[:, lanes(b) + 3, :]).then_inc(qT_kept, 1)
                        act.wait_ge(k_carried, turn(i, l, b))
                        nc.scalar.copy(kT[:, l, b, :, WINDOW:],
                                       banks[:, lanes(b), :].rearrange("p (j t) -> p j t", t=WINDOW)).then_inc(kT_kept, 1)
                    for b in range(B):
                        act.wait_ge(peaks_done, turn(i, l, b))
                        for hh in range(LH):
                            last = nc.scalar.activation(masked[:, b, hh, :], masked[:, b, hh, :], ACT.Exp,
                                                        bias=npeak[:, b, hh:hh + 1], scale=QK_SCALE,
                                                        accum_out=psum_rows[:, b, hh:hh + 1])
                        last.then_inc(exp_done, 1)
                    for b in range(B):
                        act.wait_ge(pT_done, turn(i, l, b))
                        nc.scalar.copy(pT[:, b, 0:LH // 2], banks[:, lanes(b):lanes(b) + 2, :]).then_inc(pT_kept0, 1)
                    for b in range(B):
                        act.wait_ge(oT_done, turn(i, l, b))
                        nc.scalar.copy(oT[:, b], banks[:, lanes(b), :]).then_inc(oT_kept, 1)
                    for b in range(B):
                        act.wait_ge(hnT_done, turn(i, l, b))
                        for f in range(2):
                            last = nc.scalar.activation(hnT[:, b, f], banks[:, lanes(b) + 3, f * P:(f + 1) * P],
                                                        ACT.Identity, bias=lnb_sb[:, l, f:f + 1],
                                                        scale=lng_sb[:, l, f:f + 1])
                        last.then_inc(hnT_kept, 1)
                    for b in range(B):
                        act.wait_ge(w1_done, turn(i, l, b))
                        for j in range(HB):
                            last = nc.scalar.activation(gated[:, b, j], banks[0:HP, lanes(b) + 2 + j // 4,
                                                                              (j % 4) * P:(j % 4 + 1) * P],
                                                        ACT.Gelu, bias=b1_sb[:, l, HB + j:HB + j + 1])
                        last.then_inc(gelu_done, 1)
                for b in range(B):
                    act.wait_ge(owT_done, i * B + (b + 1))
                    nc.scalar.copy(o_winT[:, b], banks[:, lanes(b) + 2, 0:2 * P]).then_inc(owT_kept, 1)
                for b in range(B):
                    act.wait_ge(y_done, i * B + (b + 1))
                    nc.scalar.activation(silu[:, b], banks[:, lanes(b) + 1, 0:D], ACT.Exp, scale=-1.0).then_inc(exp_neg, 1)

        @block.vector
        def _(dve):
            dve.wait_ge(dist_in, 16 * 5)
            for kb in range(3):
                nc.vector.tensor_scalar(dist[:, kb, :], crow[:, 0, :], ccol[:, kb, 0:1], None, ALU.subtract)
                last = nc.vector.tensor_scalar(dtmp[:, kb, :], crow[:, 1, :], ccol[:, kb, 1:2], None, ALU.subtract)
            last.then_inc(dist_step, 1)
            dve.wait_ge(dist_step, 1)
            nc.vector.tensor_tensor(dist[:], dist[:], dist[:], ALU.mult).then_inc(dist_step, 1)
            nc.vector.tensor_tensor(dtmp[:], dtmp[:], dtmp[:], ALU.mult).then_inc(dist_step, 1)
            dve.wait_ge(dist_step, 3)
            nc.vector.tensor_tensor(dist[:], dist[:], dtmp[:], ALU.add).then_inc(dist_step, 2)
            dve.wait_ge(dist_sqrt, 1)
            nc.vector.tensor_reduce(dmax[:, 0:1], dist[:], AX.XY, ALU.max).then_inc(dist_red, 1)
            dve.wait_ge(dist_red, 2)
            nc.vector.tensor_scalar(dmax[:, 2:3], dmax[:, 1:2], DIST_MIN, None, ALU.max).then_inc(dist_step, 1)
            nc.vector.tensor_scalar(dmax[:, 3:4], dmax[:, 1:2], DIST_MIN, -BIAS_STRENGTH, ALU.is_gt,
                                    ALU.mult).then_inc(dist_step, 1)
            dve.wait_ge(dist_step, 7)
            nc.vector.reciprocal(dmax[:, 5:6], dmax[:, 2:3]).then_inc(dist_step, 1)
            dve.wait_ge(dist_step, 8)
            nc.vector.tensor_tensor(dmax[:, 4:5], dmax[:, 5:6], dmax[:, 3:4], ALU.mult).then_inc(dist_scale, 1)

            def layer_norm(c, n, src, dst, done):
                base = n * 5
                for j in range(JT):
                    last = nc.vector.bn_stats(stats[:, j, :], src[:, j, :])
                last.then_inc(ln_dve, 1)
                dve.wait_ge(ln_dve, c * 10 + (base + 1))
                even, odd = stats[:, :, 1:3], stats[:, :, 4:6]
                nc.vector.tensor_tensor(total[:], even, odd, ALU.add)
                nc.vector.tensor_tensor(between[:], even[:, :, 0], odd[:, :, 0], ALU.subtract).then_inc(ln_dve, 1)
                dve.wait_ge(ln_dve, c * 10 + (base + 2))
                nc.vector.tensor_tensor(between[:], between[:], between[:], ALU.mult)
                nc.vector.tensor_scalar(mv[:, n, :, 0], total[:, :, 0], 0.5, None, ALU.mult).then_inc(ln_dve, 1)
                dve.wait_ge(ln_dve, c * 10 + (base + 3))
                nc.vector.scalar_tensor_tensor(between[:], between[:], D / 4.0, total[:, :, 1], ALU.mult,
                                               ALU.add).then_inc(ln_dve, 1)
                dve.wait_ge(ln_dve, c * 10 + (base + 4))
                nc.vector.tensor_scalar(mv[:, n, :, 1], between[:], 1.0 / D, LN_EPS, ALU.mult, ALU.add
                                        ).then_inc(ln_var, 1)
                dve.wait_ge(ln_sqrt, c * 2 + (n + 1))
                nc.vector.reciprocal(rstd[:, n], rstd[:, n]).then_inc(ln_dve, 1)
                dve.wait_ge(ln_dve, c * 10 + (base + 5))
                for j in range(JT):
                    last = nc.vector.tensor_scalar(dst[:, j, :], src[:, j, :], mv[:, n, j, 0:1], rstd[:, n, j:j + 1],
                                                   ALU.subtract, ALU.mult)
                last.then_inc(done, 1)

            nc.vector.sem_inc(rest_ready, NMB)
            with nc.vector.Fori(0, NCHUNK // 2) as it:
                for u in range(2):
                    c = it * 2 + u
                    dve.wait_ge(x_loaded[u], it * 16 + 16)
                    dve.wait_ge(xT_done, c + 1)
                    layer_norm(c, 0, x_in[:, u], xn, xn_ready)
                    dve.wait_ge(res_stored, (c + 1) * 16)
                    dve.wait_ge(xn_ready, c + 1)
                    layer_norm(c, 1, xn, xn2, xn2_ready)
                    for mb in range(NMB):
                        dve.wait_ge(part1, c * NMB + (mb + 1))
                        nc.vector.tensor_tensor(rest[:, mb], banks[:, 2 + mb, :], parts[:, mb, 0 if mb < 2 else 2],
                                                ALU.subtract).then_inc(rest_ready, 1)
            nc.vector.sem_inc(phase1_end, 1)
            dve.wait_ge(phase1_end, 5)
            dve.wait_ge(dist_exp, 1)
            nc.vector.memset(bias_exp[0:1, 0, :], 1.0).then_inc(bias_ready, 1)
            nc.vector.tensor_copy(identb[:], ident[:]).then_inc(dve_const, 1)
            for b in range(B):
                last = nc.vector.memset(k_aug[TERM_ROWS:AUG, b, :], -1.0)
            last.then_inc(dve_const, 1)

            def max_pair(before, t):
                q, half = (t // 2) % QC, t % 2
                dve.wait_ge(smax_ready, before + (t + 1))
                nc.vector.tensor_reduce(pair_max[:, q, half:half + 1], banks[:, 4 + 2 * (t % 2):6 + 2 * (t % 2), :],
                                        AX.XY, ALU.max).then_inc(smax_read, 1)

            def split_max(before, group):
                dve.wait_ge(smax_read, before * (PAIRS // GROUPS) + (group + 1) * (PAIRS // GROUPS) + 2)
                if group > 0:
                    dve.wait_ge(shift_saved, before + group)
                nc.vector.tensor_tensor(row_max[:], pair_max[:, :, 0], pair_max[:, :, 1], ALU.max).then_inc(max_step, 1)
                dve.wait_ge(max_step, before * 2 + (2 * group + 1))
                nc.vector.tensor_copy(shift[:, :, 0], row_max[:]).then_inc(max_step, 1)
                dve.wait_ge(max_step, before * 2 + (2 * group + 2))
                nc.vector.tensor_tensor(shift[:, :, 1], row_max[:], shift[:, :, 0], ALU.subtract).then_inc(shift_ready, 1)

            def save_attention(h, group):
                dve.wait_ge(sel_done, h * GROUPS + (group + 2))
                columns = banks[:, 3, :].rearrange("p (j g r) -> p j r g", g=4, r=VW)[:, :, 0:HD + 1, :]
                nc.vector.tensor_reduce(sums[:], columns, AX.X, ALU.add).then_inc(sums_done, 1)
                dve.wait_ge(sums_done, h * GROUPS + (group + 2))
                nc.vector.reciprocal(inv_sum[:], sums[:, :, HD]).then_inc(inv_done, 1)
                dve.wait_ge(inv_done, h * GROUPS + (group + 1))
                nc.vector.tensor_tensor(attn_tok[:, group * JT:(group + 1) * JT, bass.ds(h * HD, HD)],
                                        sums[:, :, 0:HD], inv_sum[:].unsqueeze(2).to_broadcast([P, JT, HD]),
                                        ALU.mult).then_inc(attn_saved, 1)

            nc.vector.sem_inc(smax_read, 2)
            nc.vector.sem_inc(sums_done, 1)
            for t in range(PAIRS // GROUPS):
                max_pair(0, t)
            split_max(0, 0)
            for t in range(PAIRS // GROUPS, (LEAD + 1) // 2 - 1):
                max_pair(0, t)
            with nc.vector.Fori(0, HEADS) as h:
                for step in range(STEPS):
                    group, kb = step // KB, step % KB
                    tile = step + LEAD
                    if tile % 2 == 1:
                        max_pair(h * PAIRS, tile // 2)
                    if tile % KB == KB - 1:
                        split_max(h * GROUPS, tile // KB)
                    if kb == KEEP_STEP and group > 0:
                        save_attention(h, group - 1)
                save_attention(h, GROUPS - 1)

            dve.wait_ge(attn_saved, HEADS * GROUPS)
            nc.vector.sem_inc(phase2_end, 1)
            dve.wait_ge(phase2_end, 4)
            dve.wait_ge(ff_const, 12)
            dve.wait_ge(ff_weights, FF_WEIGHTS)
            nc.vector.sem_inc(result_ready, B)
            nc.vector.sem_inc(turned_done, ITEMS)
            with nc.vector.Fori(0, NWIN) as i:
                steps = [0]

                def link(instruction):
                    steps[0] += 1
                    instruction.then_inc(dve_step, 1)
                    dve.wait_ge(dve_step, i * DVE_STEPS + steps[0])

                for l in range(LAYERS):
                    for b in range(B):
                        qk = banks[:, lanes(b):lanes(b) + 2, :].rearrange("p s (h d) -> p s h d", d=LD)
                        dve.wait_ge(squares_done, turn(i, l, b))
                        dve.wait_ge(tab_ready, i * ITEMS + (b * LAYERS + l + 1))
                        cos, sin = tab[:, b, l, 0::2, :], tab[:, b, l, 1::2, :]
                        tu = turned[:, b].rearrange("p s (h d) -> p s h d", d=LD)
                        cr = crossed[:, b].rearrange("p s (h d) -> p s h d", d=LD)
                        nc.vector.tensor_reduce(norms[:, b], squares[:, b].rearrange("p s (h d) -> p (s h) d", d=LD),
                                                AX.X, ALU.add).then_inc(norm_sums, 1)
                        nc.vector.tensor_tensor(tu, qk, cos.unsqueeze(2).to_broadcast([P, 2, LH, LD]), ALU.mult)
                        H2 = LD // 2
                        for half in range(2):
                            o = slice(half * H2, (half + 1) * H2)
                            s_ = slice((1 - half) * H2, (2 - half) * H2)
                            last = nc.vector.tensor_tensor(cr[:, :, :, o], qk[:, :, :, s_],
                                                           sin[:, :, o].unsqueeze(2).to_broadcast([P, 2, LH, H2]),
                                                           ALU.mult)
                        dve.wait_ge(norm_sums, turn(i, l, b))
                        nc.vector.tensor_scalar(norms[:, b], norms[:, b], NORM_MIN * NORM_MIN, None,
                                                ALU.max).then_inc(square_sums, 1)
                        link(last)
                        link(nc.vector.tensor_tensor(turned[:, b], turned[:, b], crossed[:, b], ALU.add))
                        dve.wait_ge(inv_norms, turn(i, l, b))
                        t16 = turned[:, b].rearrange("p s (h d) -> p (s h) d", d=LD)
                        nc.vector.tensor_tensor(t16, t16, norms[:, b].unsqueeze(2).to_broadcast([P, 2 * LH, LD]),
                                                ALU.mult).then_inc(turned_done, 1)
                    for b in range(B):
                        dve.wait_ge(scores_done, turn(i, l, b))
                        dve.wait_ge(mask_set, i + 1)
                        link(nc.vector.tensor_tensor(masked[:, b], banks[:, lanes(b):lanes(b) + 4, :]
                                                     .rearrange("p a (g t) -> p (a g) t", t=2 * WINDOW),
                                                     mask[:].unsqueeze(1).to_broadcast([P, LH, 2 * WINDOW]), ALU.add))
                        nc.vector.sem_inc(masked_done, 1)
                        link(nc.vector.tensor_reduce(peak[:, b], masked[:, b], AX.X, ALU.max))
                        nc.vector.tensor_scalar(npeak[:, b], peak[:, b], -QK_SCALE, None, ALU.mult).then_inc(peaks_done, 1)
                    for b in range(B):
                        dve.wait_ge(exp_done, turn(i, l, b))
                        nc.vector.reciprocal(psum_rows[:, b], psum_rows[:, b]).then_inc(inv_rows, 1)
                    for b in range(B):
                        dve.wait_ge(pT_done, turn(i, l, b))
                        nc.vector.tensor_copy(pT[:, b, LH // 2:], banks[:, lanes(b) + 2:lanes(b) + 4, :]
                                              .rearrange("p a (g c t) -> p (a g) c t", c=2, t=WINDOW)).then_inc(pT_kept1, 1)
                    for b in range(B):
                        dve.wait_ge(wo_done, turn(i, l, b))
                        dve.wait_ge(x1_carried, turn(i, l, b))
                        nc.vector.tensor_tensor(x1T[:, l, b, :, 1:], banks[:, lanes(b) + 1, 0:D]
                                                .rearrange("p (f t) -> p f t", t=WINDOW), xT[:, l, b, :, 1:],
                                                ALU.add).then_inc(x1_ready, 1)
                    for b in range(B):
                        h_tok = banks[:, lanes(b) + 2, 0:D]
                        dve.wait_ge(h_done, turn(i, l, b))
                        link(nc.vector.bn_stats(fstats[:, b], h_tok))
                        nc.vector.tensor_tensor(ftotal[:, b], fstats[:, b, 1:3], fstats[:, b, 4:6], ALU.add)
                        link(nc.vector.tensor_tensor(fbetween[:, b], fstats[:, b, 1:2], fstats[:, b, 4:5], ALU.subtract))
                        nc.vector.tensor_tensor(fbetween[:, b], fbetween[:, b], fbetween[:, b], ALU.mult)
                        link(nc.vector.tensor_scalar(fmv[:, b, 0:1], ftotal[:, b, 0:1], 0.5, None, ALU.mult))
                        link(nc.vector.scalar_tensor_tensor(fbetween[:, b], fbetween[:, b], D / 4.0, ftotal[:, b, 1:2],
                                                            ALU.mult, ALU.add))
                        nc.vector.tensor_scalar(fmv[:, b, 1:2], fbetween[:, b], 1.0 / D, LN_EPS, ALU.mult,
                                                ALU.add).then_inc(var_done, 1)
                    for b in range(B):
                        dve.wait_ge(rstd_done, turn(i, l, b))
                        nc.vector.tensor_scalar(hn[:, b], banks[:, lanes(b) + 2, 0:D], fmv[:, b, 0:1], fmv[:, b, 1:2],
                                                ALU.subtract, ALU.mult).then_inc(hn_ready, 1)
                    for b in range(B):
                        dve.wait_ge(gelu_done, turn(i, l, b))
                        for j in range(HB):
                            last = nc.vector.scalar_tensor_tensor(
                                uT[:, b, j], banks[0:HP, lanes(b) + j // 4, (j % 4) * P:(j % 4 + 1) * P],
                                b1_sb[:, l, j:j + 1], gated[:, b, j], ALU.add, ALU.mult)
                        last.then_inc(u_ready, 1)
                    for b in range(B):
                        dve.wait_ge(w2_done, turn(i, l, b))
                        if l < LAYERS - 1:
                            dve.wait_ge(x_carried, turn(i, l + 1, b))
                            dst = xT[:, l + 1, b, :, 1:]
                        else:
                            dst = yT[:, b]
                        for f in range(2):
                            last = nc.vector.scalar_tensor_tensor(
                                dst[:, f], banks[:, lanes(b), f * P:(f + 1) * P], b2_sb[:, l, f:f + 1],
                                x1T[:, l, b, f, 1:], ALU.add, ALU.add)
                        last.then_inc(x2_ready, 1)
                for b in range(B):
                    nc.vector.tensor_copy(o_win[:, b], attn_tok[:, bass.ds(i + b * NWIN, 1), :][:, 0]).then_inc(o_copied, 1)
                for b in range(B):
                    dve.wait_ge(y_done, i * B + (b + 1))
                    dve.wait_ge(exp_neg, i * B + (b + 1))
                    dve.wait_ge(final_in[b], i * 32 + 32)
                    nc.vector.tensor_tensor(s_win[:, b], banks[:, lanes(b) + 3, 0:D], res_win[:, b], ALU.add)
                    link(nc.vector.tensor_scalar(silu[:, b], silu[:, b], 1.0, None, ALU.add))
                    link(nc.vector.reciprocal(silu[:, b], silu[:, b]))
                    link(nc.vector.tensor_tensor(silu[:, b], banks[:, lanes(b) + 1, 0:D], silu[:, b], ALU.mult))
                    link(nc.vector.tensor_tensor(s_win[:, b], s_win[:, b], silu[:, b], ALU.mult))
                    nc.vector.tensor_tensor(s_win[:, b], s_win[:, b], x_win[:, b], ALU.add).then_inc(result_ready, 1)
                assert steps[0] == DVE_STEPS, steps[0]

        @block.tensor
        def _(pe):
            pe.wait_ge(pool_const, 2)
            pe.wait_ge(consts_in, 16 * NCONST)
            nc.tensor.sem_inc(xT_done, 1)
            with nc.tensor.Fori(0, NCHUNK) as c:
                pe.wait_ge(xn_ready, c + 1)
                pe.wait_ge(xnT_ready, c + 1)
                for k in range(2):
                    for j in range(JT):
                        last = nc.tensor.transpose(banks[:, k, j * P:(j + 1) * P], xn[:, j, k * P:(k + 1) * P], ident[:])
                last.then_inc(xT_done, 1)
                pe.wait_ge(xnT_ready, c + 2)
                pe.wait_ge(rest_ready, (c + 1) * NMB)
                for mb in range(NMB):
                    for k in range(2):
                        last = nc.tensor.matmul(banks[:, 2 + mb, :], wqk_sb[:, k, mb * P:(mb + 1) * P], xnT[:, k, :],
                                                start=(k == 0), stop=(k == 1))
                    last.then_inc(qk_done, 1)
                pe.wait_ge(v_saved, c + 1)
                for j in range(JT):
                    for k in range(2):
                        last = nc.tensor.matmul(banks[:, 6 + j // 2, (j % 2) * D:(j % 2 + 1) * D],
                                                xnT[:, k, j * P:(j + 1) * P], wv_sb[:, k, :],
                                                start=(k == 0), stop=(k == 1))
                last.then_inc(v_done, 1)
            nc.tensor.sem_inc(phase1_end, 1)
            pe.wait_ge(phase1_end, 5)
            pe.wait_ge(dve_const, 2)

            def max_tile(before, t):
                pair, b, q, kq = t // 2, (t // (QC * KB)) % B, (t // (N // BANK)) % KB, t % (N // BANK)
                if t % 2 == 0:
                    pe.wait_ge(smax_read, before + (pair + 1))
                mm = nc.tensor.matmul(banks[:, 4 + t % 4, :], q_aug[0:MAX_ROWS, b, q * P:(q + 1) * P],
                                      k_aug[0:MAX_ROWS, b, kq * BANK:(kq + 1) * BANK], start=True, stop=True)
                if t % 2 == 1:
                    mm.then_inc(smax_ready, 1)

            def bank_free(h, use):
                if use < SRING:
                    pe.wait_ge(prob_ready, h * STEPS + 1)
                    return
                group, kb = divmod(use - SRING, KB + 1)
                if kb == MSTEP + 1:
                    pe.wait_ge(shift_saved, h * GROUPS + (group + 2))
                else:
                    pe.wait_ge(prob_ready, h * STEPS + (group * KB + kb - (kb > MSTEP) + 2))

            def shift_rows(h, group, use):
                pe.wait_ge(shift_ready, h * GROUPS + (group + 1))
                bank_free(h, use)
                for j in range(JT):
                    last = nc.tensor.transpose(
                        banks[TERM_ROWS:AUG, use % SRING, j * P // 2:(j + 1) * P // 2].bitcast(BF16),
                        shift[:, j, :], identb[:])
                last.then_inc(st_ready, 1)

            def weighted(h, group, kb):
                step = group * KB + kb
                b = group // QC
                if kb == 0:
                    pe.wait_ge(sums_done, h * GROUPS + (group + 1))
                    pe.wait_ge(v_copied, h * 2 + (3 + b))
                if group % QC == 0 and kb < 3:
                    pe.wait_ge(bias_done, h * 6 + (b * 3 + kb + 1))
                else:
                    pe.wait_ge(prob_ready, h * STEPS + (step + 2))
                g = kb % 4
                mm = nc.tensor.matmul(banks[32 * g:32 * g + VW, 3, :], v_cur[:, b, kb, :], probs[:, step % PRING, :],
                                      start=(kb < 4), stop=(kb >= KB - 4))
                mm.then_inc(pv_done, 1)

            def add_groups(h, group):
                pe.wait_ge(acc_saved, h * GROUPS + (group + 1))
                for j in range(JT):
                    last = nc.tensor.transpose(banks[:, 3, j * P:(j + 1) * P], acc_sb[:, j * P:(j + 1) * P], ident[:])
                last.then_inc(sel_done, 1)

            nc.tensor.sem_inc(pv_done, 1)
            nc.tensor.sem_inc(sel_done, 1)
            pe.wait_ge(aug_loaded[0], 16 * 6)
            for t in range(KB):
                max_tile(0, t)
            shift_rows(0, 0, 0)
            for t in range(KB, LEAD):
                max_tile(0, t)
            with nc.tensor.Fori(0, HEADS) as h:
                use = 0
                for step in range(STEPS):
                    group, kb = step // KB, step % KB
                    b, qc = group // QC, group % QC
                    if kb == 0:
                        pe.wait_ge(shift_saved, h * GROUPS + (group + 1))
                    bank_free(h, use)
                    nc.tensor.matmul(banks[:, use % SRING, :], k_aug[0:AUG, b, kb * P:(kb + 1) * P],
                                     q_aug[0:AUG, b, qc * CHUNK:(qc + 1) * CHUNK], start=True,
                                     stop=True).then_inc(st_ready, 1)
                    use += 1
                    tile = step + LEAD
                    if tile == STEPS // 2:
                        pe.wait_ge(aug_loaded[1], h * 96 + 96)
                    if tile == STEPS:
                        pe.wait_ge(aug_loaded[0], h * 96 + 192)
                    max_tile(h * PAIRS, tile)
                    ago, first = PV_PLAN.get(kb, (-GROUPS, 0))
                    if group + ago >= 0:
                        for key in range(first, first + 4):
                            weighted(h, group + ago, key)
                    if kb == ADD_STEP and group > 0:
                        add_groups(h, group - 1)
                    if kb == MSTEP:
                        shift_rows(h, group + 1, use)
                        use += 1
                for key in range(KB - 4, KB):
                    weighted(h, GROUPS - 1, key)
                add_groups(h, GROUPS - 1)

            pe.wait_ge(sel_done, HEADS * GROUPS + 1)
            nc.tensor.sem_inc(phase2_end, 1)
            pe.wait_ge(phase2_end, 4)
            pe.wait_ge(ff_const, 12)
            pe.wait_ge(ff_weights, FF_WEIGHTS)
            with nc.tensor.Fori(0, NWIN) as i:
                for l in range(LAYERS):
                    for b in range(B):
                        if l == 0:
                            pe.wait_ge(x_window[b], i * 16 + 16)
                            pe.wait_ge(result_ready, i * B + (b + 1))
                        else:
                            pe.wait_ge(x2_ready, turn(i, l - 1, b))
                        for n in range(3):
                            for k in range(2):
                                last = nc.tensor.matmul(banks[:, lanes(b) + n, :], xT[:, l, b, k, 1 - k:1 - k + WINDOW],
                                                        wqkv_sb[:, l, k, n * INNER:(n + 1) * INNER],
                                                        start=(k == 0), stop=(k == 1))
                        last.then_inc(qkv_done, 1)
                    for b in range(B):
                        pe.wait_ge(turned_done, turn(i, l, b) + ITEMS)
                        for j in range(NPAIR):
                            nc.tensor.transpose(banks[:, lanes(b) + 3, j * P:(j + 1) * P],
                                                turned[:, b, 0, j * P:(j + 1) * P], ident[:])
                            last = nc.tensor.transpose(banks[:, lanes(b), j * P:(j + 1) * P],
                                                       turned[:, b, 1, j * P:(j + 1) * P], ident[:])
                        last.then_inc(qkT_done, 1)
                    for b in range(B):
                        pe.wait_ge(qT_kept, turn(i, l, b))
                        pe.wait_ge(kT_kept, turn(i, l, b))
                        pe.wait_ge(v_kept, turn(i, l, b))
                        for hh in range(LH):
                            r = slice((hh % 2) * LD, (hh % 2 + 1) * LD)
                            col = (place(hh) % 2) * 2 * WINDOW
                            last = nc.tensor.matmul(banks[:, lanes(b) + place(hh) // 2, col:col + 2 * WINDOW],
                                                    qT[r, b, hh // 2, :], kT[r, l, b, hh // 2, :], start=True, stop=True)
                        last.then_inc(scores_done, 1)
                    for b in range(B):
                        pe.wait_ge(probs_scaled, turn(i, l, b))
                        pe.wait_ge(masked_done, turn(i, l, b))
                        for hh in range(LH):
                            for c in range(2):
                                col = ((hh % 2) * 2 + c) * P
                                last = nc.tensor.transpose(banks[:, lanes(b) + hh // 2, col:col + P],
                                                           masked[:, b, hh, c * P:(c + 1) * P], ident[:])
                        last.then_inc(pT_done, 1)
                    for b in range(B):
                        pe.wait_ge(pT_kept0, turn(i, l, b))
                        pe.wait_ge(pT_kept1, turn(i, l, b))
                        for j in range(NPAIR):
                            for c in range(2):
                                for r in range(PAIR):
                                    hh = j * PAIR + r
                                    last = nc.tensor.matmul(banks[r * LD:(r + 1) * LD, lanes(b), j * P:(j + 1) * P],
                                                            vw[:, l, b, c, hh * LD:(hh + 1) * LD], pT[:, b, place(hh), c, :],
                                                            start=(c == 0), stop=(c == 1))
                        last.then_inc(oT_done, 1)
                    for b in range(B):
                        pe.wait_ge(oT_kept, turn(i, l, b))
                        for f in range(2):
                            for j in range(NPAIR):
                                last = nc.tensor.matmul(banks[:, lanes(b) + 1, f * P:(f + 1) * P],
                                                        wo_sb[:, l, j, f * P:(f + 1) * P], oT[:, b, j, :],
                                                        start=(j == 0), stop=(j == NPAIR - 1))
                        last.then_inc(wo_done, 1)
                    for b in range(B):
                        pe.wait_ge(x1_ready, turn(i, l, b))
                        for f in range(2):
                            last = nc.tensor.transpose(banks[:, lanes(b) + 2, f * P:(f + 1) * P],
                                                       x1T[:, l, b, f, 1 - f:1 - f + WINDOW], ident[:])
                        last.then_inc(h_done, 1)
                    for b in range(B):
                        pe.wait_ge(hn_ready, turn(i, l, b))
                        for f in range(2):
                            last = nc.tensor.transpose(banks[:, lanes(b) + 3, f * P:(f + 1) * P],
                                                       hn[:, b, f * P:(f + 1) * P], ident[:])
                        last.then_inc(hnT_done, 1)
                    for b in range(B):
                        pe.wait_ge(hnT_kept, turn(i, l, b))
                        for part in range(2):
                            for j in range(HB):
                                for k in range(2):
                                    col = (part * HB + j) * HP
                                    last = nc.tensor.matmul(
                                        banks[0:HP, lanes(b) + 2 * part + j // 4, (j % 4) * P:(j % 4 + 1) * P],
                                        w1_sb[:, l, k, col:col + HP], hnT[:, b, k, :], start=(k == 0), stop=(k == 1))
                        last.then_inc(w1_done, 1)
                    for b in range(B):
                        pe.wait_ge(u_ready, turn(i, l, b))
                        for f in range(2):
                            for j in range(HB):
                                last = nc.tensor.matmul(banks[:, lanes(b), f * P:(f + 1) * P],
                                                        w2_sb[:, l, j, f * P:(f + 1) * P], uT[:, b, j, :],
                                                        start=(j == 0), stop=(j == HB - 1))
                        last.then_inc(w2_done, 1)
                for b in range(B):
                    pe.wait_ge(o_copied, i * B + (b + 1))
                    pe.wait_ge(gelu_done, turn(i, LAYERS - 1, b))
                    for f in range(2):
                        last = nc.tensor.transpose(banks[:, lanes(b) + 2, f * P:(f + 1) * P],
                                                   o_win[:, b, f * P:(f + 1) * P], ident[:])
                    last.then_inc(owT_done, 1)
                for b in range(B):
                    pe.wait_ge(owT_kept, i * B + (b + 1))
                    for k in range(2):
                        nc.tensor.matmul(banks[:, lanes(b) + 3, 0:D], o_winT[:, b, k, :], wp_sb[:, k, :],
                                         start=(k == 0), stop=(k == 1))
                    pe.wait_ge(x2_ready, turn(i, LAYERS - 1, b))
                    for f in range(2):
                        last = nc.tensor.transpose(banks[:, lanes(b) + 1, f * P:(f + 1) * P], yT[:, b, f, :], ident[:])
                    last.then_inc(y_done, 1)


_INS = {
    "x": lambda i: i["L0_attn_x"],
    "wqkT": lambda i: i["L0_attn_W_qkv"][:2 * D].T,
    "wvT": lambda i: i["L0_attn_W_qkv"][2 * D:].T,
    "wpT": lambda i: i["L0_attn_W_proj"].T,
    "b_proj": lambda i: i["L0_attn_b_proj"],
    "gamma": lambda i: i["L0_attn_ln_gamma"],
    "beta": lambda i: i["L0_attn_ln_beta"],
    "centers": lambda i: i["L0_attn_spatial_centers"],
    "centersT": lambda i: i["L0_attn_spatial_centers"].T,
    "wqkv": lambda i: i["L0_ffn_wqkv"],
    "qk_gain": lambda i: np.stack([i["L0_ffn_q_scale"], i["L0_ffn_k_scale"]], axis=1),
    "qk_gain_swapped": lambda i: swapped(np.stack([i["L0_ffn_q_scale"], i["L0_ffn_k_scale"]], axis=1)),
    "rotary": lambda i: rotary_tables(),
    "wo": lambda i: i["L0_ffn_wo"],
    "ln_gain": lambda i: by_block(i["L0_ffn_ln_g"], 2, P),
    "ln_bias": lambda i: by_block(i["L0_ffn_ln_b"], 2, P),
    "w1": lambda i: pad_hidden(i["L0_ffn_w1"], 2),
    "b1": lambda i: by_block(pad_hidden(i["L0_ffn_b1"], 1), 2 * HB, HP),
    "w2": lambda i: pad_hidden(i["L0_ffn_w2"], 1),
    "b2": lambda i: by_block(i["L0_ffn_b2"], 2, P),
}


def rotary_tables():
    half = np.arange(0, LD, 2, dtype=np.float32)
    inv_freq = (np.float32(1.0) / np.float32(10000.0) ** (half / np.float32(LD))).astype(np.float32)
    t = np.arange(N, dtype=np.float32)
    freqs = np.concatenate([t[:, None] * inv_freq] * 2, axis=-1)
    base = (half + np.float32(0.4 * LD)) / np.float32(1.4 * LD)
    power = (t - np.float32(N // 2)) / np.float32(WINDOW // 2)
    scale = np.concatenate([base[None, :] ** power[:, None]] * 2, axis=-1).astype(np.float32)
    sign = np.where(np.arange(LD) < LD // 2, np.float32(-1), np.float32(1))
    cos, sin = np.cos(freqs), np.sin(freqs) * sign
    tabs = np.stack([cos * scale, sin * scale, cos / scale, sin / scale], axis=1)
    return np.ascontiguousarray(tabs.reshape(NWIN, WINDOW, 4, LD), dtype=np.float32)


def swapped(a):
    return np.concatenate([a[..., LD // 2:], a[..., :LD // 2]], axis=-1)


def by_block(a, blocks, size):
    return a.reshape(a.shape[0], blocks, size).transpose(2, 0, 1)


def pad_hidden(a, axis):
    halves = np.split(a, a.shape[axis] // HID, axis=axis)
    width = [(0, 0)] * a.ndim
    width[axis] = (0, HB * HP - HID)
    return np.concatenate([np.pad(p, width) for p in halves], axis=axis)

def kernel(**inputs):
    import numpy as _np
    import concourse.bacc as _bacc
    from concourse import mybir as _mybir
    from concourse.bass_utils import run_bass_kernel_spmd as _run

    nc = _bacc.Bacc("TRN2", target_bir_lowering=False, num_devices=1)
    arrays, args = {}, []
    for name, lay in _INS.items():
        a = _np.ascontiguousarray(lay(inputs))
        arrays[f"in_{name}"] = a
        args.append(nc.dram_tensor(f"in_{name}", a.shape, _mybir.dt.from_np(a.dtype), kind="ExternalInput").ap())
    out = nc.dram_tensor("out_0", (B, N, D), F32, kind="ExternalOutput").ap()
    build(nc, *args, out)
    r = _run(nc, [arrays], core_ids=[0])
    return r.results[0]["out_0"]
```

```python
from contextlib import ExitStack

import numpy as np

import concourse.bass as bass
from concourse import mybir

P = 128
F32 = mybir.dt.float32
BF16 = mybir.dt.bfloat16
ALU = mybir.AluOpType
ACT = mybir.ActivationFunctionType
AX = mybir.AxisListType
RMAX = bass.bass_isa.ReduceOp.max
BANK = 512

B, N, D = 2, 2048, 256
T = B * N
HEADS, HD = 16, 16
SCALE = float(HD) ** -0.5
PTS = 256
LN_EPS = 1e-5

CHUNK = 512
NCHUNK = T // CHUNK
JT = CHUNK // P
NMB = 2 * D // P

QC = N // CHUNK
KB = N // P
STEPS = B * QC * KB
GROUPS = B * QC
PARTS = 3
TERM_ROWS = 6 * HD
MAX_ROWS = 3 * HD
SHIFT_ROWS = 2
AUG = TERM_ROWS + SHIFT_ROWS
LEAD = KB + 5
MSTEP = 13
PRING = 16
SRING = 3
ST_USES = STEPS + GROUPS
PAIRS = STEPS // 2
VW = 32

LAYERS = 2
WINDOW = 128
NWIN = N // WINDOW
LH, LD = 8, 64
INNER = LH * LD
PAIR = P // LD
NPAIR = LH // PAIR
HID = int(D * 4 * 2 / 3)
HB = 6
HP = -(-HID // HB)
QK_SCALE = 8.0
NORM_MIN = 1e-12
MASKED = -1e30
ITEMS = LAYERS * B
DIST_MIN = 1e-6
BIAS_STRENGTH = 0.1


PV_PLAN = {9: (0, 0), 12: (0, 4), 15: (0, 8), 2: (-1, 12)}
SUMS_STEP, ADD_STEP, KEEP_STEP = 3, 6, 7


def build(nc, x, wqkT, wvT, wpT, b_proj, gamma, beta, centers, centersT, wqkv, qk_gain, qk_gain_swapped, rotary,
          wo, ln_gain, ln_bias, w1, b1, w2, b2, out):
    xT_dram = nc.dram_tensor("xT_scratch", (2, P, T), F32, kind="Internal").ap()
    q_dram = nc.dram_tensor("q_parts", (HEADS, PARTS * HD, T), BF16, kind="Internal").ap()
    k_dram = nc.dram_tensor("k_parts", (HEADS, PARTS * HD, T), BF16, kind="Internal").ap()
    res_dram = nc.dram_tensor("res_scratch", (T, D), F32, kind="Internal").ap()

    with ExitStack() as top:
        def sem(name):
            return top.enter_context(nc.semaphore(name))

        banks = top.enter_context(nc.psum_tensor("banks", [P, 8, BANK], F32))

        def keep(name, shape, dt):
            return top.enter_context(nc.sbuf_tensor(name, shape, dt))

        ident = keep("ident", [P, P], F32)
        identb = keep("identb", [P, P], BF16)
        attn_tok = keep("attn_tok", [P, T // P, D], F32)
        wqkv_sb = keep("wqkv_sb", [P, LAYERS, 2, 3 * INNER], F32)
        w1_sb = keep("w1_sb", [P, LAYERS, 2, 2 * HB * HP], F32)
        w2_sb = keep("w2_sb", [HP, LAYERS, HB, D], F32)
        wp_sb = keep("wp_sb", [P, 2, D], F32)
        b1_sb = keep("b1_sb", [HP, LAYERS, 2 * HB], F32)
        b2_sb = keep("b2_sb", [P, LAYERS, 2], F32)
        lng_sb = keep("lng_sb", [P, LAYERS, 2], F32)
        lnb_sb = keep("lnb_sb", [P, LAYERS, 2], F32)
        gains = keep("gains", [P, LAYERS, 4, LD], F32)

        early = ExitStack()

        def sb(name, shape, dt):
            return early.enter_context(nc.sbuf_tensor(name, shape, dt))

        wqk_sb = sb("wqk_sb", [P, 2, 2 * D], F32)
        wv_sb = sb("wv_sb", [P, 2, D], F32)
        gamma_sb = sb("gamma_sb", [P, D], F32)
        beta_sb = sb("beta_sb", [P, D], F32)
        bproj_sb = sb("bproj_sb", [P, D], F32)
        crow = sb("crow", [P, 2, PTS], F32)
        ccol = sb("ccol", [P, 3, 2], F32)
        dist = sb("dist", [P, 3, PTS], F32)
        dtmp = sb("dtmp", [P, 3, PTS], F32)
        bias_exp = sb("bias_exp", [P, 3, PTS], F32)
        dmax = sb("dmax", [P, 8], F32)
        v_all = sb("v_all", [P, T // P, D], F32)
        phase1 = ExitStack()
        x_in = phase1.enter_context(nc.sbuf_tensor("x_in", [P, 2, JT, D], F32))
        xn = phase1.enter_context(nc.sbuf_tensor("xn", [P, JT, D], F32))
        xn2 = phase1.enter_context(nc.sbuf_tensor("xn2", [P, JT, D], F32))
        xnT = phase1.enter_context(nc.sbuf_tensor("xnT", [P, 2, CHUNK], F32))
        stats = phase1.enter_context(nc.sbuf_tensor("stats", [P, JT, 6], F32))
        total = phase1.enter_context(nc.sbuf_tensor("total", [P, JT, 2], F32))
        between = phase1.enter_context(nc.sbuf_tensor("between", [P, JT], F32))
        mv = phase1.enter_context(nc.sbuf_tensor("mv", [P, 2, JT, 2], F32))
        rstd = phase1.enter_context(nc.sbuf_tensor("rstd", [P, 2, JT], F32))
        rest = phase1.enter_context(nc.sbuf_tensor("rest", [P, NMB, CHUNK], F32))
        parts = phase1.enter_context(nc.sbuf_tensor("parts", [P, NMB, PARTS, CHUNK], BF16))
        phase1.close()
        q_aug = sb("q_aug", [P, B, N], BF16)
        k_aug = sb("k_aug", [P, B, N], BF16)
        v_cur = sb("v_cur", [P, B, KB, VW], F32)
        probs = sb("probs", [P, PRING, CHUNK], F32)
        acc_sb = sb("acc_sb", [P, CHUNK], F32)
        pair_max = sb("pair_max", [P, QC, 2], F32)
        row_max = sb("row_max", [P, QC], F32)
        shift = sb("shift", [P, QC, SHIFT_ROWS], BF16)
        sums = sb("sums", [P, JT, HD + 1], F32)
        inv_sum = sb("inv_sum", [P, QC], F32)
        early.close()

        late = ExitStack()

        def fb(name, shape, dt=F32):
            return late.enter_context(nc.sbuf_tensor(name, shape, dt))

        tables = fb("tables", [P, 4, LD])
        tab = fb("tab", [P, LAYERS, 4, LD])
        mask = fb("mask", [P, 2 * WINDOW], BF16)
        mask_prev = fb("mask_prev", [P, WINDOW], BF16)
        one = fb("one", [P, 1])
        half_power = fb("half_power", [P, 2 * LH])
        xT = fb("xT", [P, LAYERS, B, 2, 1 + WINDOW])
        x1T = fb("x1T", [P, LAYERS, B, 2, 1 + WINDOW])
        kT = fb("kT", [P, LAYERS, B, NPAIR, 2 * WINDOW])
        vw = fb("vw", [P, LAYERS, B, 2, INNER])
        qT = fb("qT", [P, B, NPAIR, WINDOW])
        norms = fb("norms", [P, B, 2 * LH])
        masked = fb("masked", [P, B, LH, 2 * WINDOW])
        peak = fb("peak", [P, B, LH])
        npeak = fb("npeak", [P, B, LH])
        row_sums = fb("row_sums", [P, B, LH])
        pT = fb("pT", [P, B, LH, 2, WINDOW])
        flat_masked = masked[:].rearrange("p b h t -> p b (h t)")
        squares = flat_masked[:, :, 0:2 * INNER].rearrange("p b (s e) -> p b s e", s=2)
        crossed = flat_masked[:, :, 2 * INNER:4 * INNER].rearrange("p b (s e) -> p b s e", s=2)
        o_tok = flat_masked[:, :, 0:INNER]
        flat_pT = pT[:].rearrange("p b h c t -> p b (h c t)")
        turned = flat_pT[:, :, 0:2 * INNER].rearrange("p b (s e) -> p b s e", s=2)
        gated = flat_pT[0:HP, :, 0:HB * WINDOW].rearrange("p b (j t) -> p b j t", t=WINDOW)
        uT = flat_pT[0:HP, :, HB * WINDOW:2 * HB * WINDOW].rearrange("p b (j t) -> p b j t", t=WINDOW)
        oT = fb("oT", [P, B, NPAIR, WINDOW])
        fstats = fb("fstats", [P, B, 6])
        ftotal = fb("ftotal", [P, B, 2])
        fbetween = fb("fbetween", [P, B, 1])
        fmv = fb("fmv", [P, B, 2])
        hn = fb("hn", [P, B, D])
        hnT = fb("hnT", [P, B, 2, WINDOW])
        yT = fb("yT", [P, B, 2, WINDOW])
        o_win, o_winT = hn, hnT
        x_win = fb("x_win", [P, B, D])
        res_win = fb("res_win", [P, B, D])
        silu = fb("silu", [P, B, D])
        s_win = fb("s_win", [P, B, D])
        y_tok = fb("y_tok", [P, B, D])
        wo_sb = fb("wo_sb", [P, LAYERS, NPAIR, D])
        late.close()

        consts_in = sem("consts_in")
        dist_in = sem("dist_in")
        pool_const = sem("pool_const")
        dve_const = sem("dve_const")
        dist_step = sem("dist_step")
        dist_sqrt = sem("dist_sqrt")
        dist_red = sem("dist_red")
        dist_scale = sem("dist_scale")
        dist_exp = sem("dist_exp")
        bias_ready = sem("bias_ready")
        x_loaded = [sem(f"x_loaded{u}") for u in range(2)]
        ln_dve = sem("ln_dve")
        ln_var = sem("ln_var")
        ln_sqrt = sem("ln_sqrt")
        xn_ready = sem("xn_ready")
        xn2_ready = sem("xn2_ready")
        res_step = sem("res_step")
        res_ready = sem("res_ready")
        res_stored = sem("res_stored")
        xT_done = sem("xT_done")
        xnT_ready = sem("xnT_ready")
        xT_stored = sem("xT_stored")
        qk_done = sem("qk_done")
        v_done = sem("v_done")
        v_saved = sem("v_saved")
        part1 = sem("part1")
        rest_ready = sem("rest_ready")
        part2 = sem("part2")
        part3 = sem("part3")
        parts_stored = sem("parts_stored")
        aug_loaded = [sem(f"aug_loaded{b}") for b in range(B)]
        v_copied = sem("v_copied")
        st_ready = sem("st_ready")
        smax_ready = sem("smax_ready")
        smax_read = sem("smax_read")
        max_step = sem("max_step")
        shift_ready = sem("shift_ready")
        shift_saved = sem("shift_saved")
        prob_ready = sem("prob_ready")
        bias_done = sem("bias_done")
        pv_done = sem("pv_done")
        acc_saved = sem("acc_saved")
        sel_done = sem("sel_done")
        inv_done = sem("inv_done")
        sums_done = sem("sums_done")
        attn_saved = sem("attn_saved")
        phase1_end = sem("phase1_end")

        phase2_end = sem("phase2_end")
        ff_weights = sem("ff_weights")
        ff_const = sem("ff_const")
        tab_ready = sem("tab_ready")
        tables_in = sem("tables_in")
        x_window = [sem(f"x_window{b}") for b in range(B)]
        final_in = [sem(f"final_in{b}") for b in range(B)]
        qk_ready = sem("qk_ready")
        v_ready = sem("v_ready")
        squares_done = sem("squares_done")
        norm_sums = sem("norm_sums")
        inv_norms = sem("inv_norms")
        rot_step = sem("rot_step")
        turned_done = sem("turned_done")
        qkT_done = sem("qkT_done")
        qT_kept = sem("qT_kept")
        kT_kept = sem("kT_kept")
        v_kept = sem("v_kept")
        scores_done = sem("scores_done")
        peak_step = sem("peak_step")
        peaks_done = sem("peaks_done")
        exp_done = sem("exp_done")
        inv_rows = sem("inv_rows")
        pT_done = sem("pT_done")
        pT_kept0 = sem("pT_kept0")
        pT_kept1 = sem("pT_kept1")
        o_done = sem("o_done")
        o_kept = sem("o_kept")
        oT_done = sem("oT_done")
        oT_kept = sem("oT_kept")
        wo_done = sem("wo_done")
        x1_ready = sem("x1_ready")
        h_done = sem("h_done")
        norm_step = sem("norm_step")
        var_done = sem("var_done")
        rstd_done = sem("rstd_done")
        hn_ready = sem("hn_ready")
        hnT_done = sem("hnT_done")
        hnT_kept = sem("hnT_kept")
        w1_done = sem("w1_done")
        gelu_done = sem("gelu_done")
        u_ready = sem("u_ready")
        w2_done = sem("w2_done")
        x2_ready = sem("x2_ready")
        k_carried = sem("k_carried")
        v_carried = sem("v_carried")
        x_carried = sem("x_carried")
        x1_carried = sem("x1_carried")
        mask_set = sem("mask_set")
        o_copied = sem("o_copied")
        owT_done = sem("owT_done")
        owT_kept = sem("owT_kept")
        proj_done = sem("proj_done")
        y_done = sem("y_done")
        y_kept = sem("y_kept")
        tanh_done = sem("tanh_done")
        sum_ready = sem("sum_ready")
        result_step = sem("result_step")
        result_ready = sem("result_ready")
        result_stored = [sem(f"result_stored{b}") for b in range(B)]

        def at(i, k, n=1, per=1):
            return i * (ITEMS * per) + (k * per + n)

        def parts_of(k):
            return (k // B) % LAYERS, k % B

        def lanes(b):
            return 4 * b

        def place(hh):
            return (hh % 2) * (LH // 2) + hh // 2

        def head_at(p):
            return (p % (LH // 2)) * 2 + p // (LH // 2)

        block = top.enter_context(nc.Block())

        NCONST = 5
        FF_WEIGHTS = 16 * 13

        @block.sync
        def _(sp):
            sp.dma_start(wqk_sb[:], wqkT.rearrange("(k p) e -> p k e", p=P)).then_inc(consts_in, 16)
            sp.dma_start(wv_sb[:], wvT.rearrange("(k p) e -> p k e", p=P)).then_inc(consts_in, 16)
            sp.dma_start(gamma_sb[:], gamma.partition_broadcast(P)).then_inc(consts_in, 16)
            sp.dma_start(beta_sb[:], beta.partition_broadcast(P)).then_inc(consts_in, 16)
            sp.dma_start(bproj_sb[:], b_proj.partition_broadcast(P)).then_inc(consts_in, 16)
            sp.dma_start(crow[:], centersT.partition_broadcast(P)).then_inc(dist_in, 16)
            sp.dma_start(ccol[1:P, 0, :], centers[0:P - 1, :]).then_inc(dist_in, 16)
            sp.dma_start(ccol[0:1, 0, :], centers[0:1, :]).then_inc(dist_in, 16)
            sp.dma_start(ccol[:, 1, :], centers[P - 1:2 * P - 1, :]).then_inc(dist_in, 16)
            sp.dma_start(ccol[:, 2, :], centers[PTS - 1, :].partition_broadcast(P)).then_inc(dist_in, 16)
            xv = x.rearrange("b (c j p) d -> (b c) p j d", p=P, j=JT)

            def load(c, half):
                sp.dma_start(x_in[:, half], xv[c]).then_inc(x_loaded[half], 16)

            load(0, 0)
            load(1, 1)
            nc.sync.sem_inc(xT_stored, 16)
            nc.sync.sem_inc(parts_stored, 16 * PARTS * NMB)
            nc.sync.sem_inc(res_stored, 16)
            with nc.sync.Fori(0, NCHUNK // 2) as it:
                for u in range(2):
                    c = it * 2 + u
                    after_next = nc.sync.snap((c + 2) % NCHUNK)
                    token = nc.sync.snap(c * CHUNK)
                    sp.wait_ge(xn_ready, c + 1)
                    sp.dma_start(x_in[:, u], xv[bass.ds(after_next, 1)][0]).then_inc(x_loaded[u], 16)
                    sp.wait_ge(part3, c * NMB + 1)
                    sp.wait_ge(xnT_ready, c + 2)
                    sp.dma_start(xT_dram[:, :, bass.ds(token, CHUNK)].rearrange("k p t -> p k t"),
                                 xnT[:]).then_inc(xT_stored, 16)
                    for mb in range(NMB):
                        if mb > 0:
                            sp.wait_ge(part3, c * NMB + (mb + 1))
                        heads = (mb % 2) * (P // HD)
                        dst = (q_dram if mb < 2 else k_dram)[heads:heads + P // HD, :, bass.ds(token, CHUNK)]
                        for part in range(PARTS):
                            sp.dma_start(dst[:, part * HD:(part + 1) * HD, :], parts[:, mb, part]
                                         ).then_inc(parts_stored, 16)
                    sp.wait_ge(res_ready, c + 1)
                    sp.dma_start(res_dram[bass.ds(token, CHUNK), :].rearrange("(j p) d -> p j d", p=P),
                                 xn2[:]).then_inc(res_stored, 16)
            sp.wait_ge(parts_stored, 16 * PARTS * NMB * (NCHUNK + 1))
            sp.wait_ge(xT_stored, 16 * (NCHUNK + 1))
            sp.wait_ge(res_stored, 16 * (NCHUNK + 1))
            for u in range(2):
                sp.wait_ge(x_loaded[u], 16 * (NCHUNK // 2 + 1))
            nc.sync.sem_inc(phase1_end, 1)
            sp.wait_ge(phase1_end, 5)

            def load_aug(h, b):
                for dram, aug, first, single in ((q_dram, q_aug, 0, 0), (k_dram, k_aug, 1, 2)):
                    src = dram[bass.ds(h, 1), :, b * N:(b + 1) * N][0]
                    for row, part, n in ((0, first, 2), (2, single, 1), (3, 0, 3)):
                        sp.dma_start(aug[row * HD:(row + n) * HD, b, :],
                                     src[part * HD:(part + n) * HD]).then_inc(aug_loaded[b], 16)

            load_aug(0, 0)
            sp.dma_start(wqkv_sb[:], wqkv.rearrange("l (k p) e -> p l k e", p=P)).then_inc(ff_weights, 16)
            sp.dma_start(w1_sb[:], w1.rearrange("l (k p) e -> p l k e", p=P)).then_inc(ff_weights, 16)
            sp.dma_start(w2_sb[:], w2.rearrange("l (j p) e -> p l j e", p=HP)).then_inc(ff_weights, 16)
            sp.dma_start(wp_sb[:], wpT.rearrange("(k p) e -> p k e", p=P)).then_inc(ff_weights, 16)
            sp.dma_start(b1_sb[:], b1).then_inc(ff_weights, 16)
            sp.dma_start(b2_sb[:], b2).then_inc(ff_weights, 16)
            sp.dma_start(lng_sb[:], ln_gain).then_inc(ff_weights, 16)
            sp.dma_start(lnb_sb[:], ln_bias).then_inc(ff_weights, 16)
            for k, src in ((0, qk_gain), (1, qk_gain_swapped)):
                for l in range(LAYERS):
                    sp.dma_start(gains[:, l, k::2, :], src[l].partition_broadcast(P)).then_inc(ff_weights, 16)
            with nc.sync.Fori(0, HEADS) as h:
                next_head = nc.sync.snap((h + 1) % HEADS)
                sp.wait_ge(st_ready, h * ST_USES + 1)
                load_aug(h, 1)
                sp.wait_ge(st_ready, h * ST_USES + (STEPS // 2 + GROUPS // 2 + 1))
                load_aug(next_head, 0)
            sp.wait_ge(aug_loaded[0], 16 * 6 * (HEADS + 1))
            sp.wait_ge(aug_loaded[1], 16 * 6 * HEADS)
            sp.wait_ge(phase2_end, 4)
            sp.dma_start(wo_sb[:], wo.rearrange("l (k p) e -> p l k e", p=P)).then_inc(ff_weights, 16)

            for b in range(B):
                nc.sync.sem_inc(result_stored[b], 16)

            def load_window(w, b):
                sp.dma_start(xT[:, 0, b, :, 1:], xT_dram[:, :, bass.ds(w * WINDOW + b * N, WINDOW)]
                             .rearrange("k p t -> p k t")).then_inc(x_window[b], 16)

            for b in range(B):
                load_window(0, b)
            sp.dma_start(tables[:], rotary[0]).then_inc(tables_in, 16)
            with nc.sync.Fori(0, NWIN) as i:
                after = nc.sync.snap((i + 1) % NWIN)
                sp.wait_ge(tab_ready, i * LAYERS + LAYERS)
                sp.dma_start(tables[:], rotary[bass.ds(after, 1)][0]).then_inc(tables_in, 16)
                for b in range(B):
                    sp.wait_ge(result_stored[b], i * 16 + 16)
                    rows = bass.ds(i * WINDOW, WINDOW)
                    sp.dma_start(x_win[:, b], x[b, rows, :]).then_inc(final_in[b], 16)
                    sp.dma_start(res_win[:, b], res_dram[bass.ds(i * WINDOW + b * N, WINDOW), :]).then_inc(final_in[b], 16)
                for b in range(B):
                    sp.wait_ge(x_carried, at(i, b) + ITEMS)
                    load_window(after, b)
                for b in range(B):
                    sp.wait_ge(result_ready, i * B + (b + 1))
                    sp.dma_start(out[b, bass.ds(i * WINDOW, WINDOW), :], s_win[:, b]).then_inc(result_stored[b], 16)
            for b in range(B):
                sp.wait_ge(result_stored[b], 16 * (NWIN + 1))
                sp.wait_ge(final_in[b], 32 * NWIN)
                sp.wait_ge(x_window[b], 16 * (NWIN + 1))
            sp.wait_ge(tables_in, 16 * (NWIN + 1))

        @block.gpsimd
        def _(pool):
            nc.gpsimd.memset(ident[:], 0.0).then_inc(pool_const, 1)
            pool.wait_ge(pool_const, 1)
            nc.gpsimd.affine_select(out=ident[:], in_=ident[:], compare_op=ALU.not_equal, fill=1.0, base=0,
                                    pattern=[[-1, P]], channel_multiplier=1).then_inc(pool_const, 1)
            pool.wait_ge(dist_red, 1)
            nc.gpsimd.partition_all_reduce(dmax[:, 1:2], dmax[:, 0:1], P, RMAX).then_inc(dist_red, 1)
            pool.wait_ge(consts_in, 16 * NCONST)
            nc.gpsimd.tensor_tensor(beta_sb[:], beta_sb[:], bproj_sb[:], ALU.add).then_inc(res_step, 1)
            with nc.gpsimd.Fori(0, NCHUNK) as c:
                for mb in range(NMB):
                    pool.wait_ge(part2, c * NMB + (mb + 1))
                    nc.gpsimd.tensor_tensor(parts[:, mb, 2 if mb < 2 else 0], rest[:, mb], parts[:, mb, 1],
                                            ALU.subtract).then_inc(part3, 1)
                pool.wait_ge(xn2_ready, c + 1)
                pool.wait_ge(res_step, c + 1)
                nc.gpsimd.tensor_tensor(xn2[:], xn2[:], gamma_sb[:].unsqueeze(1).to_broadcast([P, JT, D]),
                                        ALU.mult).then_inc(res_step, 1)
                pool.wait_ge(res_step, c + 2)
                nc.gpsimd.tensor_tensor(xn2[:], xn2[:], beta_sb[:].unsqueeze(1).to_broadcast([P, JT, D]),
                                        ALU.add).then_inc(res_ready, 1)
            nc.gpsimd.sem_inc(phase1_end, 1)
            pool.wait_ge(phase1_end, 5)
            nc.gpsimd.memset(v_cur[:], 0.0).then_inc(v_copied, 1)
            pool.wait_ge(v_copied, 1)
            nc.gpsimd.memset(v_cur[:, :, :, HD:HD + 1], 1.0).then_inc(v_copied, 1)
            pool.wait_ge(v_copied, 2)
            pool.wait_ge(v_saved, NCHUNK + 1)
            pool.wait_ge(bias_ready, 1)
            with nc.gpsimd.Fori(0, HEADS) as h:
                pool.wait_ge(pv_done, h * STEPS + 1)
                for b in range(B):
                    nc.gpsimd.tensor_copy(v_cur[:, b, :, 0:HD],
                                          v_all[:, b * KB:(b + 1) * KB, bass.ds(h * HD, HD)]).then_inc(v_copied, 1)
                for b in range(B):
                    for kb in range(3):
                        step = b * QC * KB + kb
                        pool.wait_ge(prob_ready, h * STEPS + (step + 2))
                        rows = P if kb < 2 else 1
                        tile = probs[0:rows, step % PRING, 1:PTS + 1]
                        nc.gpsimd.tensor_tensor(tile, tile, bias_exp[0:rows, kb, :], ALU.mult).then_inc(bias_done, 1)

            pool.wait_ge(bias_done, HEADS * 6)
            nc.gpsimd.sem_inc(phase2_end, 1)
            pool.wait_ge(phase2_end, 4)
            nc.gpsimd.memset(kT[:], 0.0).then_inc(ff_const, 1)
            nc.gpsimd.memset(vw[:], 0.0).then_inc(ff_const, 1)
            nc.gpsimd.memset(xT[:, 1], 0.0).then_inc(ff_const, 1)
            nc.gpsimd.memset(xT[:, 0, :, :, 0:1], 0.0).then_inc(ff_const, 1)
            nc.gpsimd.memset(x1T[:], 0.0).then_inc(ff_const, 1)
            nc.gpsimd.memset(half_power[:], -0.5).then_inc(ff_const, 1)
            nc.gpsimd.memset(one[:], 1.0).then_inc(ff_const, 1)
            nc.gpsimd.memset(mask_prev[:], 0.0).then_inc(ff_const, 1)
            nc.gpsimd.memset(mask[:, 0:WINDOW], MASKED).then_inc(ff_const, 1)
            nc.gpsimd.memset(mask[:, WINDOW:], 0.0).then_inc(ff_const, 1)
            pool.wait_ge(ff_const, 10)
            nc.gpsimd.affine_select(out=mask_prev[:], in_=mask_prev[:], compare_op=ALU.is_ge, fill=MASKED, base=0,
                                    pattern=[[1, WINDOW]], channel_multiplier=-1).then_inc(ff_const, 1)
            nc.gpsimd.affine_select(out=mask[:, WINDOW:], in_=mask[:, WINDOW:], compare_op=ALU.is_ge, fill=MASKED,
                                    base=0, pattern=[[-1, WINDOW]], channel_multiplier=1).then_inc(ff_const, 1)
            pool.wait_ge(ff_const, 12)
            for carried in (k_carried, v_carried, x_carried, x1_carried):
                nc.gpsimd.sem_inc(carried, ITEMS)
            nc.gpsimd.sem_inc(mask_set, 1)
            pool.wait_ge(ff_weights, FF_WEIGHTS)

            def move(dst, src):
                shape = src.shape
                ones = one[:]
                while len(ones.shape) < len(shape):
                    ones = ones.unsqueeze(1)
                return nc.gpsimd.tensor_tensor(dst, src, ones.to_broadcast(shape), ALU.mult)

            def rotary_table(l):
                nc.gpsimd.tensor_tensor(tab[:, l], tables[:], gains[:, l], ALU.mult).then_inc(tab_ready, 1)

            def invert_norms(i, k):
                b = k % B
                pool.wait_ge(norm_sums, at(i, k, 2, 2))
                nc.gpsimd.tensor_tensor(norms[:, b], norms[:, b], half_power[:], ALU.pow).then_inc(inv_norms, 1)

            def carry_keys(i, k):
                l, b = parts_of(k)
                pool.wait_ge(scores_done, at(i, k))
                move(kT[:, l, b, :, 0:WINDOW], kT[:, l, b, :, WINDOW:]).then_inc(k_carried, 1)

            pool.wait_ge(tables_in, 16)
            for l in range(LAYERS):
                rotary_table(l)
            invert_norms(0, 0)
            carry_keys(0, 0)
            with nc.gpsimd.Fori(0, NWIN) as i:
                for k in range(ITEMS):
                    l, b = parts_of(k)
                    invert_norms(i, k + 1)
                    pool.wait_ge(o_done, at(i, k))
                    move(vw[:, l, b, 0], vw[:, l, b, 1]).then_inc(v_carried, 1)
                    pool.wait_ge(var_done, at(i, k))
                    nc.gpsimd.tensor_tensor(fmv[:, b, 1:2], fmv[:, b, 1:2], half_power[:, 0:1],
                                            ALU.pow).then_inc(rstd_done, 1)
                    pool.wait_ge(x1_ready, at(i, k))
                    move(xT[:, l, b, :, 0:1], xT[:, l, b, :, WINDOW:]).then_inc(x_carried, 1)
                    carry_keys(i, k + 1)
                    if k % B == 0:
                        pool.wait_ge(turned_done, at(i, k + 1))
                        pool.wait_ge(tables_in, i * 16 + 32)
                        rotary_table(l)
                    if k + 1 == ITEMS - 1:
                        move(mask[:, 0:WINDOW], mask_prev[:]).then_inc(mask_set, 1)
                    pool.wait_ge(x2_ready, at(i, k))
                    move(x1T[:, l, b, :, 0:1], x1T[:, l, b, :, WINDOW:]).then_inc(x1_carried, 1)
                    if l == LAYERS - 1:
                        steps = i * (3 * B) + 3 * b
                        pool.wait_ge(tanh_done, i * B + (b + 1))
                        nc.gpsimd.tensor_tensor(silu[:, b], silu[:, b], one[:].to_broadcast([P, D]), ALU.add
                                                ).then_inc(result_step, 1)
                        pool.wait_ge(y_kept, i * B + (b + 1 + B))
                        pool.wait_ge(result_step, steps + 1)
                        nc.gpsimd.tensor_tensor(silu[:, b], silu[:, b], y_tok[:, b], ALU.mult).then_inc(result_step, 1)
                        pool.wait_ge(sum_ready, i * B + (b + 1 + B))
                        pool.wait_ge(result_step, steps + 2)
                        nc.gpsimd.tensor_tensor(s_win[:, b], s_win[:, b], silu[:, b], ALU.mult).then_inc(result_step, 1)
                        pool.wait_ge(result_step, steps + 3)
                        nc.gpsimd.tensor_tensor(s_win[:, b], s_win[:, b], x_win[:, b], ALU.add).then_inc(result_ready, 1)

        @block.scalar
        def _(act):
            act.wait_ge(dist_step, 5)
            nc.scalar.activation(dist[:], dist[:], ACT.Sqrt).then_inc(dist_sqrt, 1)
            nc.scalar.sem_inc(xnT_ready, 1)
            nc.scalar.sem_inc(v_saved, 1)
            with nc.scalar.Fori(0, NCHUNK) as c:
                for n in range(2):
                    act.wait_ge(ln_var, c * 2 + (n + 1))
                    nc.scalar.activation(rstd[:, n], mv[:, n, :, 1], ACT.Sqrt).then_inc(ln_sqrt, 1)
                    if n == 0:
                        act.wait_ge(xT_done, c + 2)
                        act.wait_ge(xT_stored, (c + 1) * 16)
                        nc.scalar.copy(xnT[:], banks[:, 0:2, :]).then_inc(xnT_ready, 1)
                act.wait_ge(parts_stored, (c + 1) * (16 * PARTS * NMB))
                for mb in range(NMB):
                    act.wait_ge(qk_done, c * NMB + (mb + 1))
                    nc.scalar.copy(parts[:, mb, 0 if mb < 2 else 2], banks[:, 2 + mb, :]).then_inc(part1, 1)
                    act.wait_ge(rest_ready, (c + 1) * NMB + (mb + 1))
                    nc.scalar.copy(parts[:, mb, 1], rest[:, mb]).then_inc(part2, 1)
                act.wait_ge(v_done, c + 1)
                nc.scalar.copy(v_all[:, bass.ds(c * JT, JT), :],
                               banks[:, 6:8, :].rearrange("p a (j d) -> p (a j) d", d=D)).then_inc(v_saved, 1)
            nc.scalar.sem_inc(phase1_end, 1)
            act.wait_ge(phase1_end, 5)
            act.wait_ge(dist_scale, 1)
            nc.scalar.activation(bias_exp[:], dist[:], ACT.Exp, scale=dmax[:, 4:5]).then_inc(dist_exp, 1)

            def save_shift(group, use):
                b, qc = (group // QC) % B, group % QC
                nc.scalar.copy(q_aug[TERM_ROWS:AUG, b, qc * CHUNK:(qc + 1) * CHUNK],
                               banks[TERM_ROWS:AUG, use % SRING, 0:CHUNK // 2].bitcast(BF16)).then_inc(shift_saved, 1)

            def save_sums(h, group):
                act.wait_ge(pv_done, h * STEPS + ((group + 1) * KB + 1))
                act.wait_ge(sel_done, h * GROUPS + (group + 1))
                nc.scalar.copy(acc_sb[:], banks[:, 3, :]).then_inc(acc_saved, 1)

            nc.scalar.sem_inc(prob_ready, 1)
            act.wait_ge(st_ready, 1)
            save_shift(0, 0)
            with nc.scalar.Fori(0, HEADS) as h:
                use = 0
                for step in range(STEPS):
                    group, kb = step // KB, step % KB
                    act.wait_ge(st_ready, h * ST_USES + (use + 2))
                    act.wait_ge(pv_done, h * STEPS + max(1, step - PRING + 2))
                    nc.scalar.activation(probs[:, step % PRING, :], banks[:, use % SRING, :], ACT.Exp,
                                         scale=SCALE).then_inc(prob_ready, 1)
                    use += 1
                    if kb == MSTEP:
                        act.wait_ge(st_ready, h * ST_USES + (use + 2))
                        save_shift(group + 1, use)
                        use += 1
                    if kb == SUMS_STEP and group > 0:
                        save_sums(h, group - 1)
                save_sums(h, GROUPS - 1)

            act.wait_ge(acc_saved, HEADS * GROUPS)
            act.wait_ge(prob_ready, HEADS * STEPS + 1)
            act.wait_ge(shift_saved, HEADS * GROUPS + 1)
            nc.scalar.sem_inc(phase2_end, 1)
            act.wait_ge(phase2_end, 4)
            act.wait_ge(ff_const, 12)
            act.wait_ge(ff_weights, FF_WEIGHTS)
            nc.scalar.sem_inc(y_kept, B)

            def square(i, k):
                b = k % B
                for n in range(2):
                    act.wait_ge(qk_ready, at(i, k, n + 1, 2))
                    nc.scalar.activation(squares[:, b, n], banks[:, lanes(b) + n, :],
                                         ACT.Square).then_inc(squares_done, 1)

            def keep_v(i, k):
                l, b = parts_of(k)
                act.wait_ge(v_ready, at(i, k))
                act.wait_ge(v_carried, at(i, k))
                nc.scalar.copy(vw[:, l, b, 1], banks[:, lanes(b) + 2, :]).then_inc(v_kept, 1)

            def keep_qk(i, k):
                l, b = parts_of(k)
                act.wait_ge(qkT_done, at(i, k))
                nc.scalar.copy(qT[:, b], banks[:, lanes(b) + 3, :]).then_inc(qT_kept, 1)
                act.wait_ge(k_carried, at(i, k))
                nc.scalar.copy(kT[:, l, b, :, WINDOW:],
                               banks[:, lanes(b), :].rearrange("p (j t) -> p j t", t=WINDOW)).then_inc(kT_kept, 1)

            def exponentials(i, k):
                b = k % B
                act.wait_ge(peaks_done, at(i, k))
                for p in range(LH):
                    last = nc.scalar.activation(masked[:, b, p, :], banks[:, lanes(b) + p // 2, (p % 2) * 256:
                                                                          (p % 2 + 1) * 256], ACT.Exp,
                                                bias=npeak[:, b, p:p + 1], scale=QK_SCALE,
                                                accum_out=row_sums[:, b, head_at(p):head_at(p) + 1])
                    if p % (LH // 2) == LH // 2 - 1:
                        last.then_inc(exp_done, 1)

            def keep_probs(i, k):
                b = k % B
                act.wait_ge(pT_done, at(i, k, 1, 2))
                nc.scalar.copy(pT[:, b, 0:LH // 2], banks[:, lanes(b):lanes(b) + 2, :]).then_inc(pT_kept0, 1)

            def keep_o(i, k):
                b = k % B
                act.wait_ge(oT_done, at(i, k))
                nc.scalar.copy(oT[:, b], banks[:, lanes(b) + 1, :]).then_inc(oT_kept, 1)

            def keep_normed(i, k):
                l, b = parts_of(k)
                act.wait_ge(hnT_done, at(i, k))
                for f in range(2):
                    last = nc.scalar.activation(hnT[:, b, f], banks[:, lanes(b) + 3, D + f * P:D + (f + 1) * P],
                                                ACT.Identity, bias=lnb_sb[:, l, f:f + 1],
                                                scale=lng_sb[:, l, f:f + 1])
                last.then_inc(hnT_kept, 1)

            def gelu(i, k):
                l, b = parts_of(k)
                for j in range(HB):
                    if j % 4 == 0:
                        act.wait_ge(w1_done, at(i, k, j // 4 + 1, 4))
                    last = nc.scalar.activation(gated[:, b, j], banks[0:HP, lanes(b) + j // 4,
                                                                      (j % 4) * P:(j % 4 + 1) * P],
                                                ACT.Gelu, bias=b1_sb[:, l, HB + j:HB + j + 1])
                last.then_inc(gelu_done, 1)

            def keep_heads(i, b):
                act.wait_ge(owT_done, i * B + (b + 1))
                nc.scalar.copy(o_winT[:, b], banks[:, lanes(b) + 1, 0:2 * P]).then_inc(owT_kept, 1)

            def keep_branch(i, b):
                act.wait_ge(y_done, i * B + (b + 1))
                nc.scalar.activation(silu[:, b], banks[:, lanes(b) + 2, 0:D], ACT.Tanh, scale=0.5).then_inc(tanh_done, 1)
                nc.scalar.mul(y_tok[:, b], banks[:, lanes(b) + 2, 0:D], 0.5).then_inc(y_kept, 1)

            for stage in (square, keep_v, keep_qk, exponentials):
                stage(0, 0)
            with nc.scalar.Fori(0, NWIN) as i:
                for k in range(ITEMS):
                    final = k >= ITEMS - B
                    keep_probs(i, k)
                    square(i, k + 1)
                    keep_o(i, k)
                    keep_v(i, k + 1)
                    keep_qk(i, k + 1)
                    keep_normed(i, k)
                    gelu(i, k)
                    if final:
                        keep_heads(i, k % B)
                    exponentials(i, k + 1)
                    if final:
                        keep_branch(i, k % B)

        @block.vector
        def _(dve):
            dve.wait_ge(dist_in, 16 * 5)
            for kb in range(3):
                nc.vector.tensor_scalar(dist[:, kb, :], crow[:, 0, :], ccol[:, kb, 0:1], None, ALU.subtract)
                last = nc.vector.tensor_scalar(dtmp[:, kb, :], crow[:, 1, :], ccol[:, kb, 1:2], None, ALU.subtract)
            last.then_inc(dist_step, 1)
            dve.wait_ge(dist_step, 1)
            nc.vector.tensor_tensor(dist[:], dist[:], dist[:], ALU.mult).then_inc(dist_step, 1)
            nc.vector.tensor_tensor(dtmp[:], dtmp[:], dtmp[:], ALU.mult).then_inc(dist_step, 1)
            dve.wait_ge(dist_step, 3)
            nc.vector.tensor_tensor(dist[:], dist[:], dtmp[:], ALU.add).then_inc(dist_step, 2)
            dve.wait_ge(dist_sqrt, 1)
            nc.vector.tensor_reduce(dmax[:, 0:1], dist[:], AX.XY, ALU.max).then_inc(dist_red, 1)
            dve.wait_ge(dist_red, 2)
            nc.vector.tensor_scalar(dmax[:, 2:3], dmax[:, 1:2], DIST_MIN, None, ALU.max).then_inc(dist_step, 1)
            nc.vector.tensor_scalar(dmax[:, 3:4], dmax[:, 1:2], DIST_MIN, -BIAS_STRENGTH, ALU.is_gt,
                                    ALU.mult).then_inc(dist_step, 1)
            dve.wait_ge(dist_step, 7)
            nc.vector.reciprocal(dmax[:, 5:6], dmax[:, 2:3]).then_inc(dist_step, 1)
            dve.wait_ge(dist_step, 8)
            nc.vector.tensor_tensor(dmax[:, 4:5], dmax[:, 5:6], dmax[:, 3:4], ALU.mult).then_inc(dist_scale, 1)

            def layer_norm(c, n, src, dst, done):
                base = n * 5
                for j in range(JT):
                    last = nc.vector.bn_stats(stats[:, j, :], src[:, j, :])
                last.then_inc(ln_dve, 1)
                dve.wait_ge(ln_dve, c * 10 + (base + 1))
                even, odd = stats[:, :, 1:3], stats[:, :, 4:6]
                nc.vector.tensor_tensor(total[:], even, odd, ALU.add)
                nc.vector.tensor_tensor(between[:], even[:, :, 0], odd[:, :, 0], ALU.subtract).then_inc(ln_dve, 1)
                dve.wait_ge(ln_dve, c * 10 + (base + 2))
                nc.vector.tensor_tensor(between[:], between[:], between[:], ALU.mult)
                nc.vector.tensor_scalar(mv[:, n, :, 0], total[:, :, 0], 0.5, None, ALU.mult).then_inc(ln_dve, 1)
                dve.wait_ge(ln_dve, c * 10 + (base + 3))
                nc.vector.scalar_tensor_tensor(between[:], between[:], D / 4.0, total[:, :, 1], ALU.mult,
                                               ALU.add).then_inc(ln_dve, 1)
                dve.wait_ge(ln_dve, c * 10 + (base + 4))
                nc.vector.tensor_scalar(mv[:, n, :, 1], between[:], 1.0 / D, LN_EPS, ALU.mult, ALU.add
                                        ).then_inc(ln_var, 1)
                dve.wait_ge(ln_sqrt, c * 2 + (n + 1))
                nc.vector.reciprocal(rstd[:, n], rstd[:, n]).then_inc(ln_dve, 1)
                dve.wait_ge(ln_dve, c * 10 + (base + 5))
                for j in range(JT):
                    last = nc.vector.tensor_scalar(dst[:, j, :], src[:, j, :], mv[:, n, j, 0:1], rstd[:, n, j:j + 1],
                                                   ALU.subtract, ALU.mult)
                last.then_inc(done, 1)

            nc.vector.sem_inc(rest_ready, NMB)
            with nc.vector.Fori(0, NCHUNK // 2) as it:
                for u in range(2):
                    c = it * 2 + u
                    dve.wait_ge(x_loaded[u], it * 16 + 16)
                    dve.wait_ge(xT_done, c + 1)
                    layer_norm(c, 0, x_in[:, u], xn, xn_ready)
                    dve.wait_ge(res_stored, (c + 1) * 16)
                    dve.wait_ge(xn_ready, c + 1)
                    layer_norm(c, 1, xn, xn2, xn2_ready)
                    for mb in range(NMB):
                        dve.wait_ge(part1, c * NMB + (mb + 1))
                        nc.vector.tensor_tensor(rest[:, mb], banks[:, 2 + mb, :], parts[:, mb, 0 if mb < 2 else 2],
                                                ALU.subtract).then_inc(rest_ready, 1)
            nc.vector.sem_inc(phase1_end, 1)
            dve.wait_ge(phase1_end, 5)
            dve.wait_ge(dist_exp, 1)
            nc.vector.memset(bias_exp[0:1, 0, :], 1.0).then_inc(bias_ready, 1)
            nc.vector.tensor_copy(identb[:], ident[:]).then_inc(dve_const, 1)
            for b in range(B):
                last = nc.vector.memset(k_aug[TERM_ROWS:AUG, b, :], -1.0)
            last.then_inc(dve_const, 1)

            def max_pair(before, t):
                q, half = (t // 2) % QC, t % 2
                dve.wait_ge(smax_ready, before + (t + 1))
                nc.vector.tensor_reduce(pair_max[:, q, half:half + 1], banks[:, 4 + 2 * (t % 2):6 + 2 * (t % 2), :],
                                        AX.XY, ALU.max).then_inc(smax_read, 1)

            def split_max(before, group):
                dve.wait_ge(smax_read, before * (PAIRS // GROUPS) + (group + 1) * (PAIRS // GROUPS) + 2)
                if group > 0:
                    dve.wait_ge(shift_saved, before + group)
                nc.vector.tensor_tensor(row_max[:], pair_max[:, :, 0], pair_max[:, :, 1], ALU.max).then_inc(max_step, 1)
                dve.wait_ge(max_step, before * 2 + (2 * group + 1))
                nc.vector.tensor_copy(shift[:, :, 0], row_max[:]).then_inc(max_step, 1)
                dve.wait_ge(max_step, before * 2 + (2 * group + 2))
                nc.vector.tensor_tensor(shift[:, :, 1], row_max[:], shift[:, :, 0], ALU.subtract).then_inc(shift_ready, 1)

            def save_attention(h, group):
                dve.wait_ge(sel_done, h * GROUPS + (group + 2))
                columns = banks[:, 3, :].rearrange("p (j g r) -> p j r g", g=4, r=VW)[:, :, 0:HD + 1, :]
                nc.vector.tensor_reduce(sums[:], columns, AX.X, ALU.add).then_inc(sums_done, 1)
                dve.wait_ge(sums_done, h * GROUPS + (group + 2))
                nc.vector.reciprocal(inv_sum[:], sums[:, :, HD]).then_inc(inv_done, 1)
                dve.wait_ge(inv_done, h * GROUPS + (group + 1))
                nc.vector.tensor_tensor(attn_tok[:, group * JT:(group + 1) * JT, bass.ds(h * HD, HD)],
                                        sums[:, :, 0:HD], inv_sum[:].unsqueeze(2).to_broadcast([P, JT, HD]),
                                        ALU.mult).then_inc(attn_saved, 1)

            nc.vector.sem_inc(smax_read, 2)
            nc.vector.sem_inc(sums_done, 1)
            for t in range(PAIRS // GROUPS):
                max_pair(0, t)
            split_max(0, 0)
            for t in range(PAIRS // GROUPS, (LEAD + 1) // 2 - 1):
                max_pair(0, t)
            with nc.vector.Fori(0, HEADS) as h:
                for step in range(STEPS):
                    group, kb = step // KB, step % KB
                    tile = step + LEAD
                    if tile % 2 == 1:
                        max_pair(h * PAIRS, tile // 2)
                    if tile % KB == KB - 1:
                        split_max(h * GROUPS, tile // KB)
                    if kb == KEEP_STEP and group > 0:
                        save_attention(h, group - 1)
                save_attention(h, GROUPS - 1)

            dve.wait_ge(attn_saved, HEADS * GROUPS)
            nc.vector.sem_inc(phase2_end, 1)
            dve.wait_ge(phase2_end, 4)
            dve.wait_ge(ff_const, 12)
            dve.wait_ge(ff_weights, FF_WEIGHTS)
            nc.vector.sem_inc(sum_ready, B)
            H2 = LD // 2

            def turn_qk(i, k):
                l, b = parts_of(k)
                dve.wait_ge(tab_ready, i * LAYERS + (LAYERS * (k // ITEMS) + l + 1))
                for n in range(2):
                    dve.wait_ge(squares_done, at(i, k, n + 1, 2))
                    qk = banks[:, lanes(b) + n, :].rearrange("p (h d) -> p h d", d=LD)
                    cos, sin = tab[:, l, 2 * n, :], tab[:, l, 2 * n + 1, :]
                    cr = crossed[:, b, n].rearrange("p (h d) -> p h d", d=LD)
                    nc.vector.tensor_tensor(turned[:, b, n].rearrange("p (h d) -> p h d", d=LD), qk,
                                            cos.unsqueeze(1).to_broadcast([P, LH, LD]), ALU.mult)
                    for half in range(2):
                        o = slice(half * H2, (half + 1) * H2)
                        s_ = slice((1 - half) * H2, (2 - half) * H2)
                        last = nc.vector.tensor_tensor(cr[:, :, o], qk[:, :, s_],
                                                       sin[:, o].unsqueeze(1).to_broadcast([P, LH, H2]), ALU.mult)
                    if n == 0:
                        dve.wait_ge(squares_done, at(i, k, 2, 2))
                        nc.vector.tensor_reduce(norms[:, b], squares[:, b].rearrange("p s (h d) -> p (s h) d", d=LD),
                                                AX.X, ALU.add).then_inc(norm_sums, 1)
                        dve.wait_ge(norm_sums, at(i, k, 1, 2))
                        nc.vector.tensor_scalar(norms[:, b], norms[:, b], NORM_MIN * NORM_MIN, None,
                                                ALU.max).then_inc(norm_sums, 1)
                last.then_inc(rot_step, 1)

            def finish_qk(i, k):
                b = k % B
                dve.wait_ge(rot_step, at(i, k, 1, 2))
                nc.vector.tensor_tensor(turned[:, b], turned[:, b], crossed[:, b], ALU.add).then_inc(rot_step, 1)
                dve.wait_ge(rot_step, at(i, k, 2, 2))
                dve.wait_ge(inv_norms, at(i, k))
                t16 = turned[:, b].rearrange("p s (h d) -> p (s h) d", d=LD)
                nc.vector.tensor_tensor(t16, t16, norms[:, b].unsqueeze(2).to_broadcast([P, 2 * LH, LD]),
                                        ALU.mult).then_inc(turned_done, 1)

            def largest(i, k):
                b = k % B
                dve.wait_ge(scores_done, at(i, k))
                nc.vector.tensor_reduce(peak[:, b], banks[:, lanes(b):lanes(b) + 4, :]
                                        .rearrange("p a (g t) -> p (a g) t", t=2 * WINDOW), AX.X,
                                        ALU.max).then_inc(peak_step, 1)
                dve.wait_ge(peak_step, at(i, k))
                nc.vector.tensor_scalar(npeak[:, b], peak[:, b], -QK_SCALE, None, ALU.mult).then_inc(peaks_done, 1)

            def keep_probs(i, k):
                b = k % B
                dve.wait_ge(pT_done, at(i, k, 2, 2))
                nc.vector.tensor_copy(pT[:, b, LH // 2:], banks[:, lanes(b) + 2:lanes(b) + 4, :]
                                      .rearrange("p a (g c t) -> p (a g) c t", c=2, t=WINDOW)).then_inc(pT_kept1, 1)
                nc.vector.reciprocal(row_sums[:, b], row_sums[:, b]).then_inc(inv_rows, 1)

            def scale_o(i, k):
                b = k % B
                dve.wait_ge(o_done, at(i, k))
                dve.wait_ge(inv_rows, at(i, k))
                nc.vector.tensor_tensor(o_tok[:, b].rearrange("p (h d) -> p h d", d=LD),
                                        banks[:, lanes(b), :].rearrange("p (h d) -> p h d", d=LD),
                                        row_sums[:, b].unsqueeze(2).to_broadcast([P, LH, LD]),
                                        ALU.mult).then_inc(o_kept, 1)

            def add_attention(i, k):
                l, b = parts_of(k)
                dve.wait_ge(wo_done, at(i, k))
                dve.wait_ge(x1_carried, at(i, k))
                nc.vector.tensor_tensor(x1T[:, l, b, :, 1:], banks[:, lanes(b) + 2, 0:D]
                                        .rearrange("p (f t) -> p f t", t=WINDOW), xT[:, l, b, :, 1:],
                                        ALU.add).then_inc(x1_ready, 1)

            def normalise(i, k):
                b = k % B
                h_tok = banks[:, lanes(b) + 3, 0:D]
                dve.wait_ge(h_done, at(i, k))
                nc.vector.bn_stats(fstats[:, b], h_tok).then_inc(norm_step, 1)
                dve.wait_ge(norm_step, at(i, k, 1, 4))
                nc.vector.tensor_tensor(ftotal[:, b], fstats[:, b, 1:3], fstats[:, b, 4:6], ALU.add)
                nc.vector.tensor_tensor(fbetween[:, b], fstats[:, b, 1:2], fstats[:, b, 4:5], ALU.subtract
                                        ).then_inc(norm_step, 1)
                dve.wait_ge(norm_step, at(i, k, 2, 4))
                nc.vector.tensor_tensor(fbetween[:, b], fbetween[:, b], fbetween[:, b], ALU.mult)
                nc.vector.tensor_scalar(fmv[:, b, 0:1], ftotal[:, b, 0:1], 0.5, None, ALU.mult).then_inc(norm_step, 1)
                dve.wait_ge(norm_step, at(i, k, 3, 4))
                nc.vector.scalar_tensor_tensor(fbetween[:, b], fbetween[:, b], D / 4.0, ftotal[:, b, 1:2],
                                               ALU.mult, ALU.add).then_inc(norm_step, 1)
                dve.wait_ge(norm_step, at(i, k, 4, 4))
                nc.vector.tensor_scalar(fmv[:, b, 1:2], fbetween[:, b], 1.0 / D, LN_EPS, ALU.mult,
                                        ALU.add).then_inc(var_done, 1)
                dve.wait_ge(rstd_done, at(i, k))
                nc.vector.tensor_scalar(hn[:, b], h_tok, fmv[:, b, 0:1], fmv[:, b, 1:2],
                                        ALU.subtract, ALU.mult).then_inc(hn_ready, 1)

            def gate(i, k):
                l, b = parts_of(k)
                dve.wait_ge(gelu_done, at(i, k))
                for j in range(HB):
                    if j % 4 == 0:
                        dve.wait_ge(w1_done, at(i, k, j // 4 + 3, 4))
                    last = nc.vector.scalar_tensor_tensor(
                        uT[:, b, j], banks[0:HP, lanes(b) + 2 + j // 4, (j % 4) * P:(j % 4 + 1) * P],
                        b1_sb[:, l, j:j + 1], gated[:, b, j], ALU.add, ALU.mult)
                    if j % (HB // 2) == HB // 2 - 1:
                        last.then_inc(u_ready, 1)

            def add_hidden(i, k):
                l, b = parts_of(k)
                dve.wait_ge(w2_done, at(i, k))
                if l < LAYERS - 1:
                    dve.wait_ge(x_carried, at(i, k + B))
                    dst = xT[:, l + 1, b, :, 1:]
                else:
                    dst = yT[:, b]
                for f in range(2):
                    last = nc.vector.scalar_tensor_tensor(
                        dst[:, f], banks[:, lanes(b), f * P:(f + 1) * P], b2_sb[:, l, f:f + 1],
                        x1T[:, l, b, f, 1:], ALU.add, ALU.add)
                last.then_inc(x2_ready, 1)

            def take_heads(i, k):
                b = k % B
                dve.wait_ge(hnT_done, at(i, k))
                nc.vector.tensor_copy(o_win[:, b], attn_tok[:, bass.ds(i + b * NWIN, 1), :][:, 0]).then_inc(o_copied, 1)

            def add_first(i, b):
                dve.wait_ge(proj_done, i * B + (b + 1))
                dve.wait_ge(final_in[b], i * 32 + 32)
                nc.vector.tensor_tensor(s_win[:, b], banks[:, lanes(b) + 3, 0:D], res_win[:, b],
                                        ALU.add).then_inc(sum_ready, 1)

            for stage in (turn_qk, finish_qk, largest):
                stage(0, 0)
            with nc.vector.Fori(0, NWIN) as i:
                for k in range(ITEMS):
                    final = k >= ITEMS - B
                    keep_probs(i, k)
                    turn_qk(i, k + 1)
                    scale_o(i, k)
                    finish_qk(i, k + 1)
                    add_attention(i, k)
                    normalise(i, k)
                    if final:
                        take_heads(i, k)
                    largest(i, k + 1)
                    gate(i, k)
                    add_hidden(i, k)
                    if final:
                        add_first(i, k % B)

        @block.tensor
        def _(pe):
            pe.wait_ge(pool_const, 2)
            pe.wait_ge(consts_in, 16 * NCONST)
            nc.tensor.sem_inc(xT_done, 1)
            with nc.tensor.Fori(0, NCHUNK) as c:
                pe.wait_ge(xn_ready, c + 1)
                pe.wait_ge(xnT_ready, c + 1)
                for k in range(2):
                    for j in range(JT):
                        last = nc.tensor.transpose(banks[:, k, j * P:(j + 1) * P], xn[:, j, k * P:(k + 1) * P], ident[:])
                last.then_inc(xT_done, 1)
                pe.wait_ge(xnT_ready, c + 2)
                pe.wait_ge(rest_ready, (c + 1) * NMB)
                for mb in range(NMB):
                    for k in range(2):
                        last = nc.tensor.matmul(banks[:, 2 + mb, :], wqk_sb[:, k, mb * P:(mb + 1) * P], xnT[:, k, :],
                                                start=(k == 0), stop=(k == 1))
                    last.then_inc(qk_done, 1)
                pe.wait_ge(v_saved, c + 1)
                for j in range(JT):
                    for k in range(2):
                        last = nc.tensor.matmul(banks[:, 6 + j // 2, (j % 2) * D:(j % 2 + 1) * D],
                                                xnT[:, k, j * P:(j + 1) * P], wv_sb[:, k, :],
                                                start=(k == 0), stop=(k == 1))
                last.then_inc(v_done, 1)
            nc.tensor.sem_inc(phase1_end, 1)
            pe.wait_ge(phase1_end, 5)
            pe.wait_ge(dve_const, 2)

            def max_tile(before, t):
                pair, b, q, kq = t // 2, (t // (QC * KB)) % B, (t // (N // BANK)) % KB, t % (N // BANK)
                if t % 2 == 0:
                    pe.wait_ge(smax_read, before + (pair + 1))
                mm = nc.tensor.matmul(banks[:, 4 + t % 4, :], q_aug[0:MAX_ROWS, b, q * P:(q + 1) * P],
                                      k_aug[0:MAX_ROWS, b, kq * BANK:(kq + 1) * BANK], start=True, stop=True)
                if t % 2 == 1:
                    mm.then_inc(smax_ready, 1)

            def bank_free(h, use):
                if use < SRING:
                    pe.wait_ge(prob_ready, h * STEPS + 1)
                    return
                group, kb = divmod(use - SRING, KB + 1)
                if kb == MSTEP + 1:
                    pe.wait_ge(shift_saved, h * GROUPS + (group + 2))
                else:
                    pe.wait_ge(prob_ready, h * STEPS + (group * KB + kb - (kb > MSTEP) + 2))

            def shift_rows(h, group, use):
                pe.wait_ge(shift_ready, h * GROUPS + (group + 1))
                bank_free(h, use)
                for j in range(JT):
                    last = nc.tensor.transpose(
                        banks[TERM_ROWS:AUG, use % SRING, j * P // 2:(j + 1) * P // 2].bitcast(BF16),
                        shift[:, j, :], identb[:])
                last.then_inc(st_ready, 1)

            def weighted(h, group, kb):
                step = group * KB + kb
                b = group // QC
                if kb == 0:
                    pe.wait_ge(sums_done, h * GROUPS + (group + 1))
                    pe.wait_ge(v_copied, h * 2 + (3 + b))
                if group % QC == 0 and kb < 3:
                    pe.wait_ge(bias_done, h * 6 + (b * 3 + kb + 1))
                else:
                    pe.wait_ge(prob_ready, h * STEPS + (step + 2))
                g = kb % 4
                mm = nc.tensor.matmul(banks[32 * g:32 * g + VW, 3, :], v_cur[:, b, kb, :], probs[:, step % PRING, :],
                                      start=(kb < 4), stop=(kb >= KB - 4))
                mm.then_inc(pv_done, 1)

            def add_groups(h, group):
                pe.wait_ge(acc_saved, h * GROUPS + (group + 1))
                for j in range(JT):
                    last = nc.tensor.transpose(banks[:, 3, j * P:(j + 1) * P], acc_sb[:, j * P:(j + 1) * P], ident[:])
                last.then_inc(sel_done, 1)

            nc.tensor.sem_inc(pv_done, 1)
            nc.tensor.sem_inc(sel_done, 1)
            pe.wait_ge(aug_loaded[0], 16 * 6)
            for t in range(KB):
                max_tile(0, t)
            shift_rows(0, 0, 0)
            for t in range(KB, LEAD):
                max_tile(0, t)
            with nc.tensor.Fori(0, HEADS) as h:
                use = 0
                for step in range(STEPS):
                    group, kb = step // KB, step % KB
                    b, qc = group // QC, group % QC
                    if kb == 0:
                        pe.wait_ge(shift_saved, h * GROUPS + (group + 1))
                    bank_free(h, use)
                    nc.tensor.matmul(banks[:, use % SRING, :], k_aug[0:AUG, b, kb * P:(kb + 1) * P],
                                     q_aug[0:AUG, b, qc * CHUNK:(qc + 1) * CHUNK], start=True,
                                     stop=True).then_inc(st_ready, 1)
                    use += 1
                    tile = step + LEAD
                    if tile == STEPS // 2:
                        pe.wait_ge(aug_loaded[1], h * 96 + 96)
                    if tile == STEPS:
                        pe.wait_ge(aug_loaded[0], h * 96 + 192)
                    max_tile(h * PAIRS, tile)
                    ago, first = PV_PLAN.get(kb, (-GROUPS, 0))
                    if group + ago >= 0:
                        for key in range(first, first + 4):
                            weighted(h, group + ago, key)
                    if kb == ADD_STEP and group > 0:
                        add_groups(h, group - 1)
                    if kb == MSTEP:
                        shift_rows(h, group + 1, use)
                        use += 1
                for key in range(KB - 4, KB):
                    weighted(h, GROUPS - 1, key)
                add_groups(h, GROUPS - 1)

            pe.wait_ge(sel_done, HEADS * GROUPS + 1)
            nc.tensor.sem_inc(phase2_end, 1)
            pe.wait_ge(phase2_end, 4)
            pe.wait_ge(ff_const, 12)
            pe.wait_ge(ff_weights, FF_WEIGHTS)

            def project_qk(i, k):
                l, b = parts_of(k)
                if l == 0:
                    pe.wait_ge(x_window[b], i * 16 + (16 * (k // ITEMS) + 16))
                    pe.wait_ge(y_kept, i * B + (B * (k // ITEMS) + b + 1))
                    pe.wait_ge(sum_ready, i * B + (B * (k // ITEMS) + b + 1))
                else:
                    pe.wait_ge(x2_ready, at(i, k - B))
                for n in range(2):
                    for f in range(2):
                        last = nc.tensor.matmul(banks[:, lanes(b) + n, :], xT[:, l, b, f, 1 - f:1 - f + WINDOW],
                                                wqkv_sb[:, l, f, n * INNER:(n + 1) * INNER],
                                                start=(f == 0), stop=(f == 1))
                    last.then_inc(qk_ready, 1)

            def project_v(i, k, f):
                l, b = parts_of(k)
                last = nc.tensor.matmul(banks[:, lanes(b) + 2, :], xT[:, l, b, f, 1 - f:1 - f + WINDOW],
                                        wqkv_sb[:, l, f, 2 * INNER:], start=(f == 0), stop=(f == 1))
                if f == 1:
                    last.then_inc(v_ready, 1)

            def transpose_qk(i, k):
                b = k % B
                pe.wait_ge(turned_done, at(i, k))
                for j in range(NPAIR):
                    nc.tensor.transpose(banks[:, lanes(b) + 3, j * P:(j + 1) * P],
                                        turned[:, b, 0, j * P:(j + 1) * P], ident[:])
                    last = nc.tensor.transpose(banks[:, lanes(b), j * P:(j + 1) * P],
                                               turned[:, b, 1, j * P:(j + 1) * P], ident[:])
                last.then_inc(qkT_done, 1)

            def set_mask(i, k):
                b = k % B
                pe.wait_ge(mask_set, i + (k // ITEMS + 1))
                pe.wait_ge(v_kept, at(i, k))
                for a in (1, 2, 3, 0):
                    if a == 3:
                        pe.wait_ge(qT_kept, at(i, k))
                        pe.wait_ge(kT_kept, at(i, k))
                    nc.tensor.matmul(banks[:, lanes(b) + a, :].rearrange("p (g t) -> p g t", t=2 * WINDOW), identb[:],
                                     mask[:].unsqueeze(1).to_broadcast([P, 2, 2 * WINDOW]), start=True, stop=False)

            def scores(i, k, heads):
                l, b = parts_of(k)
                for hh in heads:
                    r = slice((hh % 2) * LD, (hh % 2 + 1) * LD)
                    col = (place(hh) % 2) * 2 * WINDOW
                    last = nc.tensor.matmul(banks[:, lanes(b) + place(hh) // 2, col:col + 2 * WINDOW],
                                            qT[r, b, hh // 2, :], kT[r, l, b, hh // 2, :], start=False,
                                            stop=(place(hh) % 2 == 1))
                if hh == LH - 1:
                    last.then_inc(scores_done, 1)

            def transpose_probs(i, k, half):
                b = k % B
                pe.wait_ge(exp_done, at(i, k, half + 1, 2))
                for p in range(half * LH // 2, (half + 1) * LH // 2):
                    for c in range(2):
                        col = ((p % 2) * 2 + c) * P
                        last = nc.tensor.transpose(banks[:, lanes(b) + p // 2, col:col + P],
                                                   masked[:, b, p, c * P:(c + 1) * P], ident[:])
                last.then_inc(pT_done, 1)

            def weighted_values(i, k):
                l, b = parts_of(k)
                pe.wait_ge(pT_kept0, at(i, k))
                for p in range(LH):
                    if p == LH // 2:
                        pe.wait_ge(pT_kept1, at(i, k))
                    hh = head_at(p)
                    for c in range(2):
                        last = nc.tensor.matmul(banks[:, lanes(b), hh * LD:(hh + 1) * LD], pT[:, b, p, c, :],
                                                vw[:, l, b, c, hh * LD:(hh + 1) * LD], start=(c == 0), stop=(c == 1))
                last.then_inc(o_done, 1)

            def transpose_o(i, k):
                b = k % B
                pe.wait_ge(o_kept, at(i, k))
                for j in range(NPAIR):
                    last = nc.tensor.transpose(banks[:, lanes(b) + 1, j * P:(j + 1) * P],
                                               o_tok[:, b, j * P:(j + 1) * P], ident[:])
                last.then_inc(oT_done, 1)

            def project_o(i, k, f):
                l, b = parts_of(k)
                pe.wait_ge(oT_kept, at(i, k))
                for j in range(NPAIR):
                    last = nc.tensor.matmul(banks[:, lanes(b) + 2, f * P:(f + 1) * P],
                                            wo_sb[:, l, j, f * P:(f + 1) * P], oT[:, b, j, :],
                                            start=(j == 0), stop=(j == NPAIR - 1))
                if f == 1:
                    last.then_inc(wo_done, 1)

            def transpose_h(i, k):
                l, b = parts_of(k)
                pe.wait_ge(x1_ready, at(i, k))
                for f in range(2):
                    last = nc.tensor.transpose(banks[:, lanes(b) + 3, f * P:(f + 1) * P],
                                               x1T[:, l, b, f, 1 - f:1 - f + WINDOW], ident[:])
                last.then_inc(h_done, 1)

            def transpose_normed(i, k):
                b = k % B
                pe.wait_ge(hn_ready, at(i, k))
                for f in range(2):
                    last = nc.tensor.transpose(banks[:, lanes(b) + 3, D + f * P:D + (f + 1) * P],
                                               hn[:, b, f * P:(f + 1) * P], ident[:])
                last.then_inc(hnT_done, 1)

            def hidden(i, k):
                l, b = parts_of(k)
                pe.wait_ge(hnT_kept, at(i, k))
                for bank, part in ((0, 1), (2, 0)):
                    for j in range(HB):
                        for f in range(2):
                            col = (part * HB + j) * HP
                            last = nc.tensor.matmul(
                                banks[0:HP, lanes(b) + bank + j // 4, (j % 4) * P:(j % 4 + 1) * P],
                                w1_sb[:, l, f, col:col + HP], hnT[:, b, f, :], start=(f == 0), stop=(f == 1))
                        if (j + 1) % 4 == 0 or j == HB - 1:
                            last.then_inc(w1_done, 1)

            def project_hidden(i, k):
                l, b = parts_of(k)
                for j in range(HB):
                    if j % (HB // 2) == 0:
                        pe.wait_ge(u_ready, at(i, k, j // (HB // 2) + 1, 2))
                    for f in range(2):
                        last = nc.tensor.matmul(banks[:, lanes(b), f * P:(f + 1) * P],
                                                w2_sb[:, l, j, f * P:(f + 1) * P], uT[:, b, j, :],
                                                start=(j == 0 and f == 0), stop=(j == HB - 1 and f == 1))
                last.then_inc(w2_done, 1)

            def transpose_heads(i, k):
                b = k % B
                pe.wait_ge(o_copied, i * B + (b + 1))
                pe.wait_ge(gelu_done, at(i, k))
                for f in range(2):
                    last = nc.tensor.transpose(banks[:, lanes(b) + 1, f * P:(f + 1) * P],
                                               o_win[:, b, f * P:(f + 1) * P], ident[:])
                last.then_inc(owT_done, 1)

            def project_heads(i, b):
                pe.wait_ge(owT_kept, i * B + (b + 1))
                for f in range(2):
                    last = nc.tensor.matmul(banks[:, lanes(b) + 3, 0:D], o_winT[:, b, f, :], wp_sb[:, f, :],
                                            start=(f == 0), stop=(f == 1))
                last.then_inc(proj_done, 1)

            def transpose_y(i, k):
                b = k % B
                pe.wait_ge(x2_ready, at(i, k))
                for f in range(2):
                    last = nc.tensor.transpose(banks[:, lanes(b) + 2, f * P:(f + 1) * P], yT[:, b, f, :], ident[:])
                last.then_inc(y_done, 1)

            project_qk(0, 0)
            project_v(0, 0, 0)
            project_v(0, 0, 1)
            transpose_qk(0, 0)
            set_mask(0, 0)
            scores(0, 0, range(LH))
            with nc.tensor.Fori(0, NWIN) as i:
                for k in range(ITEMS):
                    final = k >= ITEMS - B
                    transpose_probs(i, k, 0)
                    transpose_probs(i, k, 1)
                    project_qk(i, k + 1)
                    weighted_values(i, k)
                    project_v(i, k + 1, 0)
                    transpose_o(i, k)
                    project_v(i, k + 1, 1)
                    project_o(i, k, 0)
                    transpose_qk(i, k + 1)
                    project_o(i, k, 1)
                    set_mask(i, k + 1)
                    transpose_h(i, k)
                    scores(i, k + 1, range(LH - 2))
                    transpose_normed(i, k)
                    scores(i, k + 1, range(LH - 2, LH))
                    hidden(i, k)
                    if final:
                        transpose_heads(i, k)
                    project_hidden(i, k)
                    if final:
                        project_heads(i, k % B)
                        transpose_y(i, k)


_INS = {
    "x": lambda i: i["L0_attn_x"],
    "wqkT": lambda i: i["L0_attn_W_qkv"][:2 * D].T,
    "wvT": lambda i: i["L0_attn_W_qkv"][2 * D:].T,
    "wpT": lambda i: i["L0_attn_W_proj"].T,
    "b_proj": lambda i: i["L0_attn_b_proj"],
    "gamma": lambda i: i["L0_attn_ln_gamma"],
    "beta": lambda i: i["L0_attn_ln_beta"],
    "centers": lambda i: i["L0_attn_spatial_centers"],
    "centersT": lambda i: i["L0_attn_spatial_centers"].T,
    "wqkv": lambda i: i["L0_ffn_wqkv"],
    "qk_gain": lambda i: np.stack([i["L0_ffn_q_scale"], i["L0_ffn_k_scale"]], axis=1),
    "qk_gain_swapped": lambda i: swapped(np.stack([i["L0_ffn_q_scale"], i["L0_ffn_k_scale"]], axis=1)),
    "rotary": lambda i: rotary_tables(),
    "wo": lambda i: i["L0_ffn_wo"],
    "ln_gain": lambda i: by_block(i["L0_ffn_ln_g"], 2, P),
    "ln_bias": lambda i: by_block(i["L0_ffn_ln_b"], 2, P),
    "w1": lambda i: pad_hidden(i["L0_ffn_w1"], 2),
    "b1": lambda i: by_block(pad_hidden(i["L0_ffn_b1"], 1), 2 * HB, HP),
    "w2": lambda i: pad_hidden(i["L0_ffn_w2"], 1),
    "b2": lambda i: by_block(i["L0_ffn_b2"], 2, P),
}


def rotary_tables():
    half = np.arange(0, LD, 2, dtype=np.float32)
    inv_freq = (np.float32(1.0) / np.float32(10000.0) ** (half / np.float32(LD))).astype(np.float32)
    t = np.arange(N, dtype=np.float32)
    freqs = np.concatenate([t[:, None] * inv_freq] * 2, axis=-1)
    base = (half + np.float32(0.4 * LD)) / np.float32(1.4 * LD)
    power = (t - np.float32(N // 2)) / np.float32(WINDOW // 2)
    scale = np.concatenate([base[None, :] ** power[:, None]] * 2, axis=-1).astype(np.float32)
    sign = np.where(np.arange(LD) < LD // 2, np.float32(-1), np.float32(1))
    cos, sin = np.cos(freqs), np.sin(freqs) * sign
    tabs = np.stack([cos * scale, sin * scale, cos / scale, sin / scale], axis=1)
    return np.ascontiguousarray(tabs.reshape(NWIN, WINDOW, 4, LD), dtype=np.float32)


def swapped(a):
    return np.concatenate([a[..., LD // 2:], a[..., :LD // 2]], axis=-1)


def by_block(a, blocks, size):
    return a.reshape(a.shape[0], blocks, size).transpose(2, 0, 1)


def pad_hidden(a, axis):
    halves = np.split(a, a.shape[axis] // HID, axis=axis)
    width = [(0, 0)] * a.ndim
    width[axis] = (0, HB * HP - HID)
    return np.concatenate([np.pad(p, width) for p in halves], axis=axis)

def kernel(**inputs):
    import numpy as _np
    import concourse.bacc as _bacc
    from concourse import mybir as _mybir
    from concourse.bass_utils import run_bass_kernel_spmd as _run

    nc = _bacc.Bacc("TRN2", target_bir_lowering=False, num_devices=1)
    arrays, args = {}, []
    for name, lay in _INS.items():
        a = _np.ascontiguousarray(lay(inputs))
        arrays[f"in_{name}"] = a
        args.append(nc.dram_tensor(f"in_{name}", a.shape, _mybir.dt.from_np(a.dtype), kind="ExternalInput").ap())
    out = nc.dram_tensor("out_0", (B, N, D), F32, kind="ExternalOutput").ap()
    build(nc, *args, out)
    r = _run(nc, [arrays], core_ids=[0])
    return r.results[0]["out_0"]
```

```python
from contextlib import ExitStack

import numpy as np

import concourse.bass as bass
from concourse import mybir

P = 128
F32 = mybir.dt.float32
BF16 = mybir.dt.bfloat16
ALU = mybir.AluOpType
ACT = mybir.ActivationFunctionType
AX = mybir.AxisListType
RMAX = bass.bass_isa.ReduceOp.max
BANK = 512

B, N, D = 2, 2048, 256
T = B * N
HEADS, HD = 16, 16
SCALE = float(HD) ** -0.5
PTS = 256
LN_EPS = 1e-5

CHUNK = 512
NCHUNK = T // CHUNK
JT = CHUNK // P
NMB = 2 * D // P

QC = N // CHUNK
KB = N // P
STEPS = B * QC * KB
GROUPS = B * QC
PARTS = 3
TERM_ROWS = 6 * HD
MAX_ROWS = 3 * HD
SHIFT_ROWS = 2
AUG = TERM_ROWS + SHIFT_ROWS
LEAD = KB + 5
MSTEP = 13
PRING = 16
SRING = 3
ST_USES = STEPS + GROUPS
PAIRS = STEPS // 2
VW = 32

LAYERS = 2
WINDOW = 128
NWIN = N // WINDOW
LH, LD = 8, 64
INNER = LH * LD
PAIR = P // LD
NPAIR = LH // PAIR
HID = int(D * 4 * 2 / 3)
HB = 6
HP = -(-HID // HB)
QK_SCALE = 8.0
NORM_MIN = 1e-12
MASKED = -1e30
ITEMS = LAYERS * B
DIST_MIN = 1e-6
BIAS_STRENGTH = 0.1


PV_PLAN = {9: (0, 0), 12: (0, 4), 15: (0, 8), 2: (-1, 12)}
SUMS_STEP, ADD_STEP, KEEP_STEP = 3, 6, 7
FIRST_STEP = 9


def build(nc, x, wqkT, wvT, wpT, b_proj, gamma, beta, centers, centersT, wqkv, qk_gain, qk_gain_swapped, rotary,
          wo, ln_gain, ln_bias, w1, b1, w2, b2, out):
    xT_dram = nc.dram_tensor("xT_scratch", (2, P, T), F32, kind="Internal").ap()
    q_dram = nc.dram_tensor("q_parts", (HEADS, PARTS * HD, T), BF16, kind="Internal").ap()
    k_dram = nc.dram_tensor("k_parts", (HEADS, PARTS * HD, T), BF16, kind="Internal").ap()
    res_dram = nc.dram_tensor("res_scratch", (T, D), F32, kind="Internal").ap()

    with ExitStack() as top:
        def sem(name):
            return top.enter_context(nc.semaphore(name))

        banks = top.enter_context(nc.psum_tensor("banks", [P, 8, BANK], F32))

        def keep(name, shape, dt):
            return top.enter_context(nc.sbuf_tensor(name, shape, dt))

        ident = keep("ident", [P, P], F32)
        identb = keep("identb", [P, P], BF16)
        attn_tok = keep("attn_tok", [P, T // P, D], F32)
        wqkv_sb = keep("wqkv_sb", [P, LAYERS, 2, 3 * INNER], F32)
        w1_sb = keep("w1_sb", [P, LAYERS, 2, 2 * HB * HP], F32)
        w2_sb = keep("w2_sb", [HP, LAYERS, HB, D], F32)
        wp_sb = keep("wp_sb", [P, 2, D], F32)
        b1_sb = keep("b1_sb", [HP, LAYERS, 2 * HB], F32)
        b2_sb = keep("b2_sb", [P, LAYERS, 2], F32)
        lng_sb = keep("lng_sb", [P, LAYERS, 2], F32)
        lnb_sb = keep("lnb_sb", [P, LAYERS, 2], F32)
        gains = keep("gains", [P, LAYERS, 4, LD], F32)

        early = ExitStack()

        def sb(name, shape, dt):
            return early.enter_context(nc.sbuf_tensor(name, shape, dt))

        wqk_sb = sb("wqk_sb", [P, 2, 2 * D], F32)
        wv_sb = sb("wv_sb", [P, 2, D], F32)
        gamma_sb = sb("gamma_sb", [P, D], F32)
        beta_sb = sb("beta_sb", [P, D], F32)
        bproj_sb = sb("bproj_sb", [P, D], F32)
        crow = sb("crow", [P, 2, PTS], F32)
        ccol = sb("ccol", [P, 3, 2], F32)
        dist = sb("dist", [P, 3, PTS], F32)
        dtmp = sb("dtmp", [P, 3, PTS], F32)
        bias_exp = sb("bias_exp", [P, 3, PTS], F32)
        dmax = sb("dmax", [P, 8], F32)
        v_all = sb("v_all", [P, T // P, D], F32)
        phase1 = ExitStack()
        x_in = phase1.enter_context(nc.sbuf_tensor("x_in", [P, 2, JT, D], F32))
        xn = phase1.enter_context(nc.sbuf_tensor("xn", [P, 2, JT, D], F32))
        xn2 = phase1.enter_context(nc.sbuf_tensor("xn2", [P, JT, D], F32))
        xnT = phase1.enter_context(nc.sbuf_tensor("xnT", [P, 2, 2, CHUNK], F32))
        stats = phase1.enter_context(nc.sbuf_tensor("stats", [P, JT, 6], F32))
        total = phase1.enter_context(nc.sbuf_tensor("total", [P, JT, 2], F32))
        between = phase1.enter_context(nc.sbuf_tensor("between", [P, JT], F32))
        mv = phase1.enter_context(nc.sbuf_tensor("mv", [P, 2, JT, 2], F32))
        rstd = phase1.enter_context(nc.sbuf_tensor("rstd", [P, 2, JT], F32))
        rest = phase1.enter_context(nc.sbuf_tensor("rest", [P, NMB, CHUNK], F32))
        parts = phase1.enter_context(nc.sbuf_tensor("parts", [P, NMB, PARTS, CHUNK], BF16))
        phase1.close()
        q_aug = sb("q_aug", [P, B, N], BF16)
        k_aug = sb("k_aug", [P, B, N], BF16)
        v_cur = sb("v_cur", [P, B, KB, VW], F32)
        probs = sb("probs", [P, PRING, CHUNK], F32)
        acc_sb = sb("acc_sb", [P, CHUNK], F32)
        pair_max = sb("pair_max", [P, QC, 2], F32)
        row_max = sb("row_max", [P, QC], F32)
        shift = sb("shift", [P, QC, SHIFT_ROWS], BF16)
        sums = sb("sums", [P, JT, HD + 1], F32)
        inv_sum = sb("inv_sum", [P, QC], F32)
        early.close()

        late = ExitStack()

        def fb(name, shape, dt=F32):
            return late.enter_context(nc.sbuf_tensor(name, shape, dt))

        tables = fb("tables", [P, 4, LD])
        tab = fb("tab", [P, LAYERS, 4, LD])
        mask = fb("mask", [P, 2 * WINDOW], BF16)
        mask_prev = fb("mask_prev", [P, WINDOW], BF16)
        one = fb("one", [P, 1])
        half_power = fb("half_power", [P, LH])
        xT = fb("xT", [P, LAYERS, B, 2, 1 + WINDOW])
        x1T = fb("x1T", [P, LAYERS, B, 2, 1 + WINDOW])
        kT = fb("kT", [P, LAYERS, B, NPAIR, 2 * WINDOW])
        vw = fb("vw", [P, LAYERS, B, 2, INNER])
        qT = fb("qT", [P, B, NPAIR, WINDOW])
        norms = fb("norms", [P, B, 2 * LH])
        masked = fb("masked", [P, B, LH, 2 * WINDOW])
        peak = fb("peak", [P, B, LH])
        npeak = fb("npeak", [P, B, LH])
        row_sums = fb("row_sums", [P, B, LH])
        pT = fb("pT", [P, B, LH, 2, WINDOW])
        flat_masked = masked[:].rearrange("p b h t -> p b (h t)")
        squares = flat_masked[:, :, 0:2 * INNER].rearrange("p b (s e) -> p b s e", s=2)
        crossed = flat_masked[:, :, 2 * INNER:4 * INNER].rearrange("p b (s e) -> p b s e", s=2)
        flat_pT = pT[:].rearrange("p b h c t -> p b (h c t)")
        turned = flat_pT[:, :, 0:2 * INNER].rearrange("p b (s e) -> p b s e", s=2)
        gated = flat_pT[0:HP, :, 0:HB * WINDOW].rearrange("p b (j t) -> p b j t", t=WINDOW)
        uT = flat_pT[0:HP, :, HB * WINDOW:2 * HB * WINDOW].rearrange("p b (j t) -> p b j t", t=WINDOW)
        oT = fb("oT", [P, B, NPAIR, WINDOW])
        fstats = fb("fstats", [P, B, 6])
        ftotal = fb("ftotal", [P, B, 2])
        fbetween = fb("fbetween", [P, B, 1])
        fmv = fb("fmv", [P, B, 2])
        hn = fb("hn", [P, B, D])
        hnT = fb("hnT", [P, B, 2, WINDOW])
        yT = fb("yT", [P, B, 2, WINDOW])
        o_win, o_winT = hn, hnT
        x_win = fb("x_win", [P, B, D])
        res_win = fb("res_win", [P, B, D])
        silu = fb("silu", [P, B, D])
        s_win = fb("s_win", [P, B, D])
        y_tok = fb("y_tok", [P, B, D])
        wo_sb = fb("wo_sb", [P, LAYERS, NPAIR, D])
        late.close()

        consts_in = sem("consts_in")
        dist_in = sem("dist_in")
        pool_const = sem("pool_const")
        dve_const = sem("dve_const")
        dist_step = sem("dist_step")
        dist_sqrt = sem("dist_sqrt")
        dist_red = sem("dist_red")
        dist_scale = sem("dist_scale")
        dist_exp = sem("dist_exp")
        bias_ready = sem("bias_ready")
        x_loaded = [sem(f"x_loaded{u}") for u in range(2)]
        ln_dve = [sem(f"ln_dve{n}") for n in range(2)]
        ln_var = [sem(f"ln_var{n}") for n in range(2)]
        ln_sqrt = [sem(f"ln_sqrt{n}") for n in range(2)]
        xn_ready = sem("xn_ready")
        xn2_ready = sem("xn2_ready")
        res_step = sem("res_step")
        res_ready = sem("res_ready")
        res_stored = sem("res_stored")
        xT_done = sem("xT_done")
        xnT_ready = sem("xnT_ready")
        xT_stored = [sem(f"xT_stored{u}") for u in range(2)]
        qk_done = sem("qk_done")
        v_done = sem("v_done")
        v_saved = sem("v_saved")
        part1 = sem("part1")
        rest_ready = sem("rest_ready")
        part2 = sem("part2")
        part3 = sem("part3")
        parts_stored = [sem(f"parts_stored{mb}") for mb in range(NMB)]
        aug_loaded = [sem(f"aug_loaded{b}") for b in range(B)]
        v_copied = sem("v_copied")
        st_ready = sem("st_ready")
        smax_ready = sem("smax_ready")
        smax_read = sem("smax_read")
        max_step = sem("max_step")
        shift_ready = sem("shift_ready")
        shift_saved = sem("shift_saved")
        prob_ready = sem("prob_ready")
        bias_done = sem("bias_done")
        pv_done = sem("pv_done")
        acc_saved = sem("acc_saved")
        sel_done = sem("sel_done")
        inv_done = sem("inv_done")
        sums_done = sem("sums_done")
        attn_saved = sem("attn_saved")
        phase1_end = sem("phase1_end")

        phase2_end = sem("phase2_end")
        ff_weights = sem("ff_weights")
        ff_const = sem("ff_const")
        tab_ready = sem("tab_ready")
        tables_in = sem("tables_in")
        x_window = [sem(f"x_window{b}") for b in range(B)]
        final_in = [sem(f"final_in{b}") for b in range(B)]
        qk_ready = sem("qk_ready")
        v_ready = sem("v_ready")
        squares_done = sem("squares_done")
        norm_sums = sem("norm_sums")
        inv_norms = sem("inv_norms")
        rot_step = sem("rot_step")
        turned_done = sem("turned_done")
        qkT_done = sem("qkT_done")
        qT_kept = sem("qT_kept")
        kT_kept = sem("kT_kept")
        v_kept = sem("v_kept")
        scores_done = sem("scores_done")
        peak_step = sem("peak_step")
        peaks_done = sem("peaks_done")
        exp_done = sem("exp_done")
        inv_rows = sem("inv_rows")
        pT_done = sem("pT_done")
        pT_kept = sem("pT_kept")
        o_done = sem("o_done")
        o_kept = sem("o_kept")
        widened = sem("widened")
        spread_done = sem("spread_done")
        spread_kept = sem("spread_kept")
        wo_done = sem("wo_done")
        x1_ready = sem("x1_ready")
        h_done = sem("h_done")
        norm_step = sem("norm_step")
        var_done = sem("var_done")
        rstd_done = sem("rstd_done")
        hn_ready = sem("hn_ready")
        hnT_done = sem("hnT_done")
        hnT_kept = sem("hnT_kept")
        w1_done = sem("w1_done")
        gelu_done = sem("gelu_done")
        u_ready = sem("u_ready")
        w2_done = sem("w2_done")
        x2_ready = sem("x2_ready")
        k_carried = sem("k_carried")
        v_carried = sem("v_carried")
        x_carried = sem("x_carried")
        x1_carried = sem("x1_carried")
        mask_set = sem("mask_set")
        o_copied = sem("o_copied")
        owT_done = sem("owT_done")
        owT_kept = sem("owT_kept")
        proj_done = sem("proj_done")
        y_done = sem("y_done")
        y_kept = sem("y_kept")
        tanh_done = sem("tanh_done")
        sum_ready = sem("sum_ready")
        result_step = sem("result_step")
        result_ready = sem("result_ready")
        result_stored = [sem(f"result_stored{b}") for b in range(B)]

        def at(i, k, n=1, per=1):
            return i * (ITEMS * per) + (k * per + n)

        def parts_of(k):
            return (k // B) % LAYERS, k % B

        def lanes(b):
            return 4 * b

        def place(hh):
            return (hh % 2) * (LH // 2) + hh // 2

        def head_at(p):
            return (p % (LH // 2)) * 2 + p // (LH // 2)

        def use_of(step):
            return step + (step + KB - MSTEP - 1) // KB

        def turns(engine):
            yield 0, range(FIRST_STEP)
            with engine.Fori(0, HEADS) as h:
                yield h, range(FIRST_STEP, FIRST_STEP + STEPS)

        block = top.enter_context(nc.Block())

        NCONST = 5
        FF_WEIGHTS = 16 * 13

        @block.sync
        def _(sp):
            sp.dma_start(wqk_sb[:], wqkT.rearrange("(k p) e -> p k e", p=P)).then_inc(consts_in, 16)
            sp.dma_start(wv_sb[:], wvT.rearrange("(k p) e -> p k e", p=P)).then_inc(consts_in, 16)
            sp.dma_start(gamma_sb[:], gamma.partition_broadcast(P)).then_inc(consts_in, 16)
            sp.dma_start(beta_sb[:], beta.partition_broadcast(P)).then_inc(consts_in, 16)
            sp.dma_start(bproj_sb[:], b_proj.partition_broadcast(P)).then_inc(consts_in, 16)
            sp.dma_start(crow[:], centersT.partition_broadcast(P)).then_inc(dist_in, 16)
            sp.dma_start(ccol[1:P, 0, :], centers[0:P - 1, :]).then_inc(dist_in, 16)
            sp.dma_start(ccol[0:1, 0, :], centers[0:1, :]).then_inc(dist_in, 16)
            sp.dma_start(ccol[:, 1, :], centers[P - 1:2 * P - 1, :]).then_inc(dist_in, 16)
            sp.dma_start(ccol[:, 2, :], centers[PTS - 1, :].partition_broadcast(P)).then_inc(dist_in, 16)
            xv = x.rearrange("b (c j p) d -> (b c) p j d", p=P, j=JT)

            def load(c, half):
                sp.dma_start(x_in[:, half], xv[c]).then_inc(x_loaded[half], 16)

            load(0, 0)
            load(1, 1)
            for u in range(2):
                nc.sync.sem_inc(xT_stored[u], 16)
            for mb in range(NMB):
                nc.sync.sem_inc(parts_stored[mb], 16 * PARTS)
            nc.sync.sem_inc(res_stored, 16)
            with nc.sync.Fori(0, NCHUNK // 2) as it:
                for u in range(2):
                    c = it * 2 + u
                    after_next = nc.sync.snap((c + 2) % NCHUNK)
                    token = nc.sync.snap(c * CHUNK)
                    sp.wait_ge(xn_ready, c + 1)
                    sp.dma_start(x_in[:, u], xv[bass.ds(after_next, 1)][0]).then_inc(x_loaded[u], 16)
                    sp.wait_ge(part3, c * NMB + 1)
                    sp.wait_ge(xnT_ready, c + 2)
                    sp.dma_start(xT_dram[:, :, bass.ds(token, CHUNK)].rearrange("k p t -> p k t"),
                                 xnT[:, u]).then_inc(xT_stored[u], 16)
                    for mb in range(NMB):
                        if mb > 0:
                            sp.wait_ge(part3, c * NMB + (mb + 1))
                        heads = (mb % 2) * (P // HD)
                        dst = (q_dram if mb < 2 else k_dram)[heads:heads + P // HD, :, bass.ds(token, CHUNK)]
                        for part in range(PARTS):
                            sp.dma_start(dst[:, part * HD:(part + 1) * HD, :], parts[:, mb, part]
                                         ).then_inc(parts_stored[mb], 16)
                    sp.wait_ge(res_ready, c + 1)
                    sp.dma_start(res_dram[bass.ds(token, CHUNK), :].rearrange("(j p) d -> p j d", p=P),
                                 xn2[:]).then_inc(res_stored, 16)
            for mb in range(NMB):
                sp.wait_ge(parts_stored[mb], 16 * PARTS * (NCHUNK + 1))
            for u in range(2):
                sp.wait_ge(xT_stored[u], 16 * (NCHUNK // 2 + 1))
            sp.wait_ge(res_stored, 16 * (NCHUNK + 1))
            for u in range(2):
                sp.wait_ge(x_loaded[u], 16 * (NCHUNK // 2 + 1))
            nc.sync.sem_inc(phase1_end, 1)
            sp.wait_ge(phase1_end, 5)

            def load_aug(h, b):
                for dram, aug, first, single in ((q_dram, q_aug, 0, 0), (k_dram, k_aug, 1, 2)):
                    src = dram[bass.ds(h, 1), :, b * N:(b + 1) * N][0]
                    for row, part, n in ((0, first, 2), (2, single, 1), (3, 0, 3)):
                        sp.dma_start(aug[row * HD:(row + n) * HD, b, :],
                                     src[part * HD:(part + n) * HD]).then_inc(aug_loaded[b], 16)

            load_aug(0, 0)
            sp.dma_start(wqkv_sb[:], wqkv.rearrange("l (k p) e -> p l k e", p=P)).then_inc(ff_weights, 16)
            sp.dma_start(w1_sb[:], w1.rearrange("l (k p) e -> p l k e", p=P)).then_inc(ff_weights, 16)
            sp.dma_start(w2_sb[:], w2.rearrange("l (j p) e -> p l j e", p=HP)).then_inc(ff_weights, 16)
            sp.dma_start(wp_sb[:], wpT.rearrange("(k p) e -> p k e", p=P)).then_inc(ff_weights, 16)
            sp.dma_start(b1_sb[:], b1).then_inc(ff_weights, 16)
            sp.dma_start(b2_sb[:], b2).then_inc(ff_weights, 16)
            sp.dma_start(lng_sb[:], ln_gain).then_inc(ff_weights, 16)
            sp.dma_start(lnb_sb[:], ln_bias).then_inc(ff_weights, 16)
            for k, src in ((0, qk_gain), (1, qk_gain_swapped)):
                for l in range(LAYERS):
                    sp.dma_start(gains[:, l, k::2, :], src[l].partition_broadcast(P)).then_inc(ff_weights, 16)
            with nc.sync.Fori(0, HEADS) as h:
                next_head = nc.sync.snap((h + 1) % HEADS)
                sp.wait_ge(st_ready, h * ST_USES + 1)
                load_aug(h, 1)
                sp.wait_ge(st_ready, h * ST_USES + (STEPS // 2 + GROUPS // 2 + 1))
                load_aug(next_head, 0)
            sp.wait_ge(aug_loaded[0], 16 * 6 * (HEADS + 1))
            sp.wait_ge(aug_loaded[1], 16 * 6 * HEADS)
            sp.wait_ge(phase2_end, 4)
            sp.dma_start(wo_sb[:], wo.rearrange("l (k p) e -> p l k e", p=P)).then_inc(ff_weights, 16)

            for b in range(B):
                nc.sync.sem_inc(result_stored[b], 16)

            def load_window(w, b):
                sp.dma_start(xT[:, 0, b, :, 1:], xT_dram[:, :, bass.ds(w * WINDOW + b * N, WINDOW)]
                             .rearrange("k p t -> p k t")).then_inc(x_window[b], 16)

            for b in range(B):
                load_window(0, b)
            sp.dma_start(tables[:], rotary[0]).then_inc(tables_in, 16)
            with nc.sync.Fori(0, NWIN) as i:
                after = nc.sync.snap((i + 1) % NWIN)
                sp.wait_ge(tab_ready, i * LAYERS + LAYERS)
                sp.dma_start(tables[:], rotary[bass.ds(after, 1)][0]).then_inc(tables_in, 16)
                for b in range(B):
                    sp.wait_ge(result_stored[b], i * 16 + 16)
                    rows = bass.ds(i * WINDOW, WINDOW)
                    sp.dma_start(x_win[:, b], x[b, rows, :]).then_inc(final_in[b], 16)
                    sp.dma_start(res_win[:, b], res_dram[bass.ds(i * WINDOW + b * N, WINDOW), :]).then_inc(final_in[b], 16)
                for b in range(B):
                    sp.wait_ge(x_carried, at(i, b) + ITEMS)
                    load_window(after, b)
                for b in range(B):
                    sp.wait_ge(result_ready, i * B + (b + 1))
                    sp.dma_start(out[b, bass.ds(i * WINDOW, WINDOW), :], s_win[:, b]).then_inc(result_stored[b], 16)
            for b in range(B):
                sp.wait_ge(result_stored[b], 16 * (NWIN + 1))
                sp.wait_ge(final_in[b], 32 * NWIN)
                sp.wait_ge(x_window[b], 16 * (NWIN + 1))
            sp.wait_ge(tables_in, 16 * (NWIN + 1))

        @block.gpsimd
        def _(pool):
            nc.gpsimd.memset(ident[:], 0.0).then_inc(pool_const, 1)
            pool.wait_ge(pool_const, 1)
            nc.gpsimd.affine_select(out=ident[:], in_=ident[:], compare_op=ALU.not_equal, fill=1.0, base=0,
                                    pattern=[[-1, P]], channel_multiplier=1).then_inc(pool_const, 1)
            pool.wait_ge(dist_red, 1)
            nc.gpsimd.partition_all_reduce(dmax[:, 1:2], dmax[:, 0:1], P, RMAX).then_inc(dist_red, 1)
            pool.wait_ge(consts_in, 16 * NCONST)
            nc.gpsimd.tensor_tensor(beta_sb[:], beta_sb[:], bproj_sb[:], ALU.add).then_inc(res_step, 1)
            with nc.gpsimd.Fori(0, NCHUNK) as c:
                for mb in range(NMB):
                    pool.wait_ge(part2, c * NMB + (mb + 1))
                    nc.gpsimd.tensor_tensor(parts[:, mb, 2 if mb < 2 else 0], rest[:, mb], parts[:, mb, 1],
                                            ALU.subtract).then_inc(part3, 1)
                pool.wait_ge(xn2_ready, c + 1)
                pool.wait_ge(res_step, c + 1)
                nc.gpsimd.tensor_tensor(xn2[:], xn2[:], gamma_sb[:].unsqueeze(1).to_broadcast([P, JT, D]),
                                        ALU.mult).then_inc(res_step, 1)
                pool.wait_ge(res_step, c + 2)
                nc.gpsimd.tensor_tensor(xn2[:], xn2[:], beta_sb[:].unsqueeze(1).to_broadcast([P, JT, D]),
                                        ALU.add).then_inc(res_ready, 1)
            nc.gpsimd.sem_inc(phase1_end, 1)
            pool.wait_ge(phase1_end, 5)
            nc.gpsimd.memset(v_cur[:], 0.0).then_inc(v_copied, 1)
            pool.wait_ge(v_copied, 1)
            nc.gpsimd.memset(v_cur[:, :, :, HD:HD + 1], 1.0).then_inc(v_copied, 1)
            pool.wait_ge(v_copied, 2)
            pool.wait_ge(v_saved, NCHUNK + 1)
            pool.wait_ge(bias_ready, 1)
            with nc.gpsimd.Fori(0, HEADS) as h:
                pool.wait_ge(pv_done, h * STEPS + 1)
                for b in range(B):
                    nc.gpsimd.tensor_copy(v_cur[:, b, :, 0:HD],
                                          v_all[:, b * KB:(b + 1) * KB, bass.ds(h * HD, HD)]).then_inc(v_copied, 1)
                    for kb in range(3):
                        step = b * QC * KB + kb
                        pool.wait_ge(prob_ready, h * STEPS + (step + 2))
                        rows = P if kb < 2 else 1
                        tile = probs[0:rows, step % PRING, 1:PTS + 1]
                        nc.gpsimd.tensor_tensor(tile, tile, bias_exp[0:rows, kb, :], ALU.mult).then_inc(bias_done, 1)

            pool.wait_ge(bias_done, HEADS * 6)
            nc.gpsimd.sem_inc(phase2_end, 1)
            pool.wait_ge(phase2_end, 4)
            nc.gpsimd.memset(kT[:], 0.0).then_inc(ff_const, 1)
            nc.gpsimd.memset(vw[:], 0.0).then_inc(ff_const, 1)
            nc.gpsimd.memset(xT[:, 1], 0.0).then_inc(ff_const, 1)
            nc.gpsimd.memset(xT[:, 0, :, :, 0:1], 0.0).then_inc(ff_const, 1)
            nc.gpsimd.memset(x1T[:], 0.0).then_inc(ff_const, 1)
            nc.gpsimd.memset(half_power[:], -0.5).then_inc(ff_const, 1)
            nc.gpsimd.memset(one[:], 1.0).then_inc(ff_const, 1)
            nc.gpsimd.memset(mask_prev[:], 0.0).then_inc(ff_const, 1)
            nc.gpsimd.memset(mask[:, 0:WINDOW], MASKED).then_inc(ff_const, 1)
            nc.gpsimd.memset(mask[:, WINDOW:], 0.0).then_inc(ff_const, 1)
            pool.wait_ge(ff_const, 10)
            nc.gpsimd.affine_select(out=mask_prev[:], in_=mask_prev[:], compare_op=ALU.is_ge, fill=MASKED, base=0,
                                    pattern=[[1, WINDOW]], channel_multiplier=-1).then_inc(ff_const, 1)
            nc.gpsimd.affine_select(out=mask[:, WINDOW:], in_=mask[:, WINDOW:], compare_op=ALU.is_ge, fill=MASKED,
                                    base=0, pattern=[[-1, WINDOW]], channel_multiplier=1).then_inc(ff_const, 1)
            pool.wait_ge(ff_const, 12)
            for carried in (k_carried, v_carried, x_carried, x1_carried):
                nc.gpsimd.sem_inc(carried, ITEMS)
            nc.gpsimd.sem_inc(mask_set, 1)
            pool.wait_ge(ff_weights, FF_WEIGHTS)

            def move(dst, src):
                shape = src.shape
                ones = one[:]
                while len(ones.shape) < len(shape):
                    ones = ones.unsqueeze(1)
                return nc.gpsimd.tensor_tensor(dst, src, ones.to_broadcast(shape), ALU.mult)

            def rotary_table(l):
                nc.gpsimd.tensor_tensor(tab[:, l], tables[:], gains[:, l], ALU.mult).then_inc(tab_ready, 1)

            def invert_norms(i, k):
                b = k % B
                for n in range(2):
                    norm = norms[:, b, n * LH:(n + 1) * LH]
                    pool.wait_ge(norm_sums, at(i, k, 2 * n + 2, 4))
                    nc.gpsimd.tensor_tensor(norm, norm, half_power[:], ALU.pow).then_inc(inv_norms, 1)

            def carry_keys(i, k):
                l, b = parts_of(k)
                pool.wait_ge(scores_done, at(i, k))
                move(kT[:, l, b, :, 0:WINDOW], kT[:, l, b, :, WINDOW:]).then_inc(k_carried, 1)

            pool.wait_ge(tables_in, 16)
            for l in range(LAYERS):
                rotary_table(l)
            invert_norms(0, 0)
            carry_keys(0, 0)
            with nc.gpsimd.Fori(0, NWIN) as i:
                for k in range(ITEMS):
                    l, b = parts_of(k)
                    pool.wait_ge(inv_rows, at(i, k))
                    nc.gpsimd.tensor_tensor(oT[:, b].rearrange("p j (r d) -> p (j r) d", d=LD),
                                            row_sums[:, b].unsqueeze(2).to_broadcast([P, LH, LD]),
                                            one[:].unsqueeze(1).to_broadcast([P, LH, LD]), ALU.mult).then_inc(widened, 1)
                    invert_norms(i, k + 1)
                    pool.wait_ge(o_done, at(i, k))
                    move(vw[:, l, b, 0], vw[:, l, b, 1]).then_inc(v_carried, 1)
                    pool.wait_ge(var_done, at(i, k))
                    nc.gpsimd.tensor_tensor(fmv[:, b, 1:2], fmv[:, b, 1:2], half_power[:, 0:1],
                                            ALU.pow).then_inc(rstd_done, 1)
                    pool.wait_ge(x1_ready, at(i, k))
                    move(xT[:, l, b, :, 0:1], xT[:, l, b, :, WINDOW:]).then_inc(x_carried, 1)
                    carry_keys(i, k + 1)
                    if k % B == 0:
                        pool.wait_ge(turned_done, at(i, k + 1))
                        pool.wait_ge(tables_in, i * 16 + 32)
                        rotary_table(l)
                    if k + 1 == ITEMS - 1:
                        move(mask[:, 0:WINDOW], mask_prev[:]).then_inc(mask_set, 1)
                    pool.wait_ge(x2_ready, at(i, k))
                    move(x1T[:, l, b, :, 0:1], x1T[:, l, b, :, WINDOW:]).then_inc(x1_carried, 1)
                    if l == LAYERS - 1:
                        steps = i * (3 * B) + 3 * b
                        pool.wait_ge(tanh_done, i * B + (b + 1))
                        nc.gpsimd.tensor_tensor(silu[:, b], silu[:, b], one[:].to_broadcast([P, D]), ALU.add
                                                ).then_inc(result_step, 1)
                        pool.wait_ge(y_kept, i * B + (b + 1 + B))
                        pool.wait_ge(result_step, steps + 1)
                        nc.gpsimd.tensor_tensor(silu[:, b], silu[:, b], y_tok[:, b], ALU.mult).then_inc(result_step, 1)
                        pool.wait_ge(sum_ready, i * B + (b + 1 + B))
                        pool.wait_ge(result_step, steps + 2)
                        nc.gpsimd.tensor_tensor(s_win[:, b], s_win[:, b], silu[:, b], ALU.mult).then_inc(result_step, 1)
                        pool.wait_ge(result_step, steps + 3)
                        nc.gpsimd.tensor_tensor(s_win[:, b], s_win[:, b], x_win[:, b], ALU.add).then_inc(result_ready, 1)

        @block.scalar
        def _(act):
            act.wait_ge(dist_step, 5)
            nc.scalar.activation(dist[:], dist[:], ACT.Sqrt).then_inc(dist_sqrt, 1)
            nc.scalar.sem_inc(xnT_ready, 1)
            nc.scalar.sem_inc(v_saved, 1)

            def root(c, n):
                act.wait_ge(ln_var[n], c + 1)
                nc.scalar.activation(rstd[:, n], mv[:, n, :, 1], ACT.Sqrt).then_inc(ln_sqrt[n], 1)

            def keep_xT(c, u):
                act.wait_ge(xT_done, c + 2)
                nc.scalar.copy(xnT[:, u], banks[:, 0:2, :]).then_inc(xnT_ready, 1)

            root(0, 0)
            keep_xT(0, 0)
            with nc.scalar.Fori(0, NCHUNK // 2) as it:
                for u in range(2):
                    c = it * 2 + u
                    for mb in range(NMB):
                        if mb == 0:
                            root(c + 1, 0)
                        act.wait_ge(parts_stored[mb], c * (16 * PARTS) + 16 * PARTS)
                        act.wait_ge(qk_done, c * NMB + (mb + 1))
                        nc.scalar.copy(parts[:, mb, 0 if mb < 2 else 2], banks[:, 2 + mb, :]).then_inc(part1, 1)
                        act.wait_ge(rest_ready, (c + 1) * NMB + (mb + 1))
                        nc.scalar.copy(parts[:, mb, 1], rest[:, mb]).then_inc(part2, 1)
                    root(c, 1)
                    act.wait_ge(xT_stored[1 - u], it * 16 + (16 + 16 * u))
                    act.wait_ge(v_done, c + 1)
                    keep_xT(c + 1, 1 - u)
                    act.wait_ge(v_done, c + 2)
                    nc.scalar.copy(v_all[:, bass.ds(it * (2 * JT) + u * JT, JT), :],
                                   banks[:, 6:8, :].rearrange("p a (j d) -> p (a j) d", d=D)).then_inc(v_saved, 1)
            act.wait_ge(v_saved, NCHUNK + 1)
            nc.scalar.sem_inc(phase1_end, 1)
            act.wait_ge(phase1_end, 5)
            act.wait_ge(dist_scale, 1)
            nc.scalar.activation(bias_exp[:], dist[:], ACT.Exp, scale=dmax[:, 4:5]).then_inc(dist_exp, 1)

            def save_shift(group, use):
                b, qc = (group // QC) % B, group % QC
                nc.scalar.copy(q_aug[TERM_ROWS:AUG, b, qc * CHUNK:(qc + 1) * CHUNK],
                               banks[TERM_ROWS:AUG, use % SRING, 0:CHUNK // 2].bitcast(BF16)).then_inc(shift_saved, 1)

            def save_sums(h, group):
                act.wait_ge(pv_done, h * STEPS + ((group + 1) * KB + 1))
                act.wait_ge(sel_done, h * GROUPS + (group + 1))
                nc.scalar.copy(acc_sb[:], banks[:, 3, :]).then_inc(acc_saved, 1)

            nc.scalar.sem_inc(prob_ready, 1)
            act.wait_ge(st_ready, 1)
            save_shift(0, 0)
            for h, steps in turns(nc.scalar):
                first_use = use_of(steps[0])
                for step in steps:
                    group, kb, use = step // KB, step % KB, use_of(step)
                    act.wait_ge(st_ready, h * ST_USES + (use + 2))
                    act.wait_ge(pv_done, h * STEPS + max(1, step - PRING + 2))
                    nc.scalar.activation(probs[:, step % PRING, :], banks[:, (use - first_use) % SRING, :], ACT.Exp,
                                         scale=SCALE).then_inc(prob_ready, 1)
                    if kb == MSTEP:
                        act.wait_ge(st_ready, h * ST_USES + (use + 3))
                        save_shift(group + 1, use + 1 - first_use)
                    if kb == SUMS_STEP and group > 0:
                        save_sums(h, group - 1)

            act.wait_ge(acc_saved, HEADS * GROUPS)
            act.wait_ge(prob_ready, HEADS * STEPS + (FIRST_STEP + 1))
            act.wait_ge(shift_saved, HEADS * GROUPS + 1)
            nc.scalar.sem_inc(phase2_end, 1)
            act.wait_ge(phase2_end, 4)
            act.wait_ge(ff_const, 12)
            act.wait_ge(ff_weights, FF_WEIGHTS)
            nc.scalar.sem_inc(y_kept, B)

            def square(i, k):
                b = k % B
                for n in range(2):
                    act.wait_ge(qk_ready, at(i, k, n + 1, 2))
                    nc.scalar.activation(squares[:, b, n], banks[:, lanes(b) + n, :],
                                         ACT.Square).then_inc(squares_done, 1)

            def keep_v(i, k):
                l, b = parts_of(k)
                act.wait_ge(v_ready, at(i, k))
                act.wait_ge(v_carried, at(i, k))
                nc.scalar.copy(vw[:, l, b, 1], banks[:, lanes(b) + 2, :]).then_inc(v_kept, 1)

            def keep_qk(i, k):
                l, b = parts_of(k)
                act.wait_ge(qkT_done, at(i, k))
                nc.scalar.copy(qT[:, b], banks[:, lanes(b) + 3, :]).then_inc(qT_kept, 1)
                act.wait_ge(k_carried, at(i, k))
                nc.scalar.copy(kT[:, l, b, :, WINDOW:],
                               banks[:, lanes(b), :].rearrange("p (j t) -> p j t", t=WINDOW)).then_inc(kT_kept, 1)

            def exponentials(i, k):
                b = k % B
                act.wait_ge(peaks_done, at(i, k))
                for p in range(LH):
                    last = nc.scalar.activation(masked[:, b, p, :], banks[:, lanes(b) + p // 2, (p % 2) * 256:
                                                                          (p % 2 + 1) * 256], ACT.Exp,
                                                bias=npeak[:, b, p:p + 1], scale=QK_SCALE,
                                                accum_out=row_sums[:, b, head_at(p):head_at(p) + 1])
                    if p % (LH // 2) == LH // 2 - 1:
                        last.then_inc(exp_done, 1)

            def keep_probs(i, k, half):
                b = k % B
                act.wait_ge(pT_done, at(i, k, half + 1, 2))
                nc.scalar.copy(pT[:, b, half * LH // 2:(half + 1) * LH // 2],
                               banks[:, lanes(b) + 2 * half:lanes(b) + 2 * half + 2, :]).then_inc(pT_kept, 1)

            def keep_spread(i, k):
                b = k % B
                act.wait_ge(spread_done, at(i, k))
                nc.scalar.copy(oT[:, b], banks[:, lanes(b) + 1, :]).then_inc(spread_kept, 1)

            def keep_normed(i, k):
                l, b = parts_of(k)
                act.wait_ge(hnT_done, at(i, k))
                for f in range(2):
                    last = nc.scalar.activation(hnT[:, b, f], banks[:, lanes(b) + 3, D + f * P:D + (f + 1) * P],
                                                ACT.Identity, bias=lnb_sb[:, l, f:f + 1],
                                                scale=lng_sb[:, l, f:f + 1])
                last.then_inc(hnT_kept, 1)

            def gelu(i, k):
                l, b = parts_of(k)
                for j in range(HB):
                    if j % 4 == 0:
                        act.wait_ge(w1_done, at(i, k, j // 4 + 1, 4))
                    last = nc.scalar.activation(gated[:, b, j], banks[0:HP, lanes(b) + j // 4,
                                                                      (j % 4) * P:(j % 4 + 1) * P],
                                                ACT.Gelu, bias=b1_sb[:, l, HB + j:HB + j + 1])
                last.then_inc(gelu_done, 1)

            def keep_heads(i, b):
                act.wait_ge(owT_done, i * B + (b + 1))
                nc.scalar.copy(o_winT[:, b], banks[:, lanes(b) + 1, 0:2 * P]).then_inc(owT_kept, 1)

            def keep_branch(i, b):
                act.wait_ge(y_done, i * B + (b + 1))
                nc.scalar.activation(silu[:, b], banks[:, lanes(b) + 2, 0:D], ACT.Tanh, scale=0.5).then_inc(tanh_done, 1)
                nc.scalar.mul(y_tok[:, b], banks[:, lanes(b) + 2, 0:D], 0.5).then_inc(y_kept, 1)

            for stage in (square, keep_v, keep_qk, exponentials):
                stage(0, 0)
            with nc.scalar.Fori(0, NWIN) as i:
                for k in range(ITEMS):
                    final = k >= ITEMS - B
                    keep_probs(i, k, 0)
                    square(i, k + 1)
                    keep_probs(i, k, 1)
                    keep_spread(i, k)
                    keep_v(i, k + 1)
                    keep_qk(i, k + 1)
                    keep_normed(i, k)
                    gelu(i, k)
                    if final:
                        keep_heads(i, k % B)
                    exponentials(i, k + 1)
                    if final:
                        keep_branch(i, k % B)

        @block.vector
        def _(dve):
            dve.wait_ge(dist_in, 16 * 5)
            for kb in range(3):
                nc.vector.tensor_scalar(dist[:, kb, :], crow[:, 0, :], ccol[:, kb, 0:1], None, ALU.subtract)
                last = nc.vector.tensor_scalar(dtmp[:, kb, :], crow[:, 1, :], ccol[:, kb, 1:2], None, ALU.subtract)
            last.then_inc(dist_step, 1)
            dve.wait_ge(dist_step, 1)
            nc.vector.tensor_tensor(dist[:], dist[:], dist[:], ALU.mult).then_inc(dist_step, 1)
            nc.vector.tensor_tensor(dtmp[:], dtmp[:], dtmp[:], ALU.mult).then_inc(dist_step, 1)
            dve.wait_ge(dist_step, 3)
            nc.vector.tensor_tensor(dist[:], dist[:], dtmp[:], ALU.add).then_inc(dist_step, 2)
            dve.wait_ge(dist_sqrt, 1)
            nc.vector.tensor_reduce(dmax[:, 0:1], dist[:], AX.XY, ALU.max).then_inc(dist_red, 1)
            dve.wait_ge(dist_red, 2)
            nc.vector.tensor_scalar(dmax[:, 2:3], dmax[:, 1:2], DIST_MIN, None, ALU.max).then_inc(dist_step, 1)
            nc.vector.tensor_scalar(dmax[:, 3:4], dmax[:, 1:2], DIST_MIN, -BIAS_STRENGTH, ALU.is_gt,
                                    ALU.mult).then_inc(dist_step, 1)
            dve.wait_ge(dist_step, 7)
            nc.vector.reciprocal(dmax[:, 5:6], dmax[:, 2:3]).then_inc(dist_step, 1)
            dve.wait_ge(dist_step, 8)
            nc.vector.tensor_tensor(dmax[:, 4:5], dmax[:, 5:6], dmax[:, 3:4], ALU.mult).then_inc(dist_scale, 1)

            def layer_norm(c, n, src, dst, done):
                for j in range(JT):
                    last = nc.vector.bn_stats(stats[:, j, :], src[:, j, :])
                last.then_inc(ln_dve[n], 1)
                dve.wait_ge(ln_dve[n], c * 5 + (1))
                even, odd = stats[:, :, 1:3], stats[:, :, 4:6]
                nc.vector.tensor_tensor(total[:], even, odd, ALU.add)
                nc.vector.tensor_tensor(between[:], even[:, :, 0], odd[:, :, 0], ALU.subtract).then_inc(ln_dve[n], 1)
                dve.wait_ge(ln_dve[n], c * 5 + (2))
                nc.vector.tensor_tensor(between[:], between[:], between[:], ALU.mult)
                nc.vector.tensor_scalar(mv[:, n, :, 0], total[:, :, 0], 0.5, None, ALU.mult).then_inc(ln_dve[n], 1)
                dve.wait_ge(ln_dve[n], c * 5 + (3))
                nc.vector.scalar_tensor_tensor(between[:], between[:], D / 4.0, total[:, :, 1], ALU.mult,
                                               ALU.add).then_inc(ln_dve[n], 1)
                dve.wait_ge(ln_dve[n], c * 5 + (4))
                nc.vector.tensor_scalar(mv[:, n, :, 1], between[:], 1.0 / D, LN_EPS, ALU.mult, ALU.add
                                        ).then_inc(ln_var[n], 1)
                dve.wait_ge(ln_sqrt[n], c + 1)
                nc.vector.reciprocal(rstd[:, n], rstd[:, n]).then_inc(ln_dve[n], 1)
                dve.wait_ge(ln_dve[n], c * 5 + (5))
                for j in range(JT):
                    last = nc.vector.tensor_scalar(dst[:, j, :], src[:, j, :], mv[:, n, j, 0:1], rstd[:, n, j:j + 1],
                                                   ALU.subtract, ALU.mult)
                last.then_inc(done, 1)

            nc.vector.sem_inc(rest_ready, NMB)

            def first_norm(it, c, u, before):
                dve.wait_ge(x_loaded[u], it * 16 + (16 + 16 * before))
                layer_norm(c, 0, x_in[:, u], xn[:, u], xn_ready)

            first_norm(0, 0, 0, 0)
            with nc.vector.Fori(0, NCHUNK // 2) as it:
                for u in range(2):
                    c = it * 2 + u
                    for mb in range(NMB):
                        if mb == 0:
                            dve.wait_ge(xT_done, c + 1)
                            first_norm(it, c + 1, 1 - u, u)
                        dve.wait_ge(part1, c * NMB + (mb + 1))
                        nc.vector.tensor_tensor(rest[:, mb], banks[:, 2 + mb, :], parts[:, mb, 0 if mb < 2 else 2],
                                                ALU.subtract).then_inc(rest_ready, 1)
                    dve.wait_ge(res_stored, (c + 1) * 16)
                    dve.wait_ge(xn_ready, c + 1)
                    layer_norm(c, 1, xn[:, u], xn2, xn2_ready)
            dve.wait_ge(xn_ready, NCHUNK + 1)
            dve.wait_ge(rest_ready, NMB * (NCHUNK + 1))
            nc.vector.sem_inc(phase1_end, 1)
            dve.wait_ge(phase1_end, 5)
            nc.vector.tensor_copy(identb[:], ident[:])
            for b in range(B):
                nc.vector.memset(k_aug[TERM_ROWS:AUG, b, :], -1.0).then_inc(dve_const, 1)
            dve.wait_ge(dist_exp, 1)
            nc.vector.memset(bias_exp[0:1, 0, :], 1.0).then_inc(bias_ready, 1)

            def max_pair(before, t):
                q, half = (t // 2) % QC, t % 2
                dve.wait_ge(smax_ready, before + (t + 1))
                nc.vector.tensor_reduce(pair_max[:, q, half:half + 1], banks[:, 4 + 2 * (t % 2):6 + 2 * (t % 2), :],
                                        AX.XY, ALU.max).then_inc(smax_read, 1)

            def split_max(before, group):
                dve.wait_ge(smax_read, before * (PAIRS // GROUPS) + (group + 1) * (PAIRS // GROUPS) + 2)
                if group > 0:
                    dve.wait_ge(shift_saved, before + group)
                nc.vector.tensor_tensor(row_max[:], pair_max[:, :, 0], pair_max[:, :, 1], ALU.max).then_inc(max_step, 1)
                dve.wait_ge(max_step, before * 2 + (2 * group + 1))
                nc.vector.tensor_copy(shift[:, :, 0], row_max[:]).then_inc(max_step, 1)
                dve.wait_ge(max_step, before * 2 + (2 * group + 2))
                nc.vector.tensor_tensor(shift[:, :, 1], row_max[:], shift[:, :, 0], ALU.subtract).then_inc(shift_ready, 1)

            def save_attention(h, group):
                dve.wait_ge(sel_done, h * GROUPS + (group + 2))
                columns = banks[:, 3, :].rearrange("p (j g r) -> p j r g", g=4, r=VW)[:, :, 0:HD + 1, :]
                nc.vector.tensor_reduce(sums[:], columns, AX.X, ALU.add).then_inc(sums_done, 1)
                dve.wait_ge(sums_done, h * GROUPS + (group + 2))
                nc.vector.reciprocal(inv_sum[:], sums[:, :, HD]).then_inc(inv_done, 1)
                dve.wait_ge(inv_done, h * GROUPS + (group + 1))
                nc.vector.tensor_tensor(attn_tok[:, group * JT:(group + 1) * JT, bass.ds(h * HD, HD)],
                                        sums[:, :, 0:HD], inv_sum[:].unsqueeze(2).to_broadcast([P, JT, HD]),
                                        ALU.mult).then_inc(attn_saved, 1)

            nc.vector.sem_inc(smax_read, 2)
            nc.vector.sem_inc(sums_done, 1)
            for t in range(PAIRS // GROUPS):
                max_pair(0, t)
            split_max(0, 0)
            for t in range(PAIRS // GROUPS, (LEAD + 1) // 2 - 1):
                max_pair(0, t)
            for h, steps in turns(nc.vector):
                for step in steps:
                    group, kb = step // KB, step % KB
                    tile = step + LEAD
                    if tile % 2 == 1:
                        max_pair(h * PAIRS, tile // 2)
                    if tile % KB == KB - 1:
                        split_max(h * GROUPS, tile // KB)
                    if kb == KEEP_STEP and group > 0:
                        save_attention(h, group - 1)

            dve.wait_ge(attn_saved, HEADS * GROUPS)
            dve.wait_ge(smax_read, HEADS * PAIRS + ((FIRST_STEP + LEAD) // 2 + 2))
            nc.vector.sem_inc(phase2_end, 1)
            dve.wait_ge(phase2_end, 4)
            dve.wait_ge(ff_const, 12)
            dve.wait_ge(ff_weights, FF_WEIGHTS)
            nc.vector.sem_inc(sum_ready, B)
            H2 = LD // 2

            def turn_qk(i, k):
                l, b = parts_of(k)
                dve.wait_ge(tab_ready, i * LAYERS + (LAYERS * (k // ITEMS) + l + 1))
                for n in range(2):
                    dve.wait_ge(squares_done, at(i, k, n + 1, 2))
                    qk = banks[:, lanes(b) + n, :].rearrange("p (h d) -> p h d", d=LD)
                    norm = norms[:, b, n * LH:(n + 1) * LH]
                    nc.vector.tensor_reduce(norm, squares[:, b, n].rearrange("p (h d) -> p h d", d=LD), AX.X,
                                            ALU.add).then_inc(norm_sums, 1)
                    dve.wait_ge(norm_sums, at(i, k, 2 * n + 1, 4))
                    nc.vector.tensor_scalar(norm, norm, NORM_MIN * NORM_MIN, None, ALU.max).then_inc(norm_sums, 1)
                    cos, sin = tab[:, l, 2 * n, :], tab[:, l, 2 * n + 1, :]
                    cr = crossed[:, b, n].rearrange("p (h d) -> p h d", d=LD)
                    nc.vector.tensor_tensor(turned[:, b, n].rearrange("p (h d) -> p h d", d=LD), qk,
                                            cos.unsqueeze(1).to_broadcast([P, LH, LD]), ALU.mult)
                    for half in range(2):
                        o = slice(half * H2, (half + 1) * H2)
                        s_ = slice((1 - half) * H2, (2 - half) * H2)
                        last = nc.vector.tensor_tensor(cr[:, :, o], qk[:, :, s_],
                                                       sin[:, o].unsqueeze(1).to_broadcast([P, LH, H2]), ALU.mult)
                last.then_inc(rot_step, 1)

            def finish_qk(i, k):
                b = k % B
                dve.wait_ge(rot_step, at(i, k, 1, 2))
                nc.vector.tensor_tensor(turned[:, b], turned[:, b], crossed[:, b], ALU.add).then_inc(rot_step, 1)
                dve.wait_ge(rot_step, at(i, k, 2, 2))
                dve.wait_ge(inv_norms, at(i, k, 2, 2))
                t16 = turned[:, b].rearrange("p s (h d) -> p (s h) d", d=LD)
                nc.vector.tensor_tensor(t16, t16, norms[:, b].unsqueeze(2).to_broadcast([P, 2 * LH, LD]),
                                        ALU.mult).then_inc(turned_done, 1)

            def largest(i, k):
                b = k % B
                dve.wait_ge(scores_done, at(i, k))
                nc.vector.tensor_reduce(peak[:, b], banks[:, lanes(b):lanes(b) + 4, :]
                                        .rearrange("p a (g t) -> p (a g) t", t=2 * WINDOW), AX.X,
                                        ALU.max).then_inc(peak_step, 1)
                dve.wait_ge(peak_step, at(i, k))
                nc.vector.tensor_scalar(npeak[:, b], peak[:, b], -QK_SCALE, None, ALU.mult).then_inc(peaks_done, 1)

            def invert_rows(i, k):
                b = k % B
                dve.wait_ge(exp_done, at(i, k, 2, 2))
                nc.vector.reciprocal(row_sums[:, b], row_sums[:, b]).then_inc(inv_rows, 1)

            def scale_o(i, k):
                b = k % B
                dve.wait_ge(spread_kept, at(i, k))
                dve.wait_ge(o_done, at(i, k))
                nc.vector.tensor_tensor(oT[:, b], banks[:, lanes(b), :].rearrange("p (j t) -> p j t", t=WINDOW),
                                        oT[:, b], ALU.mult).then_inc(o_kept, 1)

            def add_attention(i, k):
                l, b = parts_of(k)
                dve.wait_ge(wo_done, at(i, k))
                dve.wait_ge(x1_carried, at(i, k))
                nc.vector.tensor_tensor(x1T[:, l, b, :, 1:], banks[:, lanes(b) + 2, 0:D]
                                        .rearrange("p (f t) -> p f t", t=WINDOW), xT[:, l, b, :, 1:],
                                        ALU.add).then_inc(x1_ready, 1)

            def normalise(i, k):
                b = k % B
                h_tok = banks[:, lanes(b) + 3, 0:D]
                dve.wait_ge(h_done, at(i, k))
                nc.vector.bn_stats(fstats[:, b], h_tok).then_inc(norm_step, 1)
                dve.wait_ge(norm_step, at(i, k, 1, 4))
                nc.vector.tensor_tensor(ftotal[:, b], fstats[:, b, 1:3], fstats[:, b, 4:6], ALU.add)
                nc.vector.tensor_tensor(fbetween[:, b], fstats[:, b, 1:2], fstats[:, b, 4:5], ALU.subtract
                                        ).then_inc(norm_step, 1)
                dve.wait_ge(norm_step, at(i, k, 2, 4))
                nc.vector.tensor_tensor(fbetween[:, b], fbetween[:, b], fbetween[:, b], ALU.mult)
                nc.vector.tensor_scalar(fmv[:, b, 0:1], ftotal[:, b, 0:1], 0.5, None, ALU.mult).then_inc(norm_step, 1)
                dve.wait_ge(norm_step, at(i, k, 3, 4))
                nc.vector.scalar_tensor_tensor(fbetween[:, b], fbetween[:, b], D / 4.0, ftotal[:, b, 1:2],
                                               ALU.mult, ALU.add).then_inc(norm_step, 1)
                dve.wait_ge(norm_step, at(i, k, 4, 4))
                nc.vector.tensor_scalar(fmv[:, b, 1:2], fbetween[:, b], 1.0 / D, LN_EPS, ALU.mult,
                                        ALU.add).then_inc(var_done, 1)
                dve.wait_ge(rstd_done, at(i, k))
                nc.vector.tensor_scalar(hn[:, b], h_tok, fmv[:, b, 0:1], fmv[:, b, 1:2],
                                        ALU.subtract, ALU.mult).then_inc(hn_ready, 1)

            def gate(i, k):
                l, b = parts_of(k)
                dve.wait_ge(gelu_done, at(i, k))
                for j in range(HB):
                    if j % 4 == 0:
                        dve.wait_ge(w1_done, at(i, k, j // 4 + 3, 4))
                    last = nc.vector.scalar_tensor_tensor(
                        uT[:, b, j], banks[0:HP, lanes(b) + 2 + j // 4, (j % 4) * P:(j % 4 + 1) * P],
                        b1_sb[:, l, j:j + 1], gated[:, b, j], ALU.add, ALU.mult)
                    if j % (HB // 2) == HB // 2 - 1:
                        last.then_inc(u_ready, 1)

            def add_hidden(i, k):
                l, b = parts_of(k)
                dve.wait_ge(w2_done, at(i, k))
                if l < LAYERS - 1:
                    dve.wait_ge(x_carried, at(i, k + B))
                    dst = xT[:, l + 1, b, :, 1:]
                else:
                    dst = yT[:, b]
                for f in range(2):
                    last = nc.vector.scalar_tensor_tensor(
                        dst[:, f], banks[:, lanes(b), f * P:(f + 1) * P], b2_sb[:, l, f:f + 1],
                        x1T[:, l, b, f, 1:], ALU.add, ALU.add)
                last.then_inc(x2_ready, 1)

            def take_heads(i, k):
                b = k % B
                dve.wait_ge(hnT_done, at(i, k))
                nc.vector.tensor_copy(o_win[:, b], attn_tok[:, bass.ds(i + b * NWIN, 1), :][:, 0]).then_inc(o_copied, 1)

            def add_first(i, b):
                dve.wait_ge(proj_done, i * B + (b + 1))
                dve.wait_ge(final_in[b], i * 32 + 32)
                nc.vector.tensor_tensor(s_win[:, b], banks[:, lanes(b) + 3, 0:D], res_win[:, b],
                                        ALU.add).then_inc(sum_ready, 1)

            for stage in (turn_qk, finish_qk, largest):
                stage(0, 0)
            with nc.vector.Fori(0, NWIN) as i:
                for k in range(ITEMS):
                    final = k >= ITEMS - B
                    invert_rows(i, k)
                    turn_qk(i, k + 1)
                    finish_qk(i, k + 1)
                    scale_o(i, k)
                    add_attention(i, k)
                    normalise(i, k)
                    if final:
                        take_heads(i, k)
                    largest(i, k + 1)
                    gate(i, k)
                    add_hidden(i, k)
                    if final:
                        add_first(i, k % B)

        @block.tensor
        def _(pe):
            pe.wait_ge(pool_const, 2)
            pe.wait_ge(consts_in, 16 * NCONST)
            nc.tensor.sem_inc(xT_done, 1)
            nc.tensor.sem_inc(v_done, 1)

            def transpose_x(c, u):
                pe.wait_ge(xn_ready, c + 1)
                for k in range(2):
                    for j in range(JT):
                        last = nc.tensor.transpose(banks[:, k, j * P:(j + 1) * P], xn[:, u, j, k * P:(k + 1) * P],
                                                   ident[:])
                last.then_inc(xT_done, 1)

            transpose_x(0, 0)
            with nc.tensor.Fori(0, NCHUNK // 2) as it:
                for u in range(2):
                    c = it * 2 + u
                    pe.wait_ge(xnT_ready, c + 2)
                    for mb in range(NMB):
                        pe.wait_ge(rest_ready, c * NMB + (mb + 1))
                        for k in range(2):
                            last = nc.tensor.matmul(banks[:, 2 + mb, :], wqk_sb[:, k, mb * P:(mb + 1) * P],
                                                    xnT[:, u, k, :], start=(k == 0), stop=(k == 1))
                        last.then_inc(qk_done, 1)
                    transpose_x(c + 1, 1 - u)
                    pe.wait_ge(v_saved, c + 1)
                    for j in range(JT):
                        for k in range(2):
                            last = nc.tensor.matmul(banks[:, 6 + j // 2, (j % 2) * D:(j % 2 + 1) * D],
                                                    xnT[:, u, k, j * P:(j + 1) * P], wv_sb[:, k, :],
                                                    start=(k == 0), stop=(k == 1))
                    last.then_inc(v_done, 1)
            pe.wait_ge(v_done, NCHUNK + 1)
            pe.wait_ge(xT_done, NCHUNK + 2)
            nc.tensor.sem_inc(phase1_end, 1)
            pe.wait_ge(phase1_end, 5)
            pe.wait_ge(dve_const, 1)

            def max_tile(before, t):
                pair, b, q, kq = t // 2, (t // (QC * KB)) % B, (t // (N // BANK)) % KB, t % (N // BANK)
                if t % 2 == 0:
                    pe.wait_ge(smax_read, before + (pair + 1))
                mm = nc.tensor.matmul(banks[:, 4 + t % 4, :], q_aug[0:MAX_ROWS, b, q * P:(q + 1) * P],
                                      k_aug[0:MAX_ROWS, b, kq * BANK:(kq + 1) * BANK], start=True, stop=True)
                if t % 2 == 1:
                    mm.then_inc(smax_ready, 1)

            def bank_free(h, first_step, use):
                first_use = use_of(first_step)
                if use < first_use + SRING:
                    pe.wait_ge(prob_ready, h * STEPS + (first_step + 1))
                    return
                group, kb = divmod(use - SRING, KB + 1)
                if kb == MSTEP + 1:
                    pe.wait_ge(shift_saved, h * GROUPS + (group + 2))
                else:
                    pe.wait_ge(prob_ready, h * STEPS + (group * KB + kb - (kb > MSTEP) + 2))

            def shift_rows(h, first_step, group, use):
                pe.wait_ge(shift_ready, h * GROUPS + (group + 1))
                bank_free(h, first_step, use)
                for j in range(JT):
                    last = nc.tensor.transpose(
                        banks[TERM_ROWS:AUG, (use - use_of(first_step)) % SRING, j * P // 2:(j + 1) * P // 2].bitcast(BF16),
                        shift[:, j, :], identb[:])
                last.then_inc(st_ready, 1)

            def scores_to_exp(h, first_step, step):
                group, kb, use = step // KB, step % KB, use_of(step)
                b, qc = (group // QC) % B, group % QC
                if kb == 0:
                    pe.wait_ge(shift_saved, h * GROUPS + (group + 1))
                    if group == QC:
                        pe.wait_ge(dve_const, 2)
                bank_free(h, first_step, use)
                nc.tensor.matmul(banks[:, (use - use_of(first_step)) % SRING, :], k_aug[0:AUG, b, kb * P:(kb + 1) * P],
                                 q_aug[0:AUG, b, qc * CHUNK:(qc + 1) * CHUNK], start=True,
                                 stop=True).then_inc(st_ready, 1)

            def weighted(h, group, kb):
                step = group * KB + kb
                b = group // QC
                if kb == 0:
                    pe.wait_ge(sums_done, h * GROUPS + (group + 1))
                    pe.wait_ge(v_copied, h * 2 + (3 + b))
                if group % QC == 0 and kb < 3:
                    pe.wait_ge(bias_done, h * 6 + (b * 3 + kb + 1))
                else:
                    pe.wait_ge(prob_ready, h * STEPS + (step + 2))
                g = kb % 4
                mm = nc.tensor.matmul(banks[32 * g:32 * g + VW, 3, :], v_cur[:, b, kb, :], probs[:, step % PRING, :],
                                      start=(kb < 4), stop=(kb >= KB - 4))
                mm.then_inc(pv_done, 1)

            def add_groups(h, group):
                pe.wait_ge(acc_saved, h * GROUPS + (group + 1))
                for j in range(JT):
                    last = nc.tensor.transpose(banks[:, 3, j * P:(j + 1) * P], acc_sb[:, j * P:(j + 1) * P], ident[:])
                last.then_inc(sel_done, 1)

            nc.tensor.sem_inc(pv_done, 1)
            nc.tensor.sem_inc(sel_done, 1)
            pe.wait_ge(aug_loaded[0], 16 * 6)
            for t in range(KB):
                max_tile(0, t)
            shift_rows(0, 0, 0, 0)
            for t in range(KB, LEAD):
                max_tile(0, t)
            for h, steps in turns(nc.tensor):
                first_step = steps[0]
                for step in steps:
                    group, kb = step // KB, step % KB
                    if step > first_step:
                        scores_to_exp(h, first_step, step)
                    tile = step + LEAD
                    if tile == STEPS // 2:
                        pe.wait_ge(aug_loaded[1], h * 96 + 96)
                    if tile == STEPS:
                        pe.wait_ge(aug_loaded[0], h * 96 + 192)
                    max_tile(h * PAIRS, tile)
                    ago, first = PV_PLAN.get(kb, (-2 * GROUPS, 0))
                    if group + ago >= 0:
                        for key in range(first, first + 4):
                            weighted(h, group + ago, key)
                    if kb == ADD_STEP and group > 0:
                        add_groups(h, group - 1)
                    if step == first_step:
                        scores_to_exp(h, first_step, step)
                    if kb == MSTEP:
                        shift_rows(h, first_step, group + 1, use_of(step) + 1)

            pe.wait_ge(sel_done, HEADS * GROUPS + 1)
            pe.wait_ge(prob_ready, HEADS * STEPS + (FIRST_STEP + 1))
            nc.tensor.sem_inc(phase2_end, 1)
            pe.wait_ge(phase2_end, 4)
            pe.wait_ge(ff_const, 12)
            pe.wait_ge(ff_weights, FF_WEIGHTS)

            def project_qk(i, k):
                l, b = parts_of(k)
                if l == 0:
                    pe.wait_ge(x_window[b], i * 16 + (16 * (k // ITEMS) + 16))
                    pe.wait_ge(y_kept, i * B + (B * (k // ITEMS) + b + 1))
                    pe.wait_ge(sum_ready, i * B + (B * (k // ITEMS) + b + 1))
                else:
                    pe.wait_ge(x2_ready, at(i, k - B))
                for n in range(2):
                    for f in range(2):
                        last = nc.tensor.matmul(banks[:, lanes(b) + n, :], xT[:, l, b, f, 1 - f:1 - f + WINDOW],
                                                wqkv_sb[:, l, f, n * INNER:(n + 1) * INNER],
                                                start=(f == 0), stop=(f == 1))
                    last.then_inc(qk_ready, 1)

            def project_v(i, k):
                l, b = parts_of(k)
                for f in range(2):
                    last = nc.tensor.matmul(banks[:, lanes(b) + 2, :], xT[:, l, b, f, 1 - f:1 - f + WINDOW],
                                            wqkv_sb[:, l, f, 2 * INNER:], start=(f == 0), stop=(f == 1))
                last.then_inc(v_ready, 1)

            def transpose_qk(i, k):
                b = k % B
                pe.wait_ge(turned_done, at(i, k))
                for j in range(NPAIR):
                    nc.tensor.transpose(banks[:, lanes(b) + 3, j * P:(j + 1) * P],
                                        turned[:, b, 0, j * P:(j + 1) * P], ident[:])
                    last = nc.tensor.transpose(banks[:, lanes(b), j * P:(j + 1) * P],
                                               turned[:, b, 1, j * P:(j + 1) * P], ident[:])
                last.then_inc(qkT_done, 1)

            def set_mask(i, k, pair):
                b = k % B
                if pair == (1, 2):
                    pe.wait_ge(mask_set, i + (k // ITEMS + 1))
                    pe.wait_ge(rot_step, at(i, k, 1, 2))
                    pe.wait_ge(v_kept, at(i, k))
                else:
                    pe.wait_ge(qT_kept, at(i, k))
                    pe.wait_ge(kT_kept, at(i, k))
                for a in pair:
                    nc.tensor.matmul(banks[:, lanes(b) + a, :].rearrange("p (g t) -> p g t", t=2 * WINDOW), identb[:],
                                     mask[:].unsqueeze(1).to_broadcast([P, 2, 2 * WINDOW]), start=True, stop=False)

            def scores(i, k, heads):
                l, b = parts_of(k)
                for hh in heads:
                    r = slice((hh % 2) * LD, (hh % 2 + 1) * LD)
                    col = (place(hh) % 2) * 2 * WINDOW
                    last = nc.tensor.matmul(banks[:, lanes(b) + place(hh) // 2, col:col + 2 * WINDOW],
                                            qT[r, b, hh // 2, :], kT[r, l, b, hh // 2, :], start=False,
                                            stop=(place(hh) % 2 == 1))
                if hh == LH - 1:
                    last.then_inc(scores_done, 1)

            def transpose_probs(i, k, half):
                b = k % B
                pe.wait_ge(exp_done, at(i, k, half + 1, 2))
                for p in range(half * LH // 2, (half + 1) * LH // 2):
                    for c in range(2):
                        col = ((p % 2) * 2 + c) * P
                        last = nc.tensor.transpose(banks[:, lanes(b) + p // 2, col:col + P],
                                                   masked[:, b, p, c * P:(c + 1) * P], ident[:])
                last.then_inc(pT_done, 1)

            def spread_sums(i, k):
                b = k % B
                pe.wait_ge(widened, at(i, k))
                pe.wait_ge(pT_kept, at(i, k, 1, 2))
                for j in range(NPAIR):
                    last = nc.tensor.transpose(banks[:, lanes(b) + 1, j * P:(j + 1) * P],
                                               oT[:, b, j, :], ident[:])
                last.then_inc(spread_done, 1)

            def weighted_values(i, k):
                l, b = parts_of(k)
                pe.wait_ge(pT_kept, at(i, k, 2, 2))
                for j in range(NPAIR):
                    for c in range(2):
                        for r in range(PAIR):
                            hh = j * PAIR + r
                            last = nc.tensor.matmul(banks[r * LD:(r + 1) * LD, lanes(b), j * P:(j + 1) * P],
                                                    vw[:, l, b, c, hh * LD:(hh + 1) * LD], pT[:, b, place(hh), c, :],
                                                    start=(c == 0), stop=(c == 1))
                last.then_inc(o_done, 1)

            def project_o(i, k):
                l, b = parts_of(k)
                pe.wait_ge(o_kept, at(i, k))
                for f in range(2):
                    for j in range(NPAIR):
                        last = nc.tensor.matmul(banks[:, lanes(b) + 2, f * P:(f + 1) * P],
                                                wo_sb[:, l, j, f * P:(f + 1) * P], oT[:, b, j, :],
                                                start=(j == 0), stop=(j == NPAIR - 1))
                last.then_inc(wo_done, 1)

            def transpose_h(i, k):
                l, b = parts_of(k)
                pe.wait_ge(x1_ready, at(i, k))
                for f in range(2):
                    last = nc.tensor.transpose(banks[:, lanes(b) + 3, f * P:(f + 1) * P],
                                               x1T[:, l, b, f, 1 - f:1 - f + WINDOW], ident[:])
                last.then_inc(h_done, 1)

            def transpose_normed(i, k):
                b = k % B
                pe.wait_ge(hn_ready, at(i, k))
                for f in range(2):
                    last = nc.tensor.transpose(banks[:, lanes(b) + 3, D + f * P:D + (f + 1) * P],
                                               hn[:, b, f * P:(f + 1) * P], ident[:])
                last.then_inc(hnT_done, 1)

            def hidden(i, k):
                l, b = parts_of(k)
                pe.wait_ge(hnT_kept, at(i, k))
                for bank, part in ((0, 1), (2, 0)):
                    for j in range(HB):
                        for f in range(2):
                            col = (part * HB + j) * HP
                            last = nc.tensor.matmul(
                                banks[0:HP, lanes(b) + bank + j // 4, (j % 4) * P:(j % 4 + 1) * P],
                                w1_sb[:, l, f, col:col + HP], hnT[:, b, f, :], start=(f == 0), stop=(f == 1))
                        if (j + 1) % 4 == 0 or j == HB - 1:
                            last.then_inc(w1_done, 1)

            def project_hidden(i, k):
                l, b = parts_of(k)
                for j in range(HB):
                    if j % (HB // 2) == 0:
                        pe.wait_ge(u_ready, at(i, k, j // (HB // 2) + 1, 2))
                    for f in range(2):
                        last = nc.tensor.matmul(banks[:, lanes(b), f * P:(f + 1) * P],
                                                w2_sb[:, l, j, f * P:(f + 1) * P], uT[:, b, j, :],
                                                start=(j == 0 and f == 0), stop=(j == HB - 1 and f == 1))
                last.then_inc(w2_done, 1)

            def transpose_heads(i, k):
                b = k % B
                pe.wait_ge(o_copied, i * B + (b + 1))
                pe.wait_ge(gelu_done, at(i, k))
                for f in range(2):
                    last = nc.tensor.transpose(banks[:, lanes(b) + 1, f * P:(f + 1) * P],
                                               o_win[:, b, f * P:(f + 1) * P], ident[:])
                last.then_inc(owT_done, 1)

            def project_heads(i, b):
                pe.wait_ge(owT_kept, i * B + (b + 1))
                for f in range(2):
                    last = nc.tensor.matmul(banks[:, lanes(b) + 3, 0:D], o_winT[:, b, f, :], wp_sb[:, f, :],
                                            start=(f == 0), stop=(f == 1))
                last.then_inc(proj_done, 1)

            def transpose_y(i, k):
                b = k % B
                pe.wait_ge(x2_ready, at(i, k))
                for f in range(2):
                    last = nc.tensor.transpose(banks[:, lanes(b) + 2, f * P:(f + 1) * P], yT[:, b, f, :], ident[:])
                last.then_inc(y_done, 1)

            project_qk(0, 0)
            project_v(0, 0)
            set_mask(0, 0, (1, 2))
            transpose_qk(0, 0)
            set_mask(0, 0, (3, 0))
            scores(0, 0, range(LH))
            with nc.tensor.Fori(0, NWIN) as i:
                for k in range(ITEMS):
                    final = k >= ITEMS - B
                    transpose_probs(i, k, 0)
                    project_qk(i, k + 1)
                    transpose_probs(i, k, 1)
                    spread_sums(i, k)
                    project_v(i, k + 1)
                    weighted_values(i, k)
                    set_mask(i, k + 1, (1, 2))
                    transpose_qk(i, k + 1)
                    project_o(i, k)
                    set_mask(i, k + 1, (3, 0))
                    transpose_h(i, k)
                    scores(i, k + 1, range(LH - 2))
                    transpose_normed(i, k)
                    scores(i, k + 1, range(LH - 2, LH))
                    hidden(i, k)
                    if final:
                        transpose_heads(i, k)
                    project_hidden(i, k)
                    if final:
                        project_heads(i, k % B)
                        transpose_y(i, k)


_INS = {
    "x": lambda i: i["L0_attn_x"],
    "wqkT": lambda i: i["L0_attn_W_qkv"][:2 * D].T,
    "wvT": lambda i: i["L0_attn_W_qkv"][2 * D:].T,
    "wpT": lambda i: i["L0_attn_W_proj"].T,
    "b_proj": lambda i: i["L0_attn_b_proj"],
    "gamma": lambda i: i["L0_attn_ln_gamma"],
    "beta": lambda i: i["L0_attn_ln_beta"],
    "centers": lambda i: i["L0_attn_spatial_centers"],
    "centersT": lambda i: i["L0_attn_spatial_centers"].T,
    "wqkv": lambda i: i["L0_ffn_wqkv"],
    "qk_gain": lambda i: np.stack([i["L0_ffn_q_scale"], i["L0_ffn_k_scale"]], axis=1),
    "qk_gain_swapped": lambda i: swapped(np.stack([i["L0_ffn_q_scale"], i["L0_ffn_k_scale"]], axis=1)),
    "rotary": lambda i: rotary_tables(),
    "wo": lambda i: i["L0_ffn_wo"],
    "ln_gain": lambda i: by_block(i["L0_ffn_ln_g"], 2, P),
    "ln_bias": lambda i: by_block(i["L0_ffn_ln_b"], 2, P),
    "w1": lambda i: pad_hidden(i["L0_ffn_w1"], 2),
    "b1": lambda i: by_block(pad_hidden(i["L0_ffn_b1"], 1), 2 * HB, HP),
    "w2": lambda i: pad_hidden(i["L0_ffn_w2"], 1),
    "b2": lambda i: by_block(i["L0_ffn_b2"], 2, P),
}


def rotary_tables():
    half = np.arange(0, LD, 2, dtype=np.float32)
    inv_freq = (np.float32(1.0) / np.float32(10000.0) ** (half / np.float32(LD))).astype(np.float32)
    t = np.arange(N, dtype=np.float32)
    freqs = np.concatenate([t[:, None] * inv_freq] * 2, axis=-1)
    base = (half + np.float32(0.4 * LD)) / np.float32(1.4 * LD)
    power = (t - np.float32(N // 2)) / np.float32(WINDOW // 2)
    scale = np.concatenate([base[None, :] ** power[:, None]] * 2, axis=-1).astype(np.float32)
    sign = np.where(np.arange(LD) < LD // 2, np.float32(-1), np.float32(1))
    cos, sin = np.cos(freqs), np.sin(freqs) * sign
    tabs = np.stack([cos * scale, sin * scale, cos / scale, sin / scale], axis=1)
    return np.ascontiguousarray(tabs.reshape(NWIN, WINDOW, 4, LD), dtype=np.float32)


def swapped(a):
    return np.concatenate([a[..., LD // 2:], a[..., :LD // 2]], axis=-1)


def by_block(a, blocks, size):
    return a.reshape(a.shape[0], blocks, size).transpose(2, 0, 1)


def pad_hidden(a, axis):
    halves = np.split(a, a.shape[axis] // HID, axis=axis)
    width = [(0, 0)] * a.ndim
    width[axis] = (0, HB * HP - HID)
    return np.concatenate([np.pad(p, width) for p in halves], axis=axis)

def kernel(**inputs):
    import numpy as _np
    import concourse.bacc as _bacc
    from concourse import mybir as _mybir
    from concourse.bass_utils import run_bass_kernel_spmd as _run

    nc = _bacc.Bacc("TRN2", target_bir_lowering=False, num_devices=1)
    arrays, args = {}, []
    for name, lay in _INS.items():
        a = _np.ascontiguousarray(lay(inputs))
        arrays[f"in_{name}"] = a
        args.append(nc.dram_tensor(f"in_{name}", a.shape, _mybir.dt.from_np(a.dtype), kind="ExternalInput").ap())
    out = nc.dram_tensor("out_0", (B, N, D), F32, kind="ExternalOutput").ap()
    build(nc, *args, out)
    r = _run(nc, [arrays], core_ids=[0])
    return r.results[0]["out_0"]
```
